# Optimizing a Trainium2 kernel written in Bass

```python
import numpy as np
import jax
import jax.numpy as jnp

def _softmax(x, axis=-1):
    return jax.nn.softmax(x, axis=axis)

def _gelu(x):
    return jax.nn.gelu(x, approximate=True)

def _silu(x):
    return jax.nn.silu(x)

def _sigmoid(x):
    return jax.nn.sigmoid(x)

def _layernorm(x, axis=-1, eps=1e-05):
    m = jnp.mean(x, axis=axis, keepdims=True)
    v = jnp.var(x, axis=axis, keepdims=True)
    return (x - m) / jnp.sqrt(v + eps)

def _scatter_add(tgt, idx, src, axis=0):
    return tgt.at[idx].add(src)

def _segment_sum(src, seg, n):
    return jax.ops.segment_sum(src, seg, n)
kernel_name = 'mk_xattn_ffn_d4_seqx_r8_994bdb'

def setup_inputs(seed: int=0):
    np.random.seed(seed)
    _w = jnp.asarray

    def _rec_inputs():
        import jax
        import jax.numpy as jnp
        _rk = jax.random.key(seed)
        x = -0.0003929 + 0.9999 * jax.random.normal(jax.random.fold_in(_rk, 1), (16, 100, 256), jnp.float32)
        _lenS = 100 - jax.random.randint(jax.random.fold_in(_rk, 7), (16,), 0, max(1, 100 // 4) + 1, jnp.int32)
        _lenS2 = 1444 - jax.random.randint(jax.random.fold_in(_rk, 8), (16,), 0, max(1, 1444 // 4) + 1, jnp.int32)
        _ctx_2048P = jax.random.normal(jax.random.fold_in(_rk, 11), (16, 16, 256), jnp.float32)
        _ctx_2048c = jax.random.dirichlet(jax.random.fold_in(_rk, 511), 0.3 * jnp.ones((16,), jnp.float32), (16, 1444))
        _ctx_2048t = jnp.einsum('bsk,bkd->bsd', _ctx_2048c, _ctx_2048P)
        _ctx_2048t = _ctx_2048t * jax.lax.rsqrt(jnp.mean(jnp.square(_ctx_2048t)) + 1e-12) * 0.953939
        ctx_2048 = -0.000514642 + 1.00011 * (_ctx_2048t + 0.3 * jax.random.normal(jax.random.fold_in(_rk, 611), (16, 1444, 256), jnp.float32))
        _validS = jnp.arange(100)[None, :] < _lenS[:, None]
        _validS2 = jnp.arange(1444)[None, :] < _lenS2[:, None]
        _causal = jnp.tril(jnp.ones((100, 100), dtype=bool))
        mask_BxS2_bk0 = jnp.logical_not(jnp.broadcast_to(_validS2[:, :], (16, 1444)))
        mask_BxSx4224_bf0 = jnp.logical_not(jnp.ones((16, 100, 528), dtype=bool))
        return (x, ctx_2048, mask_BxS2_bk0, mask_BxSx4224_bf0)
    x, ctx_2048, mask_BxS2_bk0, mask_BxSx4224_bf0 = _rec_inputs()

    def _L0_xattn_setup():
        import jax, jax.numpy as jnp
        import numpy as np
        DIM = 256
        NHEADS = 32
        HEAD_DIM = DIM // NHEADS
        EPS = 1e-06

        def _rmsnorm(t):
            return t * jax.lax.rsqrt(jnp.mean(t * t, axis=-1, keepdims=True) + EPS)
        key = jax.random.key(seed)
        kx, kc, kq, kk, kv = jax.random.split(key, 5)
        x = jax.random.normal(kx, (2, 512, DIM), dtype=jnp.float32)
        context = jax.random.normal(kc, (2, 64, DIM), dtype=jnp.float32)
        std = 0.02
        Wq = jax.random.normal(kq, (DIM, DIM), dtype=jnp.float32) * std
        Wk = jax.random.normal(kk, (DIM, DIM), dtype=jnp.float32) * std
        Wv = jax.random.normal(kv, (DIM, DIM), dtype=jnp.float32) * std
        return {'x': x, 'context': context, 'Wq': Wq, 'Wk': Wk, 'Wv': Wv}
    _L0_xattn_all = _L0_xattn_setup()
    _L0_xattn_in = {k: v for k, v in _L0_xattn_all.items() if k in ('Wq', 'Wk', 'Wv')}
    del _L0_xattn_all

    def _L0_ffn_setup():
        import jax, jax.numpy as jnp
        import numpy as np
        NUM_EXPERTS = 8
        TOP_K = 2
        HIDDEN = 256
        INTER = 256
        SWIGLU_LIMIT = 7.0
        BATCH, SEQ = (4, 256)
        key = jax.random.key(seed)
        k0, k1, k2, k3, k4 = jax.random.split(key, 5)
        x = jax.random.normal(k0, (BATCH, SEQ, HIDDEN), jnp.float32)
        Wr = jax.random.normal(k1, (HIDDEN, NUM_EXPERTS), jnp.float32) * 0.02
        Wg = jax.random.normal(k2, (NUM_EXPERTS, HIDDEN, INTER), jnp.float32) * 0.02
        Wu = jax.random.normal(k3, (NUM_EXPERTS, HIDDEN, INTER), jnp.float32) * 0.02
        Wd = jax.random.normal(k4, (NUM_EXPERTS, INTER, HIDDEN), jnp.float32) * 0.02
        return {'hidden_states': x, 'Wr': Wr, 'Wg': Wg, 'Wu': Wu, 'Wd': Wd}
    _L0_ffn_all = _L0_ffn_setup()
    _L0_ffn_in = {k: v for k, v in _L0_ffn_all.items() if k in ('Wr', 'Wg', 'Wu', 'Wd')}
    del _L0_ffn_all

    def _L1_xattn_setup():
        import jax, jax.numpy as jnp
        import numpy as np
        key = jax.random.key(seed)
        k1, k2, k3 = jax.random.split(key, 3)
        B, S, D, M = (8, 256, 256, 128)
        hidden_states = jax.random.normal(k1, (B, S, D), dtype=jnp.float32)
        memory_tokens = jax.random.normal(k2, (B, M, D), dtype=jnp.float32)
        memory_mask = jax.random.randint(k3, (B, M), 0, 2).astype(jnp.bool_)
        return {'hidden_states': hidden_states, 'memory_tokens': memory_tokens, 'memory_mask': memory_mask}
    _L1_xattn_all = _L1_xattn_setup()
    _L1_xattn_in = {k: v for k, v in _L1_xattn_all.items() if k in ()}
    del _L1_xattn_all

    def _L1_ffn_setup():
        import jax, jax.numpy as jnp
        import numpy as np
        B, T, D = (4, 256, 256)
        E = 8
        K = 2
        F = 1024 // (E // 2)
        key = jax.random.key(seed)
        ks = jax.random.split(key, 5)
        s_in = 1.0 / np.sqrt(D)
        s_mid = 1.0 / np.sqrt(F)
        x = jax.random.normal(ks[0], (B, T, D), dtype=jnp.float32)
        Wr = jax.random.normal(ks[1], (D, E), dtype=jnp.float32) * s_in
        Wg = jax.random.normal(ks[2], (E, D, F), dtype=jnp.float32) * s_in
        Wu = jax.random.normal(ks[3], (E, D, F), dtype=jnp.float32) * s_in
        Wd = jax.random.normal(ks[4], (E, F, D), dtype=jnp.float32) * s_mid
        return {'x': x, 'Wr': Wr, 'Wg': Wg, 'Wu': Wu, 'Wd': Wd}
    _L1_ffn_all = _L1_ffn_setup()
    _L1_ffn_in = {k: v for k, v in _L1_ffn_all.items() if k in ('Wr', 'Wg', 'Wu', 'Wd')}
    del _L1_ffn_all

    def _L2_xattn_setup():
        import jax, jax.numpy as jnp
        import numpy as np
        HIDDEN = 256
        N_HEADS = 16
        N_KV_HEADS = 4
        HEAD_DIM = 128
        EPS = 1e-06

        def rms_norm(x, w, eps=EPS):
            xf = x.astype(jnp.float32)
            var = jnp.mean(xf * xf, axis=-1, keepdims=True)
            return w * (xf * jax.lax.rsqrt(var + eps)).astype(x.dtype)
        key = jax.random.key(seed)
        ks = jax.random.split(key, 8)
        B, S, S_ENC = (4, 256, 128)
        inner = N_HEADS * HEAD_DIM
        kv_dim = N_KV_HEADS * HEAD_DIM
        s = 0.02
        return {'hidden_states': jax.random.normal(ks[0], (B, S, HIDDEN), jnp.float32), 'encoder_hidden_states': jax.random.normal(ks[1], (B, S_ENC, HIDDEN), jnp.float32), 'Wq': jax.random.normal(ks[2], (HIDDEN, inner), jnp.float32) * s, 'Wk': jax.random.normal(ks[3], (HIDDEN, kv_dim), jnp.float32) * s, 'Wv': jax.random.normal(ks[4], (HIDDEN, kv_dim), jnp.float32) * s, 'Wo': jax.random.normal(ks[5], (inner, HIDDEN), jnp.float32) * s, 'q_norm_w': jnp.ones((HEAD_DIM,), jnp.float32), 'k_norm_w': jnp.ones((HEAD_DIM,), jnp.float32)}
    _L2_xattn_all = _L2_xattn_setup()
    _L2_xattn_in = {k: v for k, v in _L2_xattn_all.items() if k in ('Wq', 'Wk', 'Wv', 'Wo', 'q_norm_w', 'k_norm_w')}
    del _L2_xattn_all

    def _L2_ffn_setup():
        import jax, jax.numpy as jnp
        import numpy as np
        E = 32
        K = 8
        H = 256
        F = 96
        B, S = (1, 128)

        def _moe(x, wg, w1, v1, w2):
            T = x.shape[0]
            logits = x @ wg.T
            scores = jax.nn.softmax(logits, axis=-1)
            weights, idx = jax.lax.top_k(scores, K)
            weights = weights / jnp.sum(weights, axis=-1, keepdims=True)
            flat_e = idx.reshape(-1)
            flat_t = jnp.repeat(jnp.arange(T), K)
            flat_w = weights.reshape(-1)
            order = jnp.argsort(flat_e)
            e_s = flat_e[order]
            t_s = flat_t[order]
            w_s = flat_w[order]
            group_sizes = jnp.bincount(e_s, length=E).astype(jnp.int32)
            xs = x[t_s]
            g = jax.lax.ragged_dot(xs, w1, group_sizes)
            u = jax.lax.ragged_dot(xs, v1, group_sizes)
            h = jax.nn.silu(g) * u
            ys = jax.lax.ragged_dot(h, w2, group_sizes)
            out = jnp.zeros((T, x.shape[1]), x.dtype).at[t_s].add(ys * w_s[:, None])
            return out
        key = jax.random.key(seed)
        k0, k1, k2, k3, k4 = jax.random.split(key, 5)
        scale = 0.02
        return {'hidden_states': jax.random.normal(k0, (B, S, H), jnp.float32), 'wg': jax.random.normal(k1, (E, H), jnp.float32) * scale, 'w1': jax.random.normal(k2, (E, H, F), jnp.float32) * scale, 'v1': jax.random.normal(k3, (E, H, F), jnp.float32) * scale, 'w2': jax.random.normal(k4, (E, F, H), jnp.float32) * scale}
    _L2_ffn_all = _L2_ffn_setup()
    _L2_ffn_in = {k: v for k, v in _L2_ffn_all.items() if k in ('wg', 'w1', 'v1', 'w2')}
    del _L2_ffn_all

    def _L3_xattn_setup():
        import jax, jax.numpy as jnp
        import numpy as np
        import math
        DIM = 256
        B, Q_LEN, KV_LEN = (8, 128, 512)
        key = jax.random.key(seed)
        ks = jax.random.split(key, 8)
        x = jax.random.normal(ks[0], (B, Q_LEN, DIM), dtype=jnp.float32)
        mask = jnp.zeros((B, Q_LEN, KV_LEN + Q_LEN), dtype=bool)
        k_cache = jax.random.normal(ks[1], (B, KV_LEN, DIM), dtype=jnp.float32)
        v_cache = jax.random.normal(ks[2], (B, KV_LEN, DIM), dtype=jnp.float32)
        scale = 1.0 / math.sqrt(DIM)
        wq = jax.random.normal(ks[3], (DIM, DIM), dtype=jnp.float32) * scale
        wk = jax.random.normal(ks[4], (DIM, DIM), dtype=jnp.float32) * scale
        wv = jax.random.normal(ks[5], (DIM, DIM), dtype=jnp.float32) * scale
        wo = jax.random.normal(ks[6], (DIM, DIM), dtype=jnp.float32) * scale
        return {'x': x, 'mask': mask, 'k_cache': k_cache, 'v_cache': v_cache, 'wq': wq, 'wk': wk, 'wv': wv, 'wo': wo}
    _L3_xattn_all = _L3_xattn_setup()
    _L3_xattn_in = {k: v for k, v in _L3_xattn_all.items() if k in ('wq', 'wk', 'wv', 'wo')}
    del _L3_xattn_all

    def _L3_ffn_setup():
        import jax, jax.numpy as jnp
        import numpy as np
        LHS_BITS = 8
        RHS_BITS = 8

        def fake_quant(x, bits, axes):
            qmax = 2.0 ** (bits - 1) - 1.0
            amax = jnp.max(jnp.abs(x), axis=axes, keepdims=True)
            scale = jnp.where(amax > 0, amax / qmax, jnp.ones_like(amax))
            q = jnp.clip(jnp.round(x / scale), -qmax, qmax) * scale
            return x + jax.lax.stop_gradient(q - x)
        key = jax.random.key(seed)
        k1, k2, k3 = jax.random.split(key, 3)
        B, S, D, F = (4, 256, 256, 256)
        x = jax.random.normal(k1, (B, S, D), dtype=jnp.float32)
        kernel = jax.random.normal(k2, (D, F), dtype=jnp.float32) * (1.0 / np.sqrt(D))
        bias = jax.random.normal(k3, (F,), dtype=jnp.float32) * 0.02
        return {'x': x, 'kernel': kernel, 'bias': bias}
    _L3_ffn_all = _L3_ffn_setup()
    _L3_ffn_in = {k: v for k, v in _L3_ffn_all.items() if k in ('kernel', 'bias')}
    del _L3_ffn_all
    return {'x': x, 'ctx_2048': ctx_2048, 'mask_BxS2_bk0': mask_BxS2_bk0, 'mask_BxSx4224_bf0': mask_BxSx4224_bf0, 'L0_xattn_Wq': _L0_xattn_in['Wq'], 'L0_xattn_Wk': _L0_xattn_in['Wk'], 'L0_xattn_Wv': _L0_xattn_in['Wv'], 'L0_ffn_Wr': _L0_ffn_in['Wr'], 'L0_ffn_Wg': _L0_ffn_in['Wg'], 'L0_ffn_Wu': _L0_ffn_in['Wu'], 'L0_ffn_Wd': _L0_ffn_in['Wd'], 'L1_ffn_Wr': _L1_ffn_in['Wr'], 'L1_ffn_Wg': _L1_ffn_in['Wg'], 'L1_ffn_Wu': _L1_ffn_in['Wu'], 'L1_ffn_Wd': _L1_ffn_in['Wd'], 'L2_xattn_Wq': _L2_xattn_in['Wq'], 'L2_xattn_Wk': _L2_xattn_in['Wk'], 'L2_xattn_Wv': _L2_xattn_in['Wv'], 'L2_xattn_Wo': _L2_xattn_in['Wo'], 'L2_xattn_q_norm_w': _L2_xattn_in['q_norm_w'], 'L2_xattn_k_norm_w': _L2_xattn_in['k_norm_w'], 'L2_ffn_wg': _L2_ffn_in['wg'], 'L2_ffn_w1': _L2_ffn_in['w1'], 'L2_ffn_v1': _L2_ffn_in['v1'], 'L2_ffn_w2': _L2_ffn_in['w2'], 'L3_xattn_wq': _L3_xattn_in['wq'], 'L3_xattn_wk': _L3_xattn_in['wk'], 'L3_xattn_wv': _L3_xattn_in['wv'], 'L3_xattn_wo': _L3_xattn_in['wo'], 'L3_ffn_kernel': _L3_ffn_in['kernel'], 'L3_ffn_bias': _L3_ffn_in['bias']}

def reference(x, ctx_2048, mask_BxS2_bk0, mask_BxSx4224_bf0, L0_xattn_Wq, L0_xattn_Wk, L0_xattn_Wv, L0_ffn_Wr, L0_ffn_Wg, L0_ffn_Wu, L0_ffn_Wd, L1_ffn_Wr, L1_ffn_Wg, L1_ffn_Wu, L1_ffn_Wd, L2_xattn_Wq, L2_xattn_Wk, L2_xattn_Wv, L2_xattn_Wo, L2_xattn_q_norm_w, L2_xattn_k_norm_w, L2_ffn_wg, L2_ffn_w1, L2_ffn_v1, L2_ffn_w2, L3_xattn_wq, L3_xattn_wk, L3_xattn_wv, L3_xattn_wo, L3_ffn_kernel, L3_ffn_bias):
    import jax
    import jax.numpy as jnp

    def _L0_xattn_ref(x, context, Wq, Wk, Wv):
        import jax, jax.numpy as jnp
        import numpy as np
        DIM = 256
        NHEADS = 32
        HEAD_DIM = DIM // NHEADS
        EPS = 1e-06

        def _rmsnorm(t):
            return t * jax.lax.rsqrt(jnp.mean(t * t, axis=-1, keepdims=True) + EPS)
        b, n, _ = x.shape
        m = context.shape[1]
        q = x @ Wq.T
        k_raw = context @ Wk.T
        v_raw = context @ Wv.T
        q = q.reshape(b, n, NHEADS, HEAD_DIM).transpose(0, 2, 1, 3)
        kv = jnp.concatenate([k_raw, v_raw], axis=-1)
        kv = kv.reshape(b, m, NHEADS, HEAD_DIM, 2)
        k = kv[..., 0].transpose(0, 2, 1, 3)
        v = kv[..., 1].transpose(0, 2, 1, 3)
        q = _rmsnorm(q)
        k = _rmsnorm(k)
        scale = HEAD_DIM ** (-0.5)
        scores = jnp.einsum('bhnd,bhmd->bhnm', q, k) * scale
        attn = jax.nn.softmax(scores, axis=-1)
        out = jnp.einsum('bhnm,bhmd->bhnd', attn, v)
        return out.transpose(0, 2, 1, 3).reshape(b, n, NHEADS * HEAD_DIM)

    def _L0_ffn_ref(hidden_states, Wr, Wg, Wu, Wd):
        import jax, jax.numpy as jnp
        import numpy as np
        NUM_EXPERTS = 8
        TOP_K = 2
        HIDDEN = 256
        INTER = 256
        SWIGLU_LIMIT = 7.0
        BATCH, SEQ = (4, 256)
        router_logits = jnp.einsum('bsh,he->bse', hidden_states, Wr)
        topk_logits, selected = jax.lax.top_k(router_logits, TOP_K)
        router_probs = jax.nn.softmax(topk_logits, axis=-1)
        out = jnp.zeros_like(hidden_states)
        for e in range(NUM_EXPERTS):
            w_e = jnp.where(selected == e, router_probs, 0.0).sum(axis=-1, keepdims=True)
            g = jnp.einsum('bsh,hi->bsi', hidden_states, Wg[e])
            g = jnp.clip(jax.nn.silu(g), -SWIGLU_LIMIT, SWIGLU_LIMIT)
            u = jnp.einsum('bsh,hi->bsi', hidden_states, Wu[e])
            h = jnp.einsum('bsi,ih->bsh', g * u, Wd[e])
            out = out + h * w_e
        return out

    def _L1_xattn_ref(hidden_states, memory_tokens, memory_mask):
        import jax, jax.numpy as jnp
        import numpy as np
        B, S, D = hidden_states.shape
        scale = 1.0 / jnp.sqrt(jnp.asarray(D, hidden_states.dtype))
        scores = jnp.einsum('bsd,bmd->bsm', hidden_states, memory_tokens) * scale
        neg_inf = jnp.asarray(-1e+30, scores.dtype)
        scores = jnp.where(memory_mask[:, None, :], scores, neg_inf)
        attn = jax.nn.softmax(scores, axis=-1)
        readout = jnp.einsum('bsm,bmd->bsd', attn, memory_tokens)
        valid_b = jnp.any(memory_mask, axis=-1)
        out = jnp.where(valid_b[:, None, None], readout, jnp.zeros_like(readout))
        return out

    def _L1_ffn_ref(x, Wr, Wg, Wu, Wd):
        import jax, jax.numpy as jnp
        import numpy as np
        B, T, D = (4, 256, 256)
        E = 8
        K = 2
        F = 1024 // (E // 2)
        probs = jax.nn.softmax(x @ Wr, axis=-1)
        topk_w, topk_idx = jax.lax.top_k(probs, K)
        topk_w = topk_w / jnp.sum(topk_w, axis=-1, keepdims=True)
        output = jnp.zeros_like(x)
        for i in range(E):
            sel = topk_idx == i
            w_i = jnp.sum(topk_w * sel.astype(x.dtype), axis=-1, keepdims=True)
            h = jax.nn.silu(x @ Wg[i]) * (x @ Wu[i])
            e_out = h @ Wd[i]
            output = output + w_i * e_out
        return output

    def _L2_xattn_ref(hidden_states, encoder_hidden_states, Wq, Wk, Wv, Wo, q_norm_w, k_norm_w):
        import jax, jax.numpy as jnp
        import numpy as np
        HIDDEN = 256
        N_HEADS = 16
        N_KV_HEADS = 4
        HEAD_DIM = 128
        EPS = 1e-06

        def rms_norm(x, w, eps=EPS):
            xf = x.astype(jnp.float32)
            var = jnp.mean(xf * xf, axis=-1, keepdims=True)
            return w * (xf * jax.lax.rsqrt(var + eps)).astype(x.dtype)
        B, S, _ = hidden_states.shape
        S_enc = encoder_hidden_states.shape[1]
        groups = N_HEADS // N_KV_HEADS
        scale = 1.0 / HEAD_DIM ** 0.5
        q = (hidden_states @ Wq).reshape(B, S, N_HEADS, HEAD_DIM)
        k = (encoder_hidden_states @ Wk).reshape(B, S_enc, N_KV_HEADS, HEAD_DIM)
        v = (encoder_hidden_states @ Wv).reshape(B, S_enc, N_KV_HEADS, HEAD_DIM)
        q = rms_norm(q, q_norm_w)
        k = rms_norm(k, k_norm_w)
        k = jnp.repeat(k, groups, axis=2)
        v = jnp.repeat(v, groups, axis=2)
        scores = jnp.einsum('bqhd,bkhd->bhqk', q, k) * scale
        probs = jax.nn.softmax(scores, axis=-1)
        out = jnp.einsum('bhqk,bkhd->bqhd', probs, v)
        out = out.reshape(B, S, N_HEADS * HEAD_DIM)
        return out @ Wo

    def _L2_ffn_ref(hidden_states, wg, w1, v1, w2):
        import jax, jax.numpy as jnp
        import numpy as np
        E = 32
        K = 8
        H = 256
        F = 96
        B, S = (1, 128)

        def _moe(x, wg, w1, v1, w2):
            T = x.shape[0]
            logits = x @ wg.T
            scores = jax.nn.softmax(logits, axis=-1)
            weights, idx = jax.lax.top_k(scores, K)
            weights = weights / jnp.sum(weights, axis=-1, keepdims=True)
            flat_e = idx.reshape(-1)
            flat_t = jnp.repeat(jnp.arange(T), K)
            flat_w = weights.reshape(-1)
            order = jnp.argsort(flat_e)
            e_s = flat_e[order]
            t_s = flat_t[order]
            w_s = flat_w[order]
            group_sizes = jnp.bincount(e_s, length=E).astype(jnp.int32)
            xs = x[t_s]
            g = jax.lax.ragged_dot(xs, w1, group_sizes)
            u = jax.lax.ragged_dot(xs, v1, group_sizes)
            h = jax.nn.silu(g) * u
            ys = jax.lax.ragged_dot(h, w2, group_sizes)
            out = jnp.zeros((T, x.shape[1]), x.dtype).at[t_s].add(ys * w_s[:, None])
            return out
        Bb, Ss, Hh = hidden_states.shape
        x = hidden_states.reshape(Bb * Ss, Hh)
        out = _moe(x, wg, w1, v1, w2)
        return out.reshape(Bb, Ss, Hh)

    def _L3_xattn_ref(x, mask, k_cache, v_cache, wq, wk, wv, wo):
        import jax, jax.numpy as jnp
        import numpy as np
        import math
        DIM = 256
        B, Q_LEN, KV_LEN = (8, 128, 512)
        q = jnp.einsum('bsd,ed->bse', x, wq)
        k_new = jnp.einsum('bsd,ed->bse', x, wk)
        v_new = jnp.einsum('bsd,ed->bse', x, wv)
        k = jnp.concatenate([k_cache, k_new], axis=1)
        v = jnp.concatenate([v_cache, v_new], axis=1)
        scale = 1.0 / math.sqrt(q.shape[-1])
        scores = jnp.einsum('bqd,bkd->bqk', q, k) * scale
        attn = jax.nn.softmax(scores, axis=-1)
        out = jnp.einsum('bqk,bkd->bqd', attn, v)
        return jnp.einsum('bqd,ed->bqe', out, wo)

    def _L3_ffn_ref(x, kernel, bias):
        import jax, jax.numpy as jnp
        import numpy as np
        LHS_BITS = 8
        RHS_BITS = 8

        def fake_quant(x, bits, axes):
            qmax = 2.0 ** (bits - 1) - 1.0
            amax = jnp.max(jnp.abs(x), axis=axes, keepdims=True)
            scale = jnp.where(amax > 0, amax / qmax, jnp.ones_like(amax))
            q = jnp.clip(jnp.round(x / scale), -qmax, qmax) * scale
            return x + jax.lax.stop_gradient(q - x)
        bq = fake_quant(bias, RHS_BITS, -1)
        xq = fake_quant(x, LHS_BITS, -1)
        kq = fake_quant(kernel, RHS_BITS, 0)
        y = jnp.einsum('bsd,df->bsf', xq, kq)
        y = y + bq[None, None, :]
        y = jax.nn.relu(y)
        return fake_quant(y, LHS_BITS, -1)
    x = x + _L0_xattn_ref(_layernorm(x, axis=-1), ctx_2048, L0_xattn_Wq, L0_xattn_Wk, L0_xattn_Wv)
    x = x + _L0_ffn_ref(_layernorm(x, axis=-1), L0_ffn_Wr, L0_ffn_Wg, L0_ffn_Wu, L0_ffn_Wd)
    x = x + _L1_xattn_ref(_layernorm(x, axis=-1), ctx_2048, mask_BxS2_bk0)
    x = x + _L1_ffn_ref(_layernorm(x, axis=-1), L1_ffn_Wr, L1_ffn_Wg, L1_ffn_Wu, L1_ffn_Wd)
    x = x + _L2_xattn_ref(_layernorm(x, axis=-1), ctx_2048, L2_xattn_Wq, L2_xattn_Wk, L2_xattn_Wv, L2_xattn_Wo, L2_xattn_q_norm_w, L2_xattn_k_norm_w)
    x = x + _L2_ffn_ref(_layernorm(x, axis=-1), L2_ffn_wg, L2_ffn_w1, L2_ffn_v1, L2_ffn_w2)
    x = x + _L3_xattn_ref(_layernorm(x, axis=-1), mask_BxSx4224_bf0, ctx_2048, ctx_2048, L3_xattn_wq, L3_xattn_wk, L3_xattn_wv, L3_xattn_wo)
    x = x + _L3_ffn_ref(_layernorm(x, axis=-1), L3_ffn_kernel, L3_ffn_bias)
    return x

_drawn_inputs = setup_inputs


def setup_inputs(seed=0):
    import zlib

    import numpy as np

    out = dict(_drawn_inputs(seed))
    spreads = {'L2_xattn_q_norm_w': (1.0, 0.6), 'L2_xattn_k_norm_w': (1.0, 0.6)}
    factors = {'L0_ffn_Wr': 2.789,
     'L2_ffn_wg': 8.0,
     'L2_ffn_w1': 8.0,
     'L2_ffn_v1': 8.0,
     'L2_ffn_w2': 8.0,
     'L3_xattn_wk': 2.682,
     'L3_ffn_bias': 17.996}
    for name, (base, spread) in spreads.items():
        noise = np.random.default_rng([zlib.crc32(name.encode()), seed]).standard_normal(out[name].shape)
        drawn = base * np.exp(spread * noise) if base else spread * noise
        out[name] = jnp.asarray(drawn.astype(out[name].dtype))
    for name, factor in factors.items():
        out[name] = (out[name] * factor).astype(out[name].dtype)
    return out
```

```python
from contextlib import ExitStack

import concourse.bass as bass
from concourse import mybir

F32 = mybir.dt.float32
F16 = mybir.dt.float16
U8 = mybir.dt.uint8
U32 = mybir.dt.uint32
ALU = mybir.AluOpType
ACT = mybir.ActivationFunctionType
AX = mybir.AxisListType

B = 16
S = 100
D = 256
M = 1444
P = 128
DC = D // P
MT = -(-M // P)
LAST = M - P * (MT - 2)
MSZ = [P] * (MT - 2) + [(LAST // 2 + 3) // 4 * 4, LAST - (LAST // 2 + 3) // 4 * 4]
MOFF = [sum(MSZ[:t]) for t in range(MT)]
BANK = 512
CH = 4
NCH = B // CH
CT = CH * S
LN_EPS = 1e-5
LN_EXP = "natural_log_exp_and_others"
RMS_EPS = 1e-6


def val(i, step, const):
    return const if i is None else i * step + const


def equal_runs(sizes, start, end):
    runs = []
    for t in range(start, end):
        if runs and sizes[runs[-1][0]] == sizes[t]:
            runs[-1][1] += 1
        else:
            runs.append([t, 1])
    return runs


def wait(eng, sem, value):
    if isinstance(value, int) and value <= 0:
        return
    eng.wait_ge(sem, value)


def pipeline(eng, items, period, lag, step, peel):
    rounds = (items - peel) // period
    for s in range(peel):
        step(s, None)
    with eng.Fori(0, rounds) as i:
        for s in range(peel, peel + period):
            step(s, i)
    for s in range(peel + rounds * period, items + lag):
        step(s, None)


class Kernel:

    def __init__(self, nc, ctx):
        self.nc, self.ctx, self.sems = nc, ctx, []
        self.X = self.sb("X", [S, B, D])
        self.XT = self.sb("XT", [P, DC, B * S])
        self.ident = self.sb("ident", [P, P])
        self.ident16 = self.sb("ident16", [P, P], F16)
        self.eps = self.sb("eps", [P, 2])
        self.psum = ctx.enter_context(nc.psum_tensor("psum", [P, 8, BANK], F32))

    def sb(self, name, shape, dt=F32):
        return self.ctx.enter_context(self.nc.sbuf_tensor(name, shape, dt))

    def sem(self, name):
        self.sems.append(self.nc.alloc_semaphore(name=name))
        return self.sems[-1]

    def recycle_semaphores(self):
        for s in self.sems:
            self.nc.sync.sem_clear(s)
            self.nc.release_semaphore(s)
        self.sems = []
        self.nc.all_engine_barrier()


def setup(k, x_dram):
    nc = k.nc
    x_in, made, id0 = k.sem("x_in"), k.sem("made"), k.sem("id0")
    with nc.Block() as block:
        @block.sync
        def _(sp):
            sp.dma_start(k.X[:], x_dram.rearrange("b s d -> s b d")).then_inc(x_in, 16)
            sp.wait_ge(x_in, 16)

        @block.gpsimd
        def _(pool):
            nc.gpsimd.memset(k.ident[:], 0.0).then_inc(id0, 1)
            pool.wait_ge(id0, 1)
            nc.gpsimd.affine_select(out=k.ident[:], in_=k.ident[:], compare_op=ALU.not_equal, fill=1.0,
                                    base=0, pattern=[[-1, P]], channel_multiplier=1).then_inc(made, 1)

        @block.vector
        def _(dve):
            nc.vector.memset(k.eps[:, 0:1], LN_EPS)
            nc.vector.memset(k.eps[:, 1:2], RMS_EPS)
            dve.wait_ge(made, 1)
            nc.vector.tensor_copy(k.ident16[:], k.ident[:]).then_inc(made, 1)


def layernorm_transposed(k, tag):
    nc = k.nc
    with ExitStack() as ctx:
        k2 = lambda name, shape, dt=F32: ctx.enter_context(nc.sbuf_tensor(f"{tag}_{name}", shape, dt))
        stats = k2("stats", [S, B, 6])
        mv = k2("mv", [S, B, 2])
        lnv = k2("lnv", [S, B])
        rstd = k2("rstd", [S, B])
        xn = k2("xn", [S, CH, D])
        sem = lambda name: k.sem(f"{tag}_{name}")
        stats_ready, mv_ready, lnv_ready, rstd_ready = sem("stats"), sem("mvr"), sem("lnvr"), sem("rstdr")
        xn_ready, xt_done, xt_read = sem("xnr"), sem("xtd"), sem("xtr")
        with nc.Block() as block:
            @block.vector
            def _(dve):
                with nc.vector.Fori(0, B) as b:
                    nc.vector.bn_stats(stats[:, bass.ds(b, 1), :], k.X[:, bass.ds(b, 1), :]).then_inc(stats_ready, 1)
                for b in range(B):
                    dve.wait_ge(stats_ready, b + 1)
                    nc.vector.bn_aggr(mv[:, b, :], stats[:, b, :]).then_inc(mv_ready, 1)
                dve.wait_ge(rstd_ready, 1)
                with nc.vector.Fori(0, NCH) as c:
                    dve.wait_ge(xt_done, c + 1)
                    for j in range(CH):
                        nc.vector.tensor_scalar(xn[:, j, :], k.X[:, bass.ds(c * CH + j, 1), :].rearrange("p a d -> p (a d)"),
                                                mv[:, bass.ds(c * CH + j, 1), 0], rstd[:, bass.ds(c * CH + j, 1)],
                                                ALU.subtract, ALU.mult).then_inc(xn_ready, 1)

            @block.scalar
            def _(act):
                nc.scalar.preload_act_table_set(LN_EXP)
                act.sem_inc(xt_read, 1)
                act.wait_ge(mv_ready, B)
                nc.scalar.activation(lnv[:], mv[:, :, 1], ACT.Ln, bias=k.eps[0:S, 0:1]).then_inc(lnv_ready, 1)
                act.wait_ge(lnv_ready, 1)
                nc.scalar.activation(rstd[:], lnv[:], ACT.Exp, scale=-0.5).then_inc(rstd_ready, 1)
                with nc.scalar.Fori(0, NCH) as c:
                    act.wait_ge(xt_done, c + 2)
                    for w in range(DC):
                        last = nc.scalar.activation(k.XT[:, w, bass.ds(c * CT, CT)], k.psum[:, w, 0:CT], ACT.Copy)
                    last.then_inc(xt_read, 1)

            @block.tensor
            def _(pe):
                pe.sem_inc(xt_done, 1)
                with nc.tensor.Fori(0, NCH) as c:
                    pe.wait_ge(xt_read, c + 1)
                    for j in range(CH):
                        pe.wait_ge(xn_ready, c * CH + j + 1)
                        for w in range(DC):
                            last = nc.tensor.transpose(k.psum[:, w, j * S:(j + 1) * S], xn[:, j, w * P:(w + 1) * P],
                                                       k.ident[0:S, 0:S])
                    last.then_inc(xt_done, 1)


def store(k, out_dram):
    nc = k.nc
    stored = k.sem("stored")
    with nc.Block() as block:
        @block.sync
        def _(sp):
            sp.dma_start(out_dram.rearrange("b s d -> s b d"), k.X[:]).then_inc(stored, 16)
            sp.wait_ge(stored, 16)


H0, HD0 = 32, 8
G0 = H0 // 4
SPLIT = 4
PERIOD = 2 * MT


def heads32_queries(k, WqT_dram, QT):
    nc = k.nc
    with ExitStack() as ctx:
        sb = lambda name, shape, dt=F32: ctx.enter_context(nc.sbuf_tensor(f"q0_{name}", shape, dt))
        sem = lambda name: k.sem(f"q0_{name}")
        Wq = sb("Wq", [P, DC, D])
        xb = sb("xb", [P, 2, DC, S])
        sq = sb("sq", [S, 2, D])
        ssq = sb("ssq", [S, 2, H0])
        lnq = sb("lnq", [S, 2, H0])
        rq = sb("rq", [S, 2, H0])
        qn = sb("qn", [S, 2, H0, HD0])
        qs = sb("qs", [S, 2, H0, SPLIT, HD0], F16)
        w_in, xb_ready, q_done, sq_ready, ssq_ready = sem("w_in"), sem("xb"), sem("q"), sem("sq"), sem("ssq")
        ln_ready, rq_ready, qn_ready, qh_ready, qs_ready = sem("ln"), sem("rq"), sem("qn"), sem("qh"), sem("qs")
        qt_done, qt_read = sem("qt"), sem("qtr")
        psum16 = k.psum[:, 2:4, :].bitcast(F16)
        with nc.Block() as block:
            @block.sync
            def _(sp):
                sp.dma_start(Wq[:], WqT_dram.rearrange("(c p) n -> p c n", p=P)).then_inc(w_in, 16)
                sp.wait_ge(w_in, 16)

            @block.tensor
            def _(pe):
                pe.wait_ge(w_in, 16)
                with nc.tensor.Fori(0, B // 2) as i:
                    for j in range(2):
                        pe.wait_ge(xb_ready, i * 2 + j + 1)
                        for w in range(DC):
                            last = nc.tensor.matmul(k.psum[0:S, j, 0:D], xb[:, j, w, :], Wq[:, w, :],
                                                    start=(w == 0), stop=(w == DC - 1))
                        last.then_inc(q_done, 1)
                    for j in range(2):
                        pe.wait_ge(qs_ready, i * 2 + j + 1)
                        flat = qs[:, j, :, :, :].rearrange("p h s d -> p (h s d)")
                        for g in range(G0):
                            last = nc.tensor.transpose(psum16[:, j, g * P:g * P + S], flat[:, g * P:(g + 1) * P],
                                                       k.ident16[0:S, 0:S])
                        last.then_inc(qt_done, 1)

            @block.scalar
            def _(act):
                nc.scalar.preload_act_table_set(LN_EXP)
                with nc.scalar.Fori(0, B // 2) as i:
                    act.wait_ge(qt_read, i * 2 + 1)
                    for j in range(2):
                        nc.scalar.activation(xb[:, j, :, :], k.XT[:, :, bass.ds(i * (2 * S) + j * S, S)],
                                             ACT.Copy).then_inc(xb_ready, 1)
                    for j in range(2):
                        act.wait_ge(q_done, i * 2 + j + 1)
                        nc.scalar.activation(sq[:, j, :], k.psum[0:S, j, 0:D], ACT.Square).then_inc(sq_ready, 1)
                    for j in range(2):
                        act.wait_ge(ssq_ready, i * 2 + j + 1)
                        nc.scalar.activation(lnq[:, j, :], ssq[:, j, :], ACT.Ln, scale=1.0 / HD0,
                                             bias=k.eps[0:S, 1:2]).then_inc(ln_ready, 1)
                        act.wait_ge(ln_ready, i * 2 + j + 1)
                        nc.scalar.activation(rq[:, j, :], lnq[:, j, :], ACT.Exp, scale=-0.5).then_inc(rq_ready, 1)

            @block.vector
            def _(dve):
                dve.sem_inc(qt_read, 1)
                with nc.vector.Fori(0, B // 2) as i:
                    for j in range(2):
                        dve.wait_ge(sq_ready, i * 2 + j + 1)
                        nc.vector.reduce_sum(ssq[:, j, :], sq[:, j, :].rearrange("p (h d) -> p h d", d=HD0),
                                             AX.X).then_inc(ssq_ready, 1)
                    for j in range(2):
                        dve.wait_ge(rq_ready, i * 2 + j + 1)
                        q = k.psum[0:S, j, 0:D].rearrange("p (h d) -> p h d", d=HD0)
                        nc.vector.tensor_tensor(qn[:, j, :, :], q, rq[:, j, :].unsqueeze(2).to_broadcast([S, H0, HD0]),
                                                ALU.mult).then_inc(qn_ready, 1)
                        dve.wait_ge(qn_ready, i * 2 + j + 1)
                        wide = qn[:, j, :, :].unsqueeze(2).to_broadcast([S, H0, 2, HD0])
                        nc.vector.tensor_scalar(qs[:, j, :, 0:2, :], wide, HD0 ** -0.5, None, ALU.mult).then_inc(qh_ready, 1)
                        dve.wait_ge(qh_ready, i * 2 + j + 1)
                        for part in range(2):
                            last = nc.vector.scalar_tensor_tensor(
                                qs[:, j, :, 2 + part, :], qn[:, j, :, :], HD0 ** -0.5, qs[:, j, :, part, :],
                                ALU.mult, ALU.subtract)
                        last.then_inc(qs_ready, 1)
                    for j in range(2):
                        dve.wait_ge(qt_done, i * 2 + j + 1)
                        src = psum16[:, j, :].rearrange("p (g n) -> p g n", g=G0)[:, :, 0:S]
                        nc.vector.tensor_copy(QT[:, bass.ds(i * 2 + j, 1), :, :].rearrange("p a g n -> p (a g) n"),
                                              src).then_inc(qt_read, 1)


def heads32_attention(k, ctxT_dram, WkvT_dram, QT):
    nc = k.nc
    NT = B * MT
    LT, LS, LV, LO = 2, 3, 4, 5
    VS = 6
    with ExitStack() as ctx:
        sb = lambda name, shape, dt=F32: ctx.enter_context(nc.sbuf_tensor(f"a0_{name}", shape, dt))
        sem = lambda name: k.sem(f"a0_{name}")
        Wkv = sb("Wkv", [P, DC, 2 * D])
        ctxT = sb("ctxT", [P, 2, DC, M])
        ksq = sb("ksq", [P, D])
        ssq = sb("ssq", [P, H0])
        lnk = sb("lnk", [P, H0])
        rk = sb("rk", [P, H0])
        kn = sb("kn", [P, H0, HD0])
        ks = sb("ks", [P, 2, H0, SPLIT, HD0], F16)
        kt = sb("kt", [P, 2, G0, P], F16)
        qbd = sb("qbd", [P, 2, G0, 4, S], F16)
        vs = sb("vs", [P, VS, H0, 32])
        pr = sb("pr", [P, 2, 4, 2, 4 * S])
        ot = sb("ot", [P, 2, 4 * S])
        rs = sb("rs", [S, 2, H0 // 2])
        on = sb("on", [S, 2, H0 // 2, HD0])
        w_in, ctx_in = sem("w_in"), [sem("ctx_in0"), sem("ctx_in1")]
        kv_done, v_ready, sq_ready, ssq_ready, ln_ready, rk_ready = (sem(n) for n in ("kv", "v", "sq", "ssq", "ln", "rk"))
        kn_ready, kh_ready, ks_ready, kt_done, kt_ready = (sem(n) for n in ("kn", "kh", "ks", "ktd", "ktr"))
        qbd_clear, qbd_ready, s_done, exp_done, pv_done = (sem(n) for n in ("qclr", "qbd", "s", "exp", "pv"))
        ot_ready, o_done, o_read, rs_ready, on_ready, x_ready = (sem(n) for n in ("ot", "o", "oread", "rs", "on", "x"))
        vs_clear = sem("vsclr")
        KV, KT, SC, PV = 0, 1, 2, 6
        ktp = k.psum[:, KT, :].bitcast(F16)

        with nc.Block() as block:
            @block.sync
            def _(sp):
                sp.dma_start(Wkv[:], WkvT_dram.rearrange("(c p) n -> p c n", p=P)).then_inc(w_in, 16)

                def load(j, i):
                    wait(sp, kv_done, val(i, PERIOD, (j - 1) * MT))
                    src = ctxT_dram[j] if i is None else ctxT_dram[bass.ds(i * 2 + j, 1)].rearrange("a d m -> (a d) m")
                    sp.dma_start(ctxT[:, j % 2, :, :], src.rearrange("(c p) m -> p c m", p=P)).then_inc(ctx_in[j % 2], 16)

                load(0, None)
                load(1, None)
                with nc.sync.Fori(0, B // 2 - 1) as i:
                    load(2, i)
                    load(3, i)

            @block.gpsimd
            def _(pool):
                nc.gpsimd.memset(qbd[:], 0.0).then_inc(qbd_clear, 1)
                pool.wait_ge(qbd_clear, 1)

                def spread(j, i):
                    wait(pool, s_done, val(i, PERIOD * 4, (j - 1) * MT * 4))
                    for h in range(4):
                        rows = slice(32 * h, 32 * h + 32)
                        src = QT[rows, j] if i is None else QT[rows, bass.ds(i * 2 + j, 1)].rearrange("p a g n -> p (a g) n")
                        last = nc.gpsimd.tensor_copy(qbd[rows, j % 2, :, h, :], src)
                    last.then_inc(qbd_ready, 1)

                spread(0, None)
                spread(1, None)
                with nc.gpsimd.Fori(0, B // 2 - 1) as i:
                    spread(2, i)
                    spread(3, i)

            @block.tensor
            def _(pe):
                pe.wait_ge(w_in, 16)
                pe.wait_ge(vs_clear, 2)

                def project(n, i):
                    b, t = divmod(n, MT)
                    if t == 0:
                        pe.wait_ge(ctx_in[b % 2], val(i, 16, 16 * (b // 2 + 1)))
                    wait(pe, kn_ready, val(i, PERIOD, n))
                    wait(pe, v_ready, val(i, PERIOD, n))
                    for w in range(DC):
                        last = nc.tensor.matmul(k.psum[0:MSZ[t], KV, :], ctxT[:, b % 2, w, MOFF[t]:MOFF[t] + MSZ[t]],
                                                Wkv[:, w, :], start=(w == 0), stop=(w == DC - 1))
                    last.then_inc(kv_done, 1)

                def transpose(n, i):
                    t = n % MT
                    pe.wait_ge(ks_ready, val(i, PERIOD, n + 1))
                    wait(pe, kt_ready, val(i, PERIOD, n))
                    flat = ks[:, n % 2, :, :, :].rearrange("p h s d -> p (h s d)")
                    for g in range(G0):
                        last = nc.tensor.transpose(ktp[:, g * P:g * P + MSZ[t]], flat[0:MSZ[t], g * P:(g + 1) * P],
                                                   k.ident16[0:MSZ[t], 0:MSZ[t]])
                    last.then_inc(kt_done, 1)

                def scores(n, r, i):
                    b, t = divmod(n, MT)
                    if r == 0:
                        pe.wait_ge(kt_ready, val(i, PERIOD, n + 1))
                        if t == 0:
                            pe.wait_ge(qbd_ready, val(i, 2, b + 1))
                    if t == 1 and r < 2 and (b > 0 or i is not None):
                        pe.wait_ge(o_read, val(i, 4, 2 * (b - 1) + r + 1))
                    wait(pe, exp_done, val(i, PERIOD * 4, 4 * n + r - 1))
                    for g in (2 * r, 2 * r + 1):
                        last = nc.tensor.matmul(k.psum[0:MSZ[t], SC + 2 * (r % 2) + g % 2, 0:4 * S],
                                                kt[:, n % 2, g, 0:MSZ[t]],
                                                qbd[:, b % 2, g, :, :].rearrange("p h n -> p (h n)"),
                                                start=True, stop=True)
                    last.then_inc(s_done, 1)

                def values(n, r, i):
                    b, t = divmod(n, MT)
                    if r == 0:
                        pe.wait_ge(v_ready, val(i, PERIOD, n + 1))
                        if t == 0:
                            wait(pe, ot_ready, val(i, 4, 2 * b))
                    pe.wait_ge(exp_done, val(i, PERIOD * 4, 4 * n + r + 1))
                    for g in (2 * r, 2 * r + 1):
                        for h in range(4):
                            last = nc.tensor.matmul(
                                k.psum[32 * h:32 * h + 32, PV + g // 4, (g % 4) * S:(g % 4 + 1) * S],
                                vs[0:MSZ[t], n % VS, 4 * g + h, :], pr[0:MSZ[t], n % 2, r, g % 2, h * S:(h + 1) * S],
                                start=(t == 0 and g % 4 == 0), stop=(t == MT - 1), skip_group_check=True)
                    if r == 3:
                        last.then_inc(pv_done, 1)

                def outputs(n, i):
                    b = n // MT
                    for r in range(2):
                        pe.wait_ge(ot_ready, val(i, 4, 2 * b + r + 1))
                        pe.wait_ge(exp_done, val(i, PERIOD * 4, 4 * (min(n + 1, NT - 1 if i is None else n + 1)) + 3 + r))
                        for g in range(4):
                            last = nc.tensor.transpose(k.psum[0:S, SC + 2 * r, g * P:(g + 1) * P],
                                                       ot[:, r, g * S:(g + 1) * S], k.ident[:])
                        last.then_inc(o_done, 1)

                def step(s, i):
                    if s - LO >= 0 and (s - LO) % MT == MT - 1:
                        outputs(s - LO, i)
                    for r in range(4):
                        if s >= LS and (i is not None or s - LS < NT):
                            scores(s - LS, r, i)
                        if r == 0 and (i is not None or s < NT):
                            project(s, i)
                        if r == 1 and s >= LT and (i is not None or s - LT < NT):
                            transpose(s - LT, i)
                        if s >= LV and (i is not None or s - LV < NT):
                            values(s - LV, r, i)

                pipeline(nc.tensor, NT, PERIOD, LO, step, peel=MT + LO + 1)

            @block.scalar
            def _(act):
                nc.scalar.preload_act_table_set(LN_EXP)
                act.wait_ge(vs_clear, 2)

                def keys_values(n, i):
                    t = n % MT
                    m = MSZ[t]
                    act.wait_ge(kv_done, val(i, PERIOD, n + 1))
                    kv = k.psum[0:m, KV, :].rearrange("p (h d two) -> p two h d", h=H0, two=2)
                    nc.scalar.activation(ksq[0:m, :].rearrange("p (h d) -> p h d", h=H0), kv[:, 0], ACT.Square).then_inc(sq_ready, 1)
                    wait(act, pv_done, val(i, PERIOD, n - VS + 1))
                    nc.scalar.activation(vs[0:m, n % VS, :, 0:HD0], kv[:, 1], ACT.Copy).then_inc(v_ready, 1)

                def norm(n, i):
                    m = MSZ[n % MT]
                    act.wait_ge(ssq_ready, val(i, PERIOD, n + 1))
                    nc.scalar.activation(lnk[0:m, :], ssq[0:m, :], ACT.Ln, scale=1.0 / HD0,
                                         bias=k.eps[0:m, 1:2]).then_inc(ln_ready, 1)
                    act.wait_ge(ln_ready, val(i, PERIOD, n + 1))
                    nc.scalar.activation(rk[0:m, :], lnk[0:m, :], ACT.Exp, scale=-0.5).then_inc(rk_ready, 1)

                def exps(n, r, i):
                    m = MSZ[n % MT]
                    if r == 0:
                        wait(act, pv_done, val(i, PERIOD, n - 1))
                    act.wait_ge(s_done, val(i, PERIOD * 4, 4 * n + r + 1))
                    bank = SC + 2 * (r % 2)
                    nc.scalar.activation(pr[0:m, n % 2, r, :, :], k.psum[0:m, bank:bank + 2, 0:4 * S],
                                         ACT.Exp).then_inc(exp_done, 1)

                def step(s, i):
                    live = s >= LS and (i is not None or s - LS < NT)
                    for r in range(4):
                        if live:
                            exps(s - LS, r, i)
                        if r == 0 and (i is not None or s < NT):
                            keys_values(s, i)
                        if r == 1 and (i is not None or s < NT):
                            norm(s, i)

                pipeline(nc.scalar, NT, PERIOD, LO, step, peel=MT + LO + 1)

            @block.vector
            def _(dve):
                nc.vector.memset(vs[:], 0.0).then_inc(vs_clear, 1)
                dve.wait_ge(vs_clear, 1)
                nc.vector.memset(vs[:, :, :, HD0:HD0 + 1], 1.0).then_inc(vs_clear, 1)

                def keys(n, i):
                    t = n % MT
                    m = MSZ[t]
                    dve.wait_ge(sq_ready, val(i, PERIOD, n + 1))
                    nc.vector.reduce_sum(ssq[0:m, :], ksq[0:m, :].rearrange("p (h d) -> p h d", d=HD0),
                                         AX.X).then_inc(ssq_ready, 1)

                def split(n, i):
                    m = MSZ[n % MT]
                    dve.wait_ge(rk_ready, val(i, PERIOD, n + 1))
                    keys = k.psum[0:m, KV, :].rearrange("p (h d two) -> p two h d", h=H0, two=2)[:, 0]
                    nc.vector.tensor_tensor(kn[0:m], keys, rk[0:m, :].unsqueeze(2).to_broadcast([m, H0, HD0]),
                                            ALU.mult).then_inc(kn_ready, 1)
                    dve.wait_ge(kn_ready, val(i, PERIOD, n + 1))
                    wait(dve, kt_done, val(i, PERIOD, n - 1))
                    for part in range(2):
                        last = nc.vector.tensor_copy(ks[0:m, n % 2, :, 2 * part, :], kn[0:m])
                    last.then_inc(kh_ready, 1)
                    dve.wait_ge(kh_ready, val(i, PERIOD, n + 1))
                    for part in range(2):
                        last = nc.vector.tensor_tensor(ks[0:m, n % 2, :, 2 * part + 1, :], kn[0:m],
                                                       ks[0:m, n % 2, :, 2 * part, :], ALU.subtract)
                    last.then_inc(ks_ready, 1)

                def keys_out(n, i):
                    m = MSZ[n % MT]
                    dve.wait_ge(kt_done, val(i, PERIOD, n + 1))
                    wait(dve, s_done, val(i, PERIOD * 4, 4 * (n - 1)))
                    nc.vector.tensor_copy(kt[:, n % 2, :, 0:m], ktp.rearrange("p (g m) -> p g m", g=G0)[:, :, 0:m]).then_inc(kt_ready, 1)

                def outputs_out(n, i):
                    b = n // MT
                    dve.wait_ge(pv_done, val(i, PERIOD, n + 1))
                    for r in range(2):
                        wait(dve, o_done, val(i, 4, 2 * b))
                        nc.vector.tensor_copy(ot[:, r, :], k.psum[:, PV + r, 0:4 * S]).then_inc(ot_ready, 1)

                def add(n, i):
                    b = n // MT
                    for r in range(2):
                        dve.wait_ge(o_done, val(i, 4, 2 * b + r + 1))
                        o = k.psum[0:S, SC + 2 * r, :].rearrange("p (h e) -> p h e", e=32)
                        nc.vector.reciprocal(rs[:, r, :], o[:, :, HD0]).then_inc(rs_ready, 1)
                        dve.wait_ge(rs_ready, val(i, 4, 2 * b + r + 1))
                        nc.vector.tensor_tensor(on[:, r, :, :], o[:, :, 0:HD0],
                                                rs[:, r, :].unsqueeze(2).to_broadcast([S, H0 // 2, HD0]),
                                                ALU.mult).then_inc(o_read, 1)
                        dve.wait_ge(o_read, val(i, 4, 2 * b + r + 1))
                        half = slice(r * D // 2, (r + 1) * D // 2)
                        xb = k.X[:, b, half] if i is None else k.X[:, bass.ds(i * 2 + b, 1), half].rearrange("p a d -> p (a d)")
                        nc.vector.tensor_tensor(xb, xb, on[:, r, :, :].rearrange("p h d -> p (h d)"), ALU.add).then_inc(x_ready, 1)

                def step(s, i):
                    if s - LO >= 0 and (s - LO) % MT == MT - 1:
                        add(s - LO, i)
                    if i is not None or s < NT:
                        keys(s, i)
                    if s >= LT and (i is not None or s - LT < NT):
                        keys_out(s - LT, i)
                    if i is not None or s < NT:
                        split(s, i)
                    if s >= LV and (s - LV) % MT == MT - 1:
                        outputs_out(s - LV, i)

                pipeline(nc.vector, NT, PERIOD, LO, step, peel=MT + LO + 1)


def router(k, tag, Wr_dram, E, K, WE):
    nc = k.nc
    with ExitStack() as ctx:
        sb = lambda name, shape, dt=F32: ctx.enter_context(nc.sbuf_tensor(f"{tag}_{name}", shape, dt))
        sem = lambda name: k.sem(f"{tag}_{name}")
        Wr = sb("Wr", [P, DC, E])
        logit = sb("logit", [S, B, E])
        top = sb("top", [S, B, 8])
        left = sb("left", [S, B, E])
        arg = sb("arg", [S, B, 8], U32)
        argf = sb("argf", [S, B, 8])
        shift = sb("shift", [S, B, E])
        ex = sb("ex", [S, B, E])
        total = sb("total", [S, B])
        w_in, l_done, step, ex_ready = sem("w_in"), sem("l"), sem("step"), sem("ex")
        bank = 0
        wide = lambda ap: ap.to_broadcast([S, B, E])

        with nc.Block() as block:
            @block.sync
            def _(sp):
                sp.dma_start(Wr[:], Wr_dram.rearrange("(c p) n -> p c n", p=P)).then_inc(w_in, 16)
                sp.wait_ge(w_in, 16)

            @block.tensor
            def _(pe):
                pe.wait_ge(w_in, 16)
                for b in range(B):
                    for w in range(DC):
                        last = nc.tensor.matmul(k.psum[0:S, bank, b * E:(b + 1) * E], k.XT[:, w, b * S:(b + 1) * S],
                                                Wr[:, w, :], start=(w == 0), stop=(w == DC - 1))
                last.then_inc(l_done, 1)

            @block.scalar
            def _(act):
                act.wait_ge(step, 1 + 2 * B if K == 8 else 1 + B)
                act.wait_ge(ex_ready, 1)
                nc.scalar.activation(ex[:], shift[:], ACT.Exp).then_inc(ex_ready, 1)

            @block.vector
            def _(dve):
                count = [0]

                def link(ins):
                    count[0] += 1
                    ins.then_inc(step, 1)
                    dve.wait_ge(step, count[0])

                dve.wait_ge(l_done, 1)
                link(nc.vector.tensor_copy(logit[:], k.psum[0:S, bank, 0:B * E].rearrange("p (b e) -> p b e", b=B)))
                for b in range(B):
                    last = nc.vector.max(top[:, b, :], logit[:, b, :])
                    last.then_inc(step, 1)
                count[0] += B
                dve.wait_ge(step, count[0])
                for b in range(B):
                    if K == 8:
                        last = nc.vector.match_replace(out=left[:, b, :], in_to_replace=top[:, b, :],
                                                       in_values=logit[:, b, :], imm_value=-3.0e38)
                    else:
                        last = nc.vector.max_index(arg[:, b, :], top[:, b, :], logit[:, b, :])
                    last.then_inc(step, 1)
                count[0] += B
                dve.wait_ge(step, count[0])
                if K == 8:
                    link(nc.vector.tensor_tensor(left[:], left[:], logit[:], ALU.not_equal))
                else:
                    link(nc.vector.tensor_copy(argf[:], arg[:]))
                    for e in range(E):
                        last = nc.vector.memset(shift[:, :, e:e + 1], float(e))
                    link(last)
                    link(nc.vector.tensor_tensor(left[:], shift[:], wide(argf[:, :, 0:1]), ALU.is_equal))
                    link(nc.vector.tensor_tensor(ex[:], shift[:], wide(argf[:, :, 1:2]), ALU.is_equal))
                    link(nc.vector.tensor_tensor(left[:], left[:], ex[:], ALU.add))
                nc.vector.tensor_tensor(shift[:], logit[:], wide(top[:, :, 0:1]), ALU.subtract).then_inc(ex_ready, 1)
                dve.wait_ge(ex_ready, 2)
                link(nc.vector.tensor_tensor(ex[:], ex[:], left[:], ALU.mult))
                link(nc.vector.reduce_sum(total[:], ex[:], AX.X))
                link(nc.vector.reciprocal(total[:], total[:]))
                link(nc.vector.tensor_scalar(total[:], total[:], 0.5, None, ALU.mult))
                link(nc.vector.tensor_tensor(WE[:], ex[:], total[:].unsqueeze(2).to_broadcast([S, B, E]), ALU.mult))


def experts(k, tag, Wg_dram, Wu_dram, Wd_dram, E, F, WE, limit=None):
    nc = k.nc
    FP = min(F, P)
    NF = F // FP
    NQ = E * NCH
    EPI = 2
    PERQ = EPI * NCH
    with ExitStack() as ctx:
        sb = lambda name, shape, dt=F32: ctx.enter_context(nc.sbuf_tensor(f"{tag}_{name}", shape, dt))
        sem = lambda name: k.sem(f"{tag}_{name}")
        Wg = sb("Wg", [P, EPI, DC, F])
        Wu = sb("Wu", [P, EPI, DC, F])
        Wd = sb("Wd", [FP, EPI, NF, D])
        th = sb("th", [FP, 2, CT])
        a = sb("a", [FP, 2, CT])
        h = sb("h", [FP, 2, NF, CT])
        w_in = [sem("w_in0"), sem("w_in1")]
        gu_done, th_ready, a_ready, h_ready, d_done, x_ready = (sem(n) for n in ("gu", "th", "a", "h", "d", "x"))

        with nc.Block() as block:
            @block.sync
            def _(sp):
                def load(e, i):
                    wait(sp, d_done, val(i, 2 * PERQ, (e - 1) * 2 * NCH))
                    for W, src in ((Wg, Wg_dram), (Wu, Wu_dram), (Wd, Wd_dram)):
                        src = src[e] if i is None else src[bass.ds(i * EPI + e, 1)].rearrange("a k n -> (a k) n")
                        sp.dma_start(W[:, e % 2, :, :], src.rearrange("(c p) n -> p c n", p=W.shape[0])).then_inc(w_in[e % 2], 16)

                load(0, None)
                load(1, None)
                with nc.sync.Fori(0, E // 2 - 1) as i:
                    load(2, i)
                    load(3, i)

            @block.tensor
            def _(pe):
                def up(q, i):
                    e, c = divmod(q, NCH)
                    if c == 0:
                        pe.wait_ge(w_in[e % 2], val(i, 48, 48 * (e // 2 + 1)))
                    for f in range(NF):
                        u = q * NF + f
                        wait(pe, h_ready, val(i, PERQ * NF, u - 1))
                        for n, W in enumerate((Wg, Wu)):
                            for w in range(DC):
                                last = nc.tensor.matmul(k.psum[0:FP, 2 * (u % 2) + n, 0:CT],
                                                        W[:, e % 2, w, f * FP:(f + 1) * FP],
                                                        k.XT[:, w, c * CT:(c + 1) * CT],
                                                        start=(w == 0), stop=(w == DC - 1))
                        last.then_inc(gu_done, 1)

                def down(q, i):
                    e, c = divmod(q, NCH)
                    pe.wait_ge(h_ready, val(i, PERQ * NF, (q + 1) * NF))
                    for r in range(2):
                        wait(pe, x_ready, val(i, PERQ * 2, 2 * (q - 2) + r + 1))
                        for j in (2 * r, 2 * r + 1):
                            for f in range(NF):
                                last = nc.tensor.matmul(k.psum[0:S, 4 + 2 * (q % 2) + r, (j % 2) * D:(j % 2 + 1) * D],
                                                        h[:, q % 2, f, j * S:(j + 1) * S], Wd[:, e % 2, f, :],
                                                        start=(f == 0), stop=(f == NF - 1))
                        last.then_inc(d_done, 1)

                def step(s, i):
                    if i is not None or s < NQ:
                        up(s, i)
                    if s >= 1:
                        down(s - 1, i)

                pipeline(nc.tensor, NQ, PERQ, 1, step, peel=NCH + 1)

            @block.scalar
            def _(act):
                def step(s, i):
                    for f in range(NF):
                        u = s * NF + f
                        act.wait_ge(gu_done, val(i, PERQ * NF, u + 1))
                        nc.scalar.activation(th[:, u % 2, :], k.psum[0:FP, 2 * (u % 2), 0:CT], ACT.Tanh,
                                             scale=0.5).then_inc(th_ready, 1)

                pipeline(nc.scalar, NQ, PERQ, 0, step, peel=0)

            @block.vector
            def _(dve):
                def gate(q, i):
                    for f in range(NF):
                        u = q * NF + f
                        dve.wait_ge(th_ready, val(i, PERQ * NF, u + 1))
                        nc.vector.scalar_tensor_tensor(a[:, u % 2, :], th[:, u % 2, :], 1.0,
                                                       k.psum[0:FP, 2 * (u % 2), 0:CT], ALU.add, ALU.mult).then_inc(a_ready, 1)
                        dve.wait_ge(a_ready, val(i, PERQ * NF, u + 1))
                        wait(dve, d_done, val(i, PERQ * 2, 2 * (q - 1)))
                        up = k.psum[0:FP, 2 * (u % 2) + 1, 0:CT]
                        if limit is None:
                            last = nc.vector.tensor_tensor(h[:, q % 2, f, :], a[:, u % 2, :], up, ALU.mult)
                        else:
                            last = nc.vector.scalar_tensor_tensor(h[:, q % 2, f, :], a[:, u % 2, :], 2.0 * limit, up,
                                                                  ALU.min, ALU.mult)
                        last.then_inc(h_ready, 1)

                def add(q, i):
                    e, c = divmod(q, NCH)
                    for r in range(2):
                        dve.wait_ge(d_done, val(i, PERQ * 2, 2 * q + r + 1))
                        wait(dve, x_ready, val(i, PERQ * 2, 2 * (q - NCH) + r + 1))
                        for j in (2 * r, 2 * r + 1):
                            b = c * CH + j
                            we = WE[:, b, e:e + 1] if i is None else WE[:, b, bass.ds(i * EPI + e, 1)]
                            last = nc.vector.scalar_tensor_tensor(
                                k.X[:, b, :], k.psum[0:S, 4 + 2 * (q % 2) + r, (j % 2) * D:(j % 2 + 1) * D],
                                we, k.X[:, b, :], ALU.mult, ALU.add)
                        last.then_inc(x_ready, 1)

                def step(s, i):
                    if i is not None or s < NQ:
                        gate(s, i)
                    if s >= 1:
                        add(s - 1, i)

                pipeline(nc.vector, NQ, PERQ, 1, step, peel=NCH + 1)


def mixture(k, tag, Wr_dram, Wg_dram, Wu_dram, Wd_dram, E, K, F, limit=None):
    with k.nc.sbuf_tensor(f"{tag}_WE", [S, B, E], F32) as WE:
        layernorm_transposed(k, f"{tag}_ln")
        router(k, f"{tag}_r", Wr_dram, E, K, WE)
        experts(k, f"{tag}_e", Wg_dram, Wu_dram, Wd_dram, E, F, WE, limit)


def wide_projections(k, tag, WqT_dram, WkT_dram, WvT_dram, QT, KNT, VN):
    nc = k.nc
    with ExitStack() as ctx:
        sb = lambda name, shape, dt=F32: ctx.enter_context(nc.sbuf_tensor(f"{tag}_{name}", shape, dt))
        sem = lambda name: k.sem(f"{tag}_{name}")
        Wq, Wk, Wv = sb("Wq", [P, DC, D]), sb("Wk", [P, DC, D]), sb("Wv", [P, DC, D])
        w_in, done, read = sem("w_in"), sem("done"), sem("read")
        NQ = NCH * 2 * DC
        with nc.Block() as block:
            @block.sync
            def _(sp):
                for W, src in ((Wq, WqT_dram), (Wk, WkT_dram), (Wv, WvT_dram)):
                    sp.dma_start(W[:], src.rearrange("(c p) n -> p c n", p=P)).then_inc(w_in, 16)
                sp.wait_ge(w_in, 48)

            @block.tensor
            def _(pe):
                pe.wait_ge(w_in, 48)
                with nc.tensor.Fori(0, NCH) as c:
                    for n, (W, o) in enumerate(((Wq, 0), (Wq, 1), (Wk, 0), (Wk, 1))):
                        pe.wait_ge(read, c * 4 + n + 1)
                        for w in range(DC):
                            last = nc.tensor.matmul(k.psum[:, n, 0:CT], W[:, w, o * P:(o + 1) * P],
                                                    k.XT[:, w, bass.ds(c * CT, CT)], start=(w == 0), stop=(w == DC - 1))
                        last.then_inc(done, 1)
                for b in range(B):
                    pe.wait_ge(read, NQ + b + 1)
                    for w in range(DC):
                        last = nc.tensor.matmul(k.psum[0:S, 4 + b % 4, 0:D], k.XT[:, w, b * S:(b + 1) * S], Wv[:, w, :],
                                                start=(w == 0), stop=(w == DC - 1))
                    last.then_inc(done, 1)

            @block.scalar
            def _(act):
                act.sem_inc(read, 4)
                with nc.scalar.Fori(0, NCH) as c:
                    for n, (T, o) in enumerate(((QT, 0), (QT, 1), (KNT, 0), (KNT, 1))):
                        act.wait_ge(done, c * 4 + n + 1)
                        nc.scalar.activation(T[:, o, bass.ds(c * CT, CT)], k.psum[:, n, 0:CT], ACT.Copy).then_inc(read, 1)
                for b in range(B):
                    act.wait_ge(done, NQ + b + 1)
                    nc.scalar.activation(VN[:, b, :], k.psum[0:S, 4 + b % 4, 0:D], ACT.Copy).then_inc(read, 1)


def wide_attention(k, tag, ctxT_dram, ctx_dram, QT, mask_dram=None, new=None):
    nc = k.nc
    NEW = S if new else 0
    W = (M + NEW) // 4
    TILES = list(zip(MOFF, MSZ)) + ([(M, S)] if new else [])
    NT = len(TILES)
    TB = 5
    NB = -(-NT // TB)
    SC, TR, OUT = 0, 4, 7
    OT = 3 * S
    SCALE = D ** -0.5
    assert W * 4 == M + NEW and W <= BANK and (NT - 2 * TB) * S <= OT and OT + DC * S <= BANK
    with ExitStack() as ctx:
        sb = lambda name, shape, dt=F32: ctx.enter_context(nc.sbuf_tensor(f"{tag}_{name}", shape, dt))
        sem = lambda name: k.sem(f"{tag}_{name}")
        ctxT = sb("ctxT", [P, 2, DC, M])
        cx = sb("cx", [P, 2, MT, D])
        qb = sb("qb", [P, 2, DC, S])
        pr = sb("pr", [S, 2, M + NEW])
        pt = sb("pt", [P, NT, S])
        mx = sb("mx", [S, 2])
        nb = sb("nb", [S, 2])
        total = sb("total", [S, 2])
        rs = sb("rs", [S, 2])
        keys_in = [sem("keys_in0"), sem("keys_in1")]
        values_in = [sem("values_in0"), sem("values_in1")]
        qb_ready, s_done, mx_ready, nb_ready, p_ready, t_done, pt_ready = (sem(n) for n in ("qb", "s", "mx", "nb", "p", "t", "pt"))
        v_done, rs_ready, o_read = sem("v"), sem("rs"), sem("oread")
        if mask_dram is not None:
            keep = sb("keep", [S, B, M], U8)
            pen = sb("pen", [S, 2, M])
            sm = sb("sm", [S, M])
            valid = sb("valid", [S, 2])
            mask_in, pen_ready, sm_ready, valid_ready = sem("mask_in"), sem("pen"), sem("sm"), sem("valid")
        if new:
            KNT, VN, WoT_dram = new
            Wo = sb("Wo", [P, DC, D])
            on = sb("on", [S, 2, D])
            ont = sb("ont", [P, DC, S])
            w_in, on_ready, ot_done, ont_ready, y_done, y_read = (sem(n) for n in ("w_in", "on", "ot", "ont", "y", "yread"))

        def batch(T, i, b, rows=slice(None)):
            return T[rows, b] if i is None else T[rows, bass.ds(i * 2 + b, 1)].rearrange("p a n -> p (a n)")

        with nc.Block() as block:
            @block.sync
            def _(sp):
                if new:
                    sp.dma_start(Wo[:], WoT_dram.rearrange("(c p) n -> p c n", p=P)).then_inc(w_in, 16)
                if mask_dram is not None:
                    sp.dma_start(keep[:], mask_dram.unsqueeze(0).to_broadcast([S, B, M])).then_inc(mask_in, 16)

                def load(b, i):
                    one = lambda T: T[b] if i is None else T[bass.ds(i * 2 + b, 1)].rearrange("a r c -> (a r) c")
                    full = (MT - 2) * P
                    wait(sp, s_done, val(i, 2, b - 1))
                    sp.dma_start(ctxT[:, b % 2, :, :], one(ctxT_dram).rearrange("(c p) m -> p c m", p=P)).then_inc(keys_in[b % 2], 16)
                    wait(sp, v_done, val(i, 2, b - 1))
                    sp.dma_start(cx[:, b % 2, 0:MT - 2, :],
                                 one(ctx_dram)[0:full, :].rearrange("(t p) d -> p t d", p=P)).then_inc(values_in[b % 2], 16)
                    for t in (MT - 2, MT - 1):
                        sp.dma_start(cx[0:MSZ[t], b % 2, t, :],
                                     one(ctx_dram)[MOFF[t]:MOFF[t] + MSZ[t], :]).then_inc(values_in[b % 2], 16)

                load(0, None)
                load(1, None)
                with nc.sync.Fori(0, B // 2 - 1) as i:
                    load(2, i)
                    load(3, i)

            if mask_dram is not None:
                @block.gpsimd
                def _(pool):
                    pool.wait_ge(mask_in, 16)

                    for b in range(B):
                        wait(pool, sm_ready, b - 1)
                        nc.gpsimd.tensor_scalar(pen[:, b % 2, :], keep[:, b, :], 1.0, 1e30,
                                                ALU.subtract, ALU.mult).then_inc(pen_ready, 1)

            @block.tensor
            def _(pe):
                if new:
                    pe.wait_ge(w_in, 16)

                def scores(b, i):
                    pe.wait_ge(keys_in[b % 2], val(i, 16, 16 * (b // 2 + 1)))
                    pe.wait_ge(qb_ready, val(i, 2, b + 1))
                    wait(pe, sm_ready if mask_dram is not None else p_ready, val(i, 2, b))
                    for g in range(4):
                        old = min(W, M - g * W)
                        for w in range(DC):
                            last = nc.tensor.matmul(k.psum[0:S, SC + g, 0:old], qb[:, b % 2, w, :],
                                                    ctxT[:, b % 2, w, g * W:g * W + old], start=(w == 0), stop=(w == DC - 1))
                        if old < W:
                            for w in range(DC):
                                at = slice(b * S, (b + 1) * S) if i is None else bass.ds(i * (2 * S) + b * S, S)
                                last = nc.tensor.matmul(k.psum[0:S, SC + g, old:W], qb[:, b % 2, w, :], KNT[:, w, at],
                                                        start=(w == 0), stop=(w == DC - 1))
                    last.then_inc(s_done, 1)

                def transpose(b, i):
                    pe.wait_ge(p_ready, val(i, 2, b + 1))
                    for g in range(NB):
                        wait(pe, pt_ready, val(i, 2 * NB, NB * (b - 1) + g + 1))
                        if new and g == 2:
                            wait(pe, ont_ready, val(i, 2, b - 1))
                        for t in range(g * TB, min(NT, (g + 1) * TB)):
                            at, m = TILES[t]
                            last = nc.tensor.transpose(k.psum[0:m, TR + g, (t % TB) * S:(t % TB + 1) * S],
                                                       pr[:, b % 2, at:at + m], k.ident[0:S, 0:S])
                        last.then_inc(t_done, 1)

                def values(b, i):
                    pe.wait_ge(values_in[b % 2], val(i, 48, 48 * (b // 2 + 1)))
                    wait(pe, o_read, val(i, 2, b))
                    if new:
                        wait(pe, y_read, val(i, 2, b))
                    for t, (at, m) in enumerate(TILES):
                        if t % TB == 0:
                            pe.wait_ge(pt_ready, val(i, 2 * NB, NB * b + t // TB + 1))
                        rhs = cx[0:m, b % 2, t, :] if t < MT else batch(VN, i, b)
                        last = nc.tensor.matmul(k.psum[0:S, OUT, 0:D], pt[0:m, t, :], rhs, start=(t == 0), stop=(t == NT - 1))
                    last.then_inc(v_done, 1)

                def turn(b, i):
                    pe.wait_ge(on_ready, val(i, 2, b + 1))
                    wait(pe, ont_ready, val(i, 2, b))
                    for w in range(DC):
                        last = nc.tensor.transpose(k.psum[:, TR + 2, OT + w * S:OT + (w + 1) * S],
                                                   on[:, b % 2, w * P:(w + 1) * P], k.ident[0:S, 0:S])
                    last.then_inc(ot_done, 1)

                def project(b, i):
                    pe.wait_ge(ont_ready, val(i, 2, b + 1))
                    pe.wait_ge(o_read, val(i, 2, b + 1))
                    for w in range(DC):
                        last = nc.tensor.matmul(k.psum[0:S, OUT, 0:D], ont[:, w, :], Wo[:, w, :], start=(w == 0), stop=(w == DC - 1))
                    last.then_inc(y_done, 1)

                def step(s, i):
                    if s >= 1 and (i is not None or s - 1 < B):
                        transpose(s - 1, i)
                    if new and s >= 2:
                        turn(s - 2, i)
                    if i is not None or s < B:
                        scores(s, i)
                    if new and s >= 2:
                        project(s - 2, i)
                    if s >= 1 and (i is not None or s - 1 < B):
                        values(s - 1, i)

                pipeline(nc.tensor, B, 2, 2, step, peel=4)

            @block.scalar
            def _(act):
                def queries(b, i):
                    wait(act, s_done, val(i, 2, b - 1))
                    at = slice(b * S, (b + 1) * S) if i is None else bass.ds(i * (2 * S) + b * S, S)
                    nc.scalar.activation(qb[:, b % 2, :, :], QT[:, :, at], ACT.Copy).then_inc(qb_ready, 1)

                def exps(b, i):
                    act.wait_ge(nb_ready, val(i, 2, b + 1))
                    wait(act, t_done, val(i, 2 * NB, NB * (b - 1)))
                    wait(act, rs_ready, val(i, 2, b - 1))
                    src = sm[:].rearrange("p (g n) -> p g n", g=4) if mask_dram is not None else k.psum[0:S, SC:SC + 4, 0:W]
                    nc.scalar.activation(pr[:, b % 2, :].rearrange("p (g n) -> p g n", g=4), src, ACT.Exp,
                                         scale=SCALE, bias=nb[:, b % 2:b % 2 + 1],
                                         accum_out=total[:, b % 2:b % 2 + 1]).then_inc(p_ready, 1)

                def step(s, i):
                    if i is not None or s < B:
                        queries(s, i)
                    if s >= 1 and (i is not None or s - 1 < B):
                        exps(s - 1, i)

                pipeline(nc.scalar, B, 2, 2, step, peel=4)

            @block.vector
            def _(dve):
                def probabilities_out(b, i):
                    for g in range(NB):
                        dve.wait_ge(t_done, val(i, 2 * NB, NB * b + g + 1))
                        if g == 0:
                            wait(dve, v_done, val(i, 2, b))
                        if new and g == 2:
                            wait(dve, ot_done, val(i, 2, b))
                        for t0, n in equal_runs([m for _, m in TILES], g * TB, min(NT, (g + 1) * TB)):
                            m = TILES[t0][1]
                            src = k.psum[0:m, TR + g, (t0 % TB) * S:(t0 % TB + n) * S]
                            last = nc.vector.tensor_copy(pt[0:m, t0:t0 + n, :].rearrange("p t n -> p (t n)"), src)
                        last.then_inc(pt_ready, 1)

                def maximum(b, i):
                    dve.wait_ge(s_done, val(i, 2, b + 1))
                    m = mx[:, b % 2:b % 2 + 1]
                    wait(dve, p_ready, val(i, 2, b))
                    if mask_dram is not None:
                        dve.wait_ge(pen_ready, val(i, 2, b + 1))
                        nc.vector.tensor_tensor(sm[:].rearrange("p (g n) -> p g n", g=4), k.psum[0:S, SC:SC + 4, 0:W],
                                                pen[:, b % 2, :].rearrange("p (g n) -> p g n", g=4), ALU.add).then_inc(sm_ready, 1)
                        dve.wait_ge(sm_ready, val(i, 2, b + 1))
                        nc.vector.tensor_reduce(m, sm[:], AX.X, ALU.max).then_inc(mx_ready, 1)
                    else:
                        nc.vector.tensor_reduce(m, k.psum[0:S, SC:SC + 4, 0:W], AX.XY, ALU.max).then_inc(mx_ready, 1)
                    dve.wait_ge(mx_ready, val(i, 2, b + 1))
                    nc.vector.tensor_scalar(nb[:, b % 2:b % 2 + 1], m, -SCALE, None, ALU.mult).then_inc(nb_ready, 1)

                def outputs(b, i):
                    r = rs[:, b % 2:b % 2 + 1]
                    dve.wait_ge(p_ready, val(i, 2, b + 1))
                    if mask_dram is not None:
                        nc.vector.tensor_scalar(valid[:, b % 2:b % 2 + 1], mx[:, b % 2:b % 2 + 1], -1e29, None,
                                                ALU.is_gt).then_inc(valid_ready, 1)
                        nc.vector.reciprocal(total[:, b % 2:b % 2 + 1], total[:, b % 2:b % 2 + 1]).then_inc(valid_ready, 1)
                        dve.wait_ge(valid_ready, val(i, 4, 2 * b + 2))
                        nc.vector.tensor_tensor(r, total[:, b % 2:b % 2 + 1], valid[:, b % 2:b % 2 + 1], ALU.mult).then_inc(rs_ready, 1)
                    else:
                        nc.vector.reciprocal(r, total[:, b % 2:b % 2 + 1]).then_inc(rs_ready, 1)
                    dve.wait_ge(rs_ready, val(i, 2, b + 1))
                    dve.wait_ge(v_done, val(i, 2, b + 1))
                    if new:
                        wait(dve, ot_done, val(i, 2, b - 1))
                        nc.vector.tensor_scalar(on[:, b % 2, :], k.psum[0:S, OUT, 0:D], r, None, ALU.mult).then_inc(on_ready, 1)
                        dve.wait_ge(on_ready, val(i, 2, b + 1))
                        dve.sem_inc(o_read, 1)
                    else:
                        xb = batch(k.X, i, b)
                        nc.vector.scalar_tensor_tensor(xb, k.psum[0:S, OUT, 0:D], r, xb, ALU.mult, ALU.add).then_inc(o_read, 1)

                def turned_out(b, i):
                    dve.wait_ge(ot_done, val(i, 2, b + 1))
                    wait(dve, y_done, val(i, 2, b))
                    nc.vector.tensor_copy(ont[:].rearrange("p c n -> p (c n)"), k.psum[:, TR + 2, OT:OT + DC * S]).then_inc(ont_ready, 1)

                def add(b, i):
                    dve.wait_ge(y_done, val(i, 2, b + 1))
                    xb = batch(k.X, i, b)
                    nc.vector.tensor_tensor(xb, k.psum[0:S, OUT, 0:D], xb, ALU.add).then_inc(y_read, 1)

                def step(s, i):
                    if s >= 1 and (i is not None or s - 1 < B):
                        probabilities_out(s - 1, i)
                    if new and s >= 2:
                        turned_out(s - 2, i)
                    if i is not None or s < B:
                        maximum(s, i)
                    if new and s >= 2:
                        add(s - 2, i)
                    if s >= 1 and (i is not None or s - 1 < B):
                        outputs(s - 1, i)

                pipeline(nc.vector, B, 2, 2, step, peel=4)


H2, KV2, HD2 = 16, 4, 128
GRP = H2 // KV2
ITEMS = MT + H2 // GRP


def grouped_attention(k, ctxT_dram, Wq_dram, Wk_dram, Wv_dram, Wo_dram, qw_dram, kw_dram):
    nc = k.nc
    LT = 2
    TB = 5
    NB = -(-MT // TB)
    SC, TR, OUT, Y = 0, 3, 6, 7
    KB, TA = 0, 4
    SCALE = HD2 ** -0.5
    KVW = KV2 * HD2
    with ExitStack() as ctx:
        sb = lambda name, shape, dt=F32: ctx.enter_context(nc.sbuf_tensor(f"g2_{name}", shape, dt))
        sem = lambda name: k.sem(f"g2_{name}")
        Wq, Wk, Wv, Wo = sb("Wq", [P, DC, H2 * HD2]), sb("Wk", [P, DC, KVW]), sb("Wv", [P, DC, KVW]), sb("Wo", [P, H2, D])
        w2 = sb("w2", [P, 2])
        w = sb("w", [P, 1])
        ctxT = sb("ctxT", [P, 2, DC, M])
        xb = sb("xb", [P, DC, S])
        sq = sb("sq", [P, KVW])
        ssq = sb("ssq", [P, KV2])
        lnn = sb("lnn", [P, KV2])
        rn = sb("rn", [P, KV2])
        nn = sb("nn", [P, 2, KVW])
        KT = sb("KT", [P, KV2, M])
        V = sb("V", [P, MT, KVW])
        QT = sb("QT", [P, H2, S])
        pr = sb("pr", [S, 2, M])
        pt = sb("pt", [P, 2, MT, S])
        ot = sb("ot", [P, 2, S])
        mx, nb, total, rs = sb("mx", [S, 2]), sb("nb", [S, 2]), sb("total", [S, 2]), sb("rs", [S, 2])
        w_in, w2_in, w_ready, ctx_in = sem("w_in"), sem("w2_in"), sem("w"), [sem("ctx_in0"), sem("ctx_in1")]
        xb_ready, a_done, v_ready, sq_ready, ssq_ready, ln_ready, rn_ready, nn_ready, ta_done, ta_read = (
            sem(n) for n in ("xb", "a", "v", "sq", "ssq", "ln", "rn", "nn", "ta", "tar"))
        s_done, mx_ready, nb_ready, e_ready, rs_ready, p_ready, t_done, pt_ready, o_done, ot_ready, y_done, y_read = (
            sem(n) for n in ("s", "mx", "nb", "e", "rs", "p", "t", "pt", "o", "ot", "y", "yr"))
        rows = [MSZ[j] if j < MT else S for j in range(ITEMS)]

        def batches(eng, body):
            body(0, None)
            body(1, None)
            with eng.Fori(0, B // 2 - 1) as i:
                body(2, i)
                body(3, i)

        with nc.Block() as block:
            @block.sync
            def _(sp):
                for W, src in ((Wk, Wk_dram), (Wv, Wv_dram), (Wq, Wq_dram), (Wo, Wo_dram)):
                    sp.dma_start(W[:], src.rearrange("(c p) n -> p c n", p=P)).then_inc(w_in, 16)
                sp.dma_start(w2[:, 0:1], qw_dram.unsqueeze(1)).then_inc(w2_in, 16)
                sp.dma_start(w2[:, 1:2], kw_dram.unsqueeze(1)).then_inc(w2_in, 16)

                def load(b, i):
                    wait(sp, a_done, val(i, 2 * ITEMS, (b - 1) * ITEMS))
                    src = ctxT_dram[b] if i is None else ctxT_dram[bass.ds(i * 2 + b, 1)].rearrange("a d m -> (a d) m")
                    sp.dma_start(ctxT[:, b % 2, :, :], src.rearrange("(c p) m -> p c m", p=P)).then_inc(ctx_in[b % 2], 16)

                batches(nc.sync, load)

            @block.tensor
            def _(pe):
                pe.wait_ge(w_in, 64)

                def body(b, i):
                    item = lambda j, per=1: val(i, 2 * ITEMS * per, (b * ITEMS + j) * per)
                    unit = lambda h, per=1: val(i, 2 * H2 * per, (b * H2 + h) * per)

                    def project(j):
                        m, bank = rows[j], KB + 2 * (j % 2)
                        if j == 0:
                            pe.wait_ge(ctx_in[b % 2], val(i, 16, 16 * (b // 2 + 1)))
                            wait(pe, p_ready, unit(0))
                            wait(pe, pt_ready, unit(0, NB))
                        wait(pe, nn_ready, item(j - 1))
                        wait(pe, v_ready, val(i, 2 * MT, b * MT + min(j - 1, MT)))
                        if j < MT:
                            for n, W in enumerate((Wk, Wv)):
                                for c in range(DC):
                                    last = nc.tensor.matmul(k.psum[0:m, bank + n, :], ctxT[:, b % 2, c, MOFF[j]:MOFF[j] + m],
                                                            W[:, c, :], start=(c == 0), stop=(c == DC - 1))
                        else:
                            pe.wait_ge(xb_ready, val(i, 2, b + 1))
                            for c in range(DC):
                                last = nc.tensor.matmul(k.psum[0:m, bank, :], xb[:, c, :],
                                                        Wq[:, c, (j - MT) * KVW:(j - MT + 1) * KVW],
                                                        start=(c == 0), stop=(c == DC - 1))
                        last.then_inc(a_done, 1)

                    def turn(j):
                        m = rows[j]
                        pe.wait_ge(nn_ready, item(j + 1))
                        wait(pe, ta_read, item(j - 1))
                        for g in range(KV2):
                            last = nc.tensor.transpose(k.psum[:, TA + j % 2, g * m:(g + 1) * m],
                                                       nn[0:m, j % 2, g * HD2:(g + 1) * HD2], k.ident[0:m, 0:m])
                        last.then_inc(ta_done, 1)

                    def scores(h):
                        if h == 0:
                            pe.wait_ge(ta_read, item(ITEMS))
                            pe.wait_ge(v_ready, val(i, 2 * MT, (b + 1) * MT))
                        wait(pe, e_ready, unit(h))
                        for g in range(0, M, BANK):
                            n = min(BANK, M - g)
                            last = nc.tensor.matmul(k.psum[0:S, SC + g // BANK, 0:n], QT[:, h, :], KT[:, h // GRP, g:g + n],
                                                    start=True, stop=True)
                        last.then_inc(s_done, 1)

                    def transpose(h):
                        pe.wait_ge(p_ready, unit(h + 1))
                        for g in range(NB):
                            wait(pe, pt_ready, val(i, 2 * H2 * NB, (b * H2 + h - 1) * NB + g + 1))
                            for t in range(g * TB, min(MT, (g + 1) * TB)):
                                last = nc.tensor.transpose(k.psum[0:MSZ[t], TR + g, (t % TB) * S:(t % TB + 1) * S],
                                                           pr[:, h % 2, MOFF[t]:MOFF[t] + MSZ[t]], k.ident[0:S, 0:S])
                            last.then_inc(t_done, 1)

                    def values(h):
                        wait(pe, ot_ready, unit(h))
                        for t in range(MT):
                            if t % TB == 0:
                                pe.wait_ge(pt_ready, val(i, 2 * H2 * NB, (b * H2 + h) * NB + t // TB + 1))
                            g = h // GRP
                            last = nc.tensor.matmul(k.psum[:, OUT, 0:S], V[0:MSZ[t], t, g * HD2:(g + 1) * HD2],
                                                    pt[0:MSZ[t], h % 2, t, :], start=(t == 0), stop=(t == MT - 1))
                        last.then_inc(o_done, 1)

                    def output(h):
                        pe.wait_ge(ot_ready, unit(h + 1))
                        wait(pe, y_read, unit(h))
                        nc.tensor.matmul(k.psum[0:S, Y, 0:D], ot[:, h % 2, :], Wo[:, h, :], start=True,
                                         stop=True).then_inc(y_done, 1)

                    for s in range(ITEMS + LT):
                        if s < ITEMS:
                            project(s)
                        if s >= LT:
                            turn(s - LT)
                    for s in range(H2 + 3):
                        if s < H2:
                            scores(s)
                        if 1 <= s < H2 + 1:
                            transpose(s - 1)
                        if s >= 3:
                            output(s - 3)
                        if 2 <= s < H2 + 2:
                            values(s - 2)

                batches(nc.tensor, body)

            @block.scalar
            def _(act):
                nc.scalar.preload_act_table_set(LN_EXP)

                def body(b, i):
                    item = lambda j, per=1: val(i, 2 * ITEMS * per, (b * ITEMS + j) * per)
                    unit = lambda h, per=1: val(i, 2 * H2 * per, (b * H2 + h) * per)

                    def square(j):
                        m, bank = rows[j], KB + 2 * (j % 2)
                        act.wait_ge(a_done, item(j + 1))
                        nc.scalar.activation(sq[0:m, :], k.psum[0:m, bank, :], ACT.Square).then_inc(sq_ready, 1)
                        if j < MT:
                            nc.scalar.activation(V[0:m, j, :], k.psum[0:m, bank + 1, :], ACT.Copy).then_inc(v_ready, 1)

                    def norm(j):
                        m = rows[j]
                        act.wait_ge(ssq_ready, item(j + 1))
                        nc.scalar.activation(lnn[0:m, :], ssq[0:m, :], ACT.Ln, scale=1.0 / HD2,
                                             bias=k.eps[0:m, 1:2]).then_inc(ln_ready, 1)
                        act.wait_ge(ln_ready, item(j + 1))
                        nc.scalar.activation(rn[0:m, :], lnn[0:m, :], ACT.Exp, scale=-0.5).then_inc(rn_ready, 1)

                    def exps(h):
                        act.wait_ge(nb_ready, unit(h + 1))
                        wait(act, t_done, unit(h - 1, NB))
                        nc.scalar.activation(pr[:, h % 2, :], k.psum[0:S, SC:SC + 3, :].rearrange("p g n -> p (g n)")[:, 0:M],
                                             ACT.Exp, scale=SCALE, bias=nb[:, h % 2:h % 2 + 1],
                                             accum_out=total[:, h % 2:h % 2 + 1]).then_inc(e_ready, 1)

                    def output_out(h):
                        act.wait_ge(o_done, unit(h + 1))
                        wait(act, y_done, unit(h - 1))
                        nc.scalar.activation(ot[:, h % 2, :], k.psum[:, OUT, 0:S], ACT.Copy).then_inc(ot_ready, 1)

                    wait(act, a_done, item(0))
                    at = slice(b * S, (b + 1) * S) if i is None else bass.ds(i * (2 * S) + b * S, S)
                    nc.scalar.activation(xb[:], k.XT[:, :, at], ACT.Copy).then_inc(xb_ready, 1)
                    for j in range(ITEMS):
                        square(j)
                        norm(j)
                    for s in range(H2 + 2):
                        if s < H2:
                            exps(s)
                        if s >= 2:
                            output_out(s - 2)

                batches(nc.scalar, body)

            @block.vector
            def _(dve):
                dve.wait_ge(w2_in, 32)
                nc.vector.tensor_tensor(w[:], w2[:, 0:1], w2[:, 1:2], ALU.mult).then_inc(w_ready, 1)
                dve.wait_ge(w_ready, 1)

                def body(b, i):
                    item = lambda j, per=1: val(i, 2 * ITEMS * per, (b * ITEMS + j) * per)
                    unit = lambda h, per=1: val(i, 2 * H2 * per, (b * H2 + h) * per)

                    def squares(j):
                        m = rows[j]
                        dve.wait_ge(sq_ready, item(j + 1))
                        nc.vector.reduce_sum(ssq[0:m, :], sq[0:m, :].rearrange("p (g d) -> p g d", g=KV2), AX.X).then_inc(ssq_ready, 1)

                    def normalise(j):
                        m, bank = rows[j], KB + 2 * (j % 2)
                        dve.wait_ge(rn_ready, item(j + 1))
                        wait(dve, ta_done, item(j - 1))
                        nc.vector.tensor_tensor(nn[0:m, j % 2, :].rearrange("p (g d) -> p g d", g=KV2),
                                                k.psum[0:m, bank, :].rearrange("p (g d) -> p g d", g=KV2),
                                                rn[0:m, :].unsqueeze(2).to_broadcast([m, KV2, HD2]), ALU.mult).then_inc(nn_ready, 1)

                    def turned_out(j):
                        m = rows[j]
                        dve.wait_ge(ta_done, item(j + 1))
                        src = k.psum[:, TA + j % 2, 0:KV2 * m].rearrange("p (g m) -> p g m", g=KV2)
                        if j < MT:
                            last = nc.vector.tensor_copy(KT[:, :, MOFF[j]:MOFF[j] + m], src)
                        else:
                            q = j - MT
                            last = nc.vector.tensor_scalar(QT[:, q * GRP:(q + 1) * GRP, :], src, w[:, 0:1], None, ALU.mult)
                        last.then_inc(ta_read, 1)

                    def maximum(h):
                        dve.wait_ge(s_done, unit(h + 1))
                        m = mx[:, h % 2:h % 2 + 1]
                        nc.vector.tensor_reduce(m, k.psum[0:S, SC:SC + 3, :].rearrange("p g n -> p (g n)")[:, 0:M],
                                                AX.X, ALU.max).then_inc(mx_ready, 1)
                        dve.wait_ge(mx_ready, unit(h + 1))
                        nc.vector.tensor_scalar(nb[:, h % 2:h % 2 + 1], m, -SCALE, None, ALU.mult).then_inc(nb_ready, 1)

                    def divide(h):
                        dve.wait_ge(e_ready, unit(h + 1))
                        nc.vector.reciprocal(rs[:, h % 2:h % 2 + 1], total[:, h % 2:h % 2 + 1]).then_inc(rs_ready, 1)
                        dve.wait_ge(rs_ready, unit(h + 1))
                        nc.vector.tensor_scalar(pr[:, h % 2, :], pr[:, h % 2, :], rs[:, h % 2:h % 2 + 1], None,
                                                ALU.mult).then_inc(p_ready, 1)

                    def probabilities_out(h):
                        for g in range(NB):
                            dve.wait_ge(t_done, val(i, 2 * H2 * NB, (b * H2 + h) * NB + g + 1))
                            if g == 0:
                                wait(dve, o_done, unit(h - 1))
                            for t0, n in equal_runs(MSZ, g * TB, min(MT, (g + 1) * TB)):
                                m = MSZ[t0]
                                last = nc.vector.tensor_copy(pt[0:m, h % 2, t0:t0 + n, :].rearrange("p t n -> p (t n)"),
                                                             k.psum[0:m, TR + g, (t0 % TB) * S:(t0 % TB + n) * S])
                            last.then_inc(pt_ready, 1)

                    def add(h):
                        dve.wait_ge(y_done, unit(h + 1))
                        wait(dve, y_read, unit(h))
                        xr = k.X[:, b, :] if i is None else k.X[:, bass.ds(i * 2 + b, 1), :].rearrange("p a d -> p (a d)")
                        nc.vector.tensor_tensor(xr, k.psum[0:S, Y, 0:D], xr, ALU.add).then_inc(y_read, 1)

                    for s in range(ITEMS + LT):
                        if s < ITEMS:
                            squares(s)
                        if s >= LT:
                            turned_out(s - LT)
                        if s < ITEMS:
                            normalise(s)
                    for s in range(H2 + 3):
                        if s >= 1 and s < H2 + 1:
                            divide(s - 1)
                        if s < H2:
                            maximum(s)
                        if 1 <= s < H2 + 1:
                            probabilities_out(s - 1)
                        if s >= 3:
                            add(s - 3)

                batches(nc.vector, body)


QMAX = 127.0
ROUND = 1.5 * 2.0 ** 23


def quantise(nc, link, T, amax, scale, inv):
    p, g, n = T.shape
    wide = lambda ap: ap.unsqueeze(2).to_broadcast([p, g, n])
    link(nc.vector.tensor_reduce(amax, T, AX.X, ALU.max, apply_absolute_value=True))
    link(nc.vector.tensor_scalar(scale, amax, 0.0, None, ALU.is_equal))
    link(nc.vector.scalar_tensor_tensor(scale, amax, 1.0 / QMAX, scale, ALU.mult, ALU.add))
    link(nc.vector.reciprocal(inv, scale))
    link(nc.vector.tensor_tensor(T, T, wide(inv), ALU.mult))
    link(nc.vector.tensor_scalar(T, T, ROUND, ROUND, ALU.add, ALU.subtract))
    link(nc.vector.tensor_scalar(T, T, QMAX, -QMAX, ALU.min, ALU.max))
    link(nc.vector.tensor_tensor(T, T, wide(scale), ALU.mult))


def quantised_layer(k, KT_dram, bias_dram):
    nc = k.nc
    with ExitStack() as ctx:
        sb = lambda name, shape, dt=F32: ctx.enter_context(nc.sbuf_tensor(f"q3_{name}", shape, dt))
        sem = lambda name: k.sem(f"q3_{name}")
        KTq = sb("KTq", [P, DC, D])
        Kq = sb("Kq", [P, DC, D])
        bq = sb("bq", [S, 1, D])
        T = sb("T", [S, B, D])
        stats, mv, lnv, rstd = sb("stats", [S, B, 6]), sb("mv", [S, B, 2]), sb("lnv", [S, B]), sb("rstd", [S, B])
        amax, scale, inv = sb("amax", [P, B]), sb("scale", [P, B]), sb("inv", [P, B])
        w_in, step, mv_ready, ln_ready, rstd_ready = sem("w_in"), sem("step"), sem("mv"), sem("ln"), sem("rstd")
        kq_ready, kt_done, kq_read, t_ready, xt_done, xt_read, y_done = (
            sem(n) for n in ("kq", "ktd", "kqr", "t", "xtd", "xtr", "y"))
        with nc.Block() as block:
            @block.sync
            def _(sp):
                sp.dma_start(KTq[:], KT_dram.rearrange("(c p) n -> p c n", p=P)).then_inc(w_in, 16)
                sp.dma_start(bq[:], bias_dram.unsqueeze(0).unsqueeze(0).to_broadcast([S, 1, D])).then_inc(w_in, 16)
                sp.wait_ge(w_in, 32)

            @block.scalar
            def _(act):
                nc.scalar.preload_act_table_set(LN_EXP)
                act.wait_ge(mv_ready, B)
                nc.scalar.activation(lnv[:], mv[:, :, 1], ACT.Ln, bias=k.eps[0:S, 0:1]).then_inc(ln_ready, 1)
                act.wait_ge(ln_ready, 1)
                nc.scalar.activation(rstd[:], lnv[:], ACT.Exp, scale=-0.5).then_inc(rstd_ready, 1)
                act.wait_ge(kt_done, 1)
                nc.scalar.activation(Kq[:], k.psum[:, 0:DC, 0:D], ACT.Copy).then_inc(kq_read, 1)
                for c in range(NCH):
                    act.wait_ge(xt_done, c + 1)
                    nc.scalar.activation(k.XT[:, :, c * CT:(c + 1) * CT], k.psum[:, 2 + 2 * (c % 2):4 + 2 * (c % 2), 0:CT],
                                         ACT.Copy).then_inc(xt_read, 1)

            @block.tensor
            def _(pe):
                pe.wait_ge(kq_ready, 1)
                for o in range(DC):
                    for w in range(DC):
                        last = nc.tensor.transpose(k.psum[:, w, o * P:(o + 1) * P], KTq[:, o, w * P:(w + 1) * P], k.ident[:])
                last.then_inc(kt_done, 1)
                pe.wait_ge(t_ready, 1)
                for c in range(NCH):
                    wait(pe, xt_read, c - 1)
                    for j in range(CH):
                        for w in range(DC):
                            last = nc.tensor.transpose(k.psum[:, 2 + 2 * (c % 2) + w, j * S:(j + 1) * S],
                                                       T[:, c * CH + j, w * P:(w + 1) * P], k.ident[0:S, 0:S])
                    last.then_inc(xt_done, 1)
                pe.wait_ge(kq_read, 1)
                pe.wait_ge(xt_read, NCH)
                for b in range(B):
                    for w in range(DC):
                        last = nc.tensor.matmul(k.psum[0:S, b // 2, (b % 2) * D:(b % 2 + 1) * D],
                                                k.XT[:, w, b * S:(b + 1) * S], Kq[:, w, :], start=(w == 0), stop=(w == DC - 1))
                last.then_inc(y_done, 1)

            @block.vector
            def _(dve):
                count = [0]

                def link(ins):
                    count[0] += 1
                    ins.then_inc(step, 1)
                    dve.wait_ge(step, count[0])

                for b in range(B):
                    last = nc.vector.bn_stats(stats[:, b, :], k.X[:, b, :])
                    last.then_inc(step, 1)
                count[0] += B
                dve.wait_ge(step, count[0])
                for b in range(B):
                    nc.vector.bn_aggr(mv[:, b, :], stats[:, b, :]).then_inc(mv_ready, 1)
                dve.wait_ge(w_in, 32)
                quantise(nc, link, KTq[:], amax[:, 0:DC], scale[:, 0:DC], inv[:, 0:DC])
                dve.sem_inc(kq_ready, 1)
                quantise(nc, link, bq[:], amax[0:S, 0:1], scale[0:S, 0:1], inv[0:S, 0:1])
                dve.wait_ge(rstd_ready, 1)
                for b in range(B):
                    last = nc.vector.tensor_scalar(T[:, b, :], k.X[:, b, :], mv[:, b, 0:1], rstd[:, b:b + 1],
                                                   ALU.subtract, ALU.mult)
                    last.then_inc(step, 1)
                count[0] += B
                dve.wait_ge(step, count[0])
                quantise(nc, link, T[:], amax[0:S, :], scale[0:S, :], inv[0:S, :])
                dve.sem_inc(t_ready, 1)
                dve.wait_ge(y_done, 1)
                y = k.psum[0:S, :, 0:2 * D].rearrange("p g (two d) -> p (g two) d", two=2)[:, 0:B, :]
                link(nc.vector.tensor_tensor(T[:], y, bq[:].to_broadcast([S, B, D]), ALU.add))
                link(nc.vector.tensor_scalar(T[:], T[:], 0.0, None, ALU.max))
                quantise(nc, link, T[:], amax[0:S, :], scale[0:S, :], inv[0:S, :])
                link(nc.vector.tensor_tensor(k.X[:], k.X[:], T[:], ALU.add))


def program(nc, x, ctx, ctxT, mask, L0_WqT, L0_WkvT, L0_Wr, L0_Wg, L0_Wu, L0_Wd, L1_Wr, L1_Wg, L1_Wu, L1_Wd,
            L2_Wq, L2_Wk, L2_Wv, L2_Wo, L2_qw, L2_kw, L2_WrT, L2_w1, L2_v1, L2_w2,
            L3_WqT, L3_WkT, L3_WvT, L3_WoT, L3_kernelT, L3_bias, out):
    with ExitStack() as stack:
        k = Kernel(nc, stack)
        setup(k, x)
        layernorm_transposed(k, "ln0")
        with nc.sbuf_tensor("QT0", [P, B, G0, S], F16) as QT:
            heads32_queries(k, L0_WqT, QT)
            heads32_attention(k, ctxT, L0_WkvT, QT)
        mixture(k, "m0", L0_Wr, L0_Wg, L0_Wu, L0_Wd, 8, 2, 256, limit=7.0)
        layernorm_transposed(k, "ln1")
        wide_attention(k, "w1", ctxT, ctx, k.XT, mask_dram=mask.bitcast(U8))
        mixture(k, "m1", L1_Wr, L1_Wg, L1_Wu, L1_Wd, 8, 2, 256)
        k.recycle_semaphores()
        layernorm_transposed(k, "ln2")
        grouped_attention(k, ctxT, L2_Wq, L2_Wk, L2_Wv, L2_Wo, L2_qw, L2_kw)
        mixture(k, "m2", L2_WrT, L2_w1, L2_v1, L2_w2, 32, 8, 96)
        layernorm_transposed(k, "ln3")
        with (nc.sbuf_tensor("QT3", [P, DC, B * S], F32) as QT, nc.sbuf_tensor("KNT3", [P, DC, B * S], F32) as KNT,
              nc.sbuf_tensor("VN3", [S, B, D], F32) as VN):
            wide_projections(k, "p3", L3_WqT, L3_WkT, L3_WvT, QT, KNT, VN)
            wide_attention(k, "w3", ctxT, ctx, QT, new=(KNT, VN, L3_WoT))
        quantised_layer(k, L3_kernelT, L3_bias)
        store(k, out)


def kernel(x, ctx_2048, mask_BxS2_bk0, mask_BxSx4224_bf0, L0_xattn_Wq, L0_xattn_Wk, L0_xattn_Wv, L0_ffn_Wr, L0_ffn_Wg,
           L0_ffn_Wu, L0_ffn_Wd, L1_ffn_Wr, L1_ffn_Wg, L1_ffn_Wu, L1_ffn_Wd, L2_xattn_Wq, L2_xattn_Wk, L2_xattn_Wv,
           L2_xattn_Wo, L2_xattn_q_norm_w, L2_xattn_k_norm_w, L2_ffn_wg, L2_ffn_w1, L2_ffn_v1, L2_ffn_w2,
           L3_xattn_wq, L3_xattn_wk, L3_xattn_wv, L3_xattn_wo, L3_ffn_kernel, L3_ffn_bias):
    import numpy as np
    import concourse.bacc as bacc
    from concourse.bass_utils import run_bass_kernel_spmd

    a = {n: np.asarray(v) for n, v in locals().items() if n not in ("np", "bacc", "run_bass_kernel_spmd")}
    ins = dict(
        x=a["x"], ctx=a["ctx_2048"], ctxT=a["ctx_2048"].transpose(0, 2, 1), mask=a["mask_BxS2_bk0"].view(np.int32),
        L0_WqT=a["L0_xattn_Wq"].T, L0_WkvT=np.concatenate([a["L0_xattn_Wk"], a["L0_xattn_Wv"]]).T,
        L0_Wr=a["L0_ffn_Wr"], L0_Wg=a["L0_ffn_Wg"], L0_Wu=a["L0_ffn_Wu"], L0_Wd=a["L0_ffn_Wd"],
        L1_Wr=a["L1_ffn_Wr"], L1_Wg=a["L1_ffn_Wg"], L1_Wu=a["L1_ffn_Wu"], L1_Wd=a["L1_ffn_Wd"],
        L2_Wq=a["L2_xattn_Wq"], L2_Wk=a["L2_xattn_Wk"], L2_Wv=a["L2_xattn_Wv"], L2_Wo=a["L2_xattn_Wo"],
        L2_qw=a["L2_xattn_q_norm_w"], L2_kw=a["L2_xattn_k_norm_w"], L2_WrT=a["L2_ffn_wg"].T,
        L2_w1=a["L2_ffn_w1"], L2_v1=a["L2_ffn_v1"], L2_w2=a["L2_ffn_w2"],
        L3_WqT=a["L3_xattn_wq"].T, L3_WkT=a["L3_xattn_wk"].T, L3_WvT=a["L3_xattn_wv"].T, L3_WoT=a["L3_xattn_wo"].T,
        L3_kernelT=a["L3_ffn_kernel"].T, L3_bias=a["L3_ffn_bias"],
    )
    ins = {n: np.ascontiguousarray(v) for n, v in ins.items()}
    nc = bacc.Bacc("TRN2", target_bir_lowering=False, num_devices=1)
    aps = {n: nc.dram_tensor(f"in_{n}", v.shape, mybir.dt.from_np(v.dtype), kind="ExternalInput").ap() for n, v in ins.items()}
    out = nc.dram_tensor("out", (B, S, D), F32, kind="ExternalOutput").ap()
    program(nc, out=out, **aps)
    got = run_bass_kernel_spmd(nc, [{f"in_{n}": v for n, v in ins.items()}], core_ids=[0])
    return got.results[0]["out"]
```

```python
from contextlib import ExitStack

import concourse.bass as bass
from concourse import mybir

F32 = mybir.dt.float32
F16 = mybir.dt.float16
U8 = mybir.dt.uint8
U32 = mybir.dt.uint32
ALU = mybir.AluOpType
ACT = mybir.ActivationFunctionType
AX = mybir.AxisListType

B = 16
S = 100
D = 256
M = 1444
P = 128
DC = D // P
MT = -(-M // P)
LAST = M - P * (MT - 2)
MSZ = [P] * (MT - 2) + [(LAST // 2 + 3) // 4 * 4, LAST - (LAST // 2 + 3) // 4 * 4]
MOFF = [sum(MSZ[:t]) for t in range(MT)]
BANK = 512
CH = 4
NCH = B // CH
CT = CH * S
LN_EPS = 1e-5
LN_EXP = "natural_log_exp_and_others"
RMS_EPS = 1e-6


def val(i, step, const):
    return const if i is None else i * step + const


def equal_runs(sizes, start, end):
    runs = []
    for t in range(start, end):
        if runs and sizes[runs[-1][0]] == sizes[t]:
            runs[-1][1] += 1
        else:
            runs.append([t, 1])
    return runs


def wait(eng, sem, value):
    if isinstance(value, int) and value <= 0:
        return
    eng.wait_ge(sem, value)


def pipeline(eng, items, period, lag, step, peel):
    rounds = (items - peel) // period
    for s in range(peel):
        step(s, None)
    with eng.Fori(0, rounds) as i:
        for s in range(peel, peel + period):
            step(s, i)
    for s in range(peel + rounds * period, items + lag):
        step(s, None)


class Kernel:

    def __init__(self, nc, ctx):
        self.nc, self.ctx, self.sems = nc, ctx, []
        self.X = self.sb("X", [S, B, D])
        self.XT = self.sb("XT", [P, DC, B * S])
        self.ident = self.sb("ident", [P, P])
        self.ident16 = self.sb("ident16", [P, P], F16)
        self.eps = self.sb("eps", [P, 2])
        self.ctx_max = self.sb("ctx_max", [P, B, 2 * DC])
        self.psum = ctx.enter_context(nc.psum_tensor("psum", [P, 8, BANK], F32))

    def sb(self, name, shape, dt=F32):
        return self.ctx.enter_context(self.nc.sbuf_tensor(name, shape, dt))

    def sem(self, name):
        self.sems.append(self.nc.alloc_semaphore(name=name))
        return self.sems[-1]

    def recycle_semaphores(self):
        for s in self.sems:
            self.nc.sync.sem_clear(s)
            self.nc.release_semaphore(s)
        self.sems = []
        self.nc.all_engine_barrier()


def setup(k, x_dram):
    nc = k.nc
    x_in, made, id0 = k.sem("x_in"), k.sem("made"), k.sem("id0")
    with nc.Block() as block:
        @block.sync
        def _(sp):
            sp.dma_start(k.X[:], x_dram.rearrange("b s d -> s b d")).then_inc(x_in, 16)
            sp.wait_ge(x_in, 16)

        @block.gpsimd
        def _(pool):
            nc.gpsimd.memset(k.ident[:], 0.0).then_inc(id0, 1)
            pool.wait_ge(id0, 1)
            nc.gpsimd.affine_select(out=k.ident[:], in_=k.ident[:], compare_op=ALU.not_equal, fill=1.0,
                                    base=0, pattern=[[-1, P]], channel_multiplier=1).then_inc(made, 1)

        @block.vector
        def _(dve):
            nc.vector.memset(k.eps[:, 0:1], LN_EPS)
            nc.vector.memset(k.eps[:, 1:2], RMS_EPS)
            dve.wait_ge(made, 1)
            nc.vector.tensor_copy(k.ident16[:], k.ident[:]).then_inc(made, 1)


def layernorm_transposed(k, tag):
    nc = k.nc
    with ExitStack() as ctx:
        k2 = lambda name, shape, dt=F32: ctx.enter_context(nc.sbuf_tensor(f"{tag}_{name}", shape, dt))
        stats = k2("stats", [S, B, 6])
        mv = k2("mv", [S, B, 2])
        lnv = k2("lnv", [S, B])
        rstd = k2("rstd", [S, B])
        xn = k2("xn", [S, CH, D])
        sem = lambda name: k.sem(f"{tag}_{name}")
        stats_ready, mv_ready, lnv_ready, rstd_ready = sem("stats"), sem("mvr"), sem("lnvr"), sem("rstdr")
        xn_ready, xt_done, xt_read = sem("xnr"), sem("xtd"), sem("xtr")
        with nc.Block() as block:
            @block.vector
            def _(dve):
                with nc.vector.Fori(0, B) as b:
                    nc.vector.bn_stats(stats[:, bass.ds(b, 1), :], k.X[:, bass.ds(b, 1), :]).then_inc(stats_ready, 1)
                for b in range(B):
                    dve.wait_ge(stats_ready, b + 1)
                    nc.vector.bn_aggr(mv[:, b, :], stats[:, b, :]).then_inc(mv_ready, 1)
                dve.wait_ge(rstd_ready, 1)
                with nc.vector.Fori(0, NCH) as c:
                    dve.wait_ge(xt_done, c + 1)
                    for j in range(CH):
                        nc.vector.tensor_scalar(xn[:, j, :], k.X[:, bass.ds(c * CH + j, 1), :].rearrange("p a d -> p (a d)"),
                                                mv[:, bass.ds(c * CH + j, 1), 0], rstd[:, bass.ds(c * CH + j, 1)],
                                                ALU.subtract, ALU.mult).then_inc(xn_ready, 1)

            @block.scalar
            def _(act):
                nc.scalar.preload_act_table_set(LN_EXP)
                act.sem_inc(xt_read, 1)
                act.wait_ge(mv_ready, B)
                nc.scalar.activation(lnv[:], mv[:, :, 1], ACT.Ln, bias=k.eps[0:S, 0:1]).then_inc(lnv_ready, 1)
                act.wait_ge(lnv_ready, 1)
                nc.scalar.activation(rstd[:], lnv[:], ACT.Exp, scale=-0.5).then_inc(rstd_ready, 1)
                with nc.scalar.Fori(0, NCH) as c:
                    act.wait_ge(xt_done, c + 2)
                    for w in range(DC):
                        last = nc.scalar.activation(k.XT[:, w, bass.ds(c * CT, CT)], k.psum[:, w, 0:CT], ACT.Copy)
                    last.then_inc(xt_read, 1)

            @block.tensor
            def _(pe):
                pe.sem_inc(xt_done, 1)
                with nc.tensor.Fori(0, NCH) as c:
                    pe.wait_ge(xt_read, c + 1)
                    for j in range(CH):
                        pe.wait_ge(xn_ready, c * CH + j + 1)
                        for w in range(DC):
                            last = nc.tensor.transpose(k.psum[:, w, j * S:(j + 1) * S], xn[:, j, w * P:(w + 1) * P],
                                                       k.ident[0:S, 0:S])
                    last.then_inc(xt_done, 1)


def store(k, out_dram):
    nc = k.nc
    stored = k.sem("stored")
    with nc.Block() as block:
        @block.sync
        def _(sp):
            sp.dma_start(out_dram.rearrange("b s d -> s b d"), k.X[:]).then_inc(stored, 16)
            sp.wait_ge(stored, 16)


H0, HD0 = 32, 8
G0 = H0 // 4
SPLIT = 4
PERIOD = 2 * MT


def heads32_queries(k, WqT_dram, QT):
    nc = k.nc
    with ExitStack() as ctx:
        sb = lambda name, shape, dt=F32: ctx.enter_context(nc.sbuf_tensor(f"q0_{name}", shape, dt))
        sem = lambda name: k.sem(f"q0_{name}")
        Wq = sb("Wq", [P, DC, D])
        xb = sb("xb", [P, 2, DC, S])
        sq = sb("sq", [S, 2, D])
        ssq = sb("ssq", [S, 2, H0])
        lnq = sb("lnq", [S, 2, H0])
        rq = sb("rq", [S, 2, H0])
        qn = sb("qn", [S, 2, H0, HD0])
        qs = sb("qs", [S, 2, H0, SPLIT, HD0], F16)
        w_in, xb_ready, q_done, sq_ready, ssq_ready = sem("w_in"), sem("xb"), sem("q"), sem("sq"), sem("ssq")
        ln_ready, rq_ready, qn_ready, qh_ready, qs_ready = sem("ln"), sem("rq"), sem("qn"), sem("qh"), sem("qs")
        qt_done, qt_read = sem("qt"), sem("qtr")
        psum16 = k.psum[:, 2:4, :].bitcast(F16)
        with nc.Block() as block:
            @block.sync
            def _(sp):
                sp.dma_start(Wq[:], WqT_dram.rearrange("(c p) n -> p c n", p=P)).then_inc(w_in, 16)
                sp.wait_ge(w_in, 16)

            @block.tensor
            def _(pe):
                pe.wait_ge(w_in, 16)
                with nc.tensor.Fori(0, B // 2) as i:
                    for j in range(2):
                        pe.wait_ge(xb_ready, i * 2 + j + 1)
                        for w in range(DC):
                            last = nc.tensor.matmul(k.psum[0:S, j, 0:D], xb[:, j, w, :], Wq[:, w, :],
                                                    start=(w == 0), stop=(w == DC - 1))
                        last.then_inc(q_done, 1)
                    for j in range(2):
                        pe.wait_ge(qs_ready, i * 2 + j + 1)
                        flat = qs[:, j, :, :, :].rearrange("p h s d -> p (h s d)")
                        for g in range(G0):
                            last = nc.tensor.transpose(psum16[:, j, g * P:g * P + S], flat[:, g * P:(g + 1) * P],
                                                       k.ident16[0:S, 0:S])
                        last.then_inc(qt_done, 1)

            @block.scalar
            def _(act):
                nc.scalar.preload_act_table_set(LN_EXP)
                with nc.scalar.Fori(0, B // 2) as i:
                    act.wait_ge(qt_read, i * 2 + 1)
                    for j in range(2):
                        nc.scalar.activation(xb[:, j, :, :], k.XT[:, :, bass.ds(i * (2 * S) + j * S, S)],
                                             ACT.Copy).then_inc(xb_ready, 1)
                    for j in range(2):
                        act.wait_ge(q_done, i * 2 + j + 1)
                        nc.scalar.activation(sq[:, j, :], k.psum[0:S, j, 0:D], ACT.Square).then_inc(sq_ready, 1)
                    for j in range(2):
                        act.wait_ge(ssq_ready, i * 2 + j + 1)
                        nc.scalar.activation(lnq[:, j, :], ssq[:, j, :], ACT.Ln, scale=1.0 / HD0,
                                             bias=k.eps[0:S, 1:2]).then_inc(ln_ready, 1)
                        act.wait_ge(ln_ready, i * 2 + j + 1)
                        nc.scalar.activation(rq[:, j, :], lnq[:, j, :], ACT.Exp, scale=-0.5).then_inc(rq_ready, 1)

            @block.vector
            def _(dve):
                dve.sem_inc(qt_read, 1)
                with nc.vector.Fori(0, B // 2) as i:
                    for j in range(2):
                        dve.wait_ge(sq_ready, i * 2 + j + 1)
                        nc.vector.reduce_sum(ssq[:, j, :], sq[:, j, :].rearrange("p (h d) -> p h d", d=HD0),
                                             AX.X).then_inc(ssq_ready, 1)
                    for j in range(2):
                        dve.wait_ge(rq_ready, i * 2 + j + 1)
                        q = k.psum[0:S, j, 0:D].rearrange("p (h d) -> p h d", d=HD0)
                        nc.vector.tensor_tensor(qn[:, j, :, :], q, rq[:, j, :].unsqueeze(2).to_broadcast([S, H0, HD0]),
                                                ALU.mult).then_inc(qn_ready, 1)
                        dve.wait_ge(qn_ready, i * 2 + j + 1)
                        wide = qn[:, j, :, :].unsqueeze(2).to_broadcast([S, H0, 2, HD0])
                        nc.vector.tensor_scalar(qs[:, j, :, 0:2, :], wide, HD0 ** -0.5, None, ALU.mult).then_inc(qh_ready, 1)
                        dve.wait_ge(qh_ready, i * 2 + j + 1)
                        for part in range(2):
                            last = nc.vector.scalar_tensor_tensor(
                                qs[:, j, :, 2 + part, :], qn[:, j, :, :], HD0 ** -0.5, qs[:, j, :, part, :],
                                ALU.mult, ALU.subtract)
                        last.then_inc(qs_ready, 1)
                    for j in range(2):
                        dve.wait_ge(qt_done, i * 2 + j + 1)
                        src = psum16[:, j, :].rearrange("p (g n) -> p g n", g=G0)[:, :, 0:S]
                        nc.vector.tensor_copy(QT[:, bass.ds(i * 2 + j, 1), :, :].rearrange("p a g n -> p (a g) n"),
                                              src).then_inc(qt_read, 1)


def heads32_attention(k, ctxT_dram, WkvT_dram, QT):
    nc = k.nc
    NT = B * MT
    LT, LS, LV, LO = 2, 3, 4, 5
    VS = 6
    with ExitStack() as ctx:
        sb = lambda name, shape, dt=F32: ctx.enter_context(nc.sbuf_tensor(f"a0_{name}", shape, dt))
        sem = lambda name: k.sem(f"a0_{name}")
        Wkv = sb("Wkv", [P, DC, 2 * D])
        ctxT = sb("ctxT", [P, 2, DC, M])
        ksq = sb("ksq", [P, D])
        ssq = sb("ssq", [P, H0])
        lnk = sb("lnk", [P, H0])
        rk = sb("rk", [P, H0])
        kn = sb("kn", [P, H0, HD0])
        ks = sb("ks", [P, 2, H0, SPLIT, HD0], F16)
        kt = sb("kt", [P, 2, G0, P], F16)
        qbd = sb("qbd", [P, 2, G0, 4, S], F16)
        vs = sb("vs", [P, VS, H0, 32])
        pr = sb("pr", [P, 2, 4, 2, 4 * S])
        ot = sb("ot", [P, 2, 4 * S])
        rs = sb("rs", [S, 2, H0 // 2])
        on = sb("on", [S, 2, H0 // 2, HD0])
        w_in, ctx_in = sem("w_in"), [sem("ctx_in0"), sem("ctx_in1")]
        kv_done, v_ready, sq_ready, ssq_ready, ln_ready, rk_ready = (sem(n) for n in ("kv", "v", "sq", "ssq", "ln", "rk"))
        kn_ready, kh_ready, ks_ready, kt_done, kt_ready = (sem(n) for n in ("kn", "kh", "ks", "ktd", "ktr"))
        qbd_clear, qbd_ready, s_done, exp_done, pv_done = (sem(n) for n in ("qclr", "qbd", "s", "exp", "pv"))
        ot_ready, o_done, o_read, rs_ready, on_ready, x_ready = (sem(n) for n in ("ot", "o", "oread", "rs", "on", "x"))
        vs_clear = sem("vsclr")
        KV, KT, SC, PV = 0, 1, 2, 6
        ktp = k.psum[:, KT, :].bitcast(F16)

        with nc.Block() as block:
            @block.sync
            def _(sp):
                sp.dma_start(Wkv[:], WkvT_dram.rearrange("(c p) n -> p c n", p=P)).then_inc(w_in, 16)

                def load(j, i):
                    wait(sp, kn_ready, val(i, PERIOD, (j - 1) * MT))
                    src = ctxT_dram[j] if i is None else ctxT_dram[bass.ds(i * 2 + j, 1)].rearrange("a d m -> (a d) m")
                    sp.dma_start(ctxT[:, j % 2, :, :], src.rearrange("(c p) m -> p c m", p=P)).then_inc(ctx_in[j % 2], 16)

                load(0, None)
                load(1, None)
                with nc.sync.Fori(0, B // 2 - 1) as i:
                    load(2, i)
                    load(3, i)

            @block.gpsimd
            def _(pool):
                nc.gpsimd.memset(qbd[:], 0.0).then_inc(qbd_clear, 1)
                pool.wait_ge(qbd_clear, 1)

                def spread(j, i):
                    wait(pool, s_done, val(i, PERIOD * 4, (j - 1) * MT * 4))
                    for h in range(4):
                        rows = slice(32 * h, 32 * h + 32)
                        src = QT[rows, j] if i is None else QT[rows, bass.ds(i * 2 + j, 1)].rearrange("p a g n -> p (a g) n")
                        last = nc.gpsimd.tensor_copy(qbd[rows, j % 2, :, h, :], src)
                    last.then_inc(qbd_ready, 1)

                spread(0, None)
                spread(1, None)
                with nc.gpsimd.Fori(0, B // 2 - 1) as i:
                    spread(2, i)
                    spread(3, i)

            @block.tensor
            def _(pe):
                pe.wait_ge(w_in, 16)
                pe.wait_ge(vs_clear, 2)

                def project(n, i):
                    b, t = divmod(n, MT)
                    if t == 0:
                        pe.wait_ge(ctx_in[b % 2], val(i, 16, 16 * (b // 2 + 1)))
                    wait(pe, kn_ready, val(i, PERIOD, n))
                    wait(pe, v_ready, val(i, PERIOD, n))
                    for w in range(DC):
                        last = nc.tensor.matmul(k.psum[0:MSZ[t], KV, :], ctxT[:, b % 2, w, MOFF[t]:MOFF[t] + MSZ[t]],
                                                Wkv[:, w, :], start=(w == 0), stop=(w == DC - 1))
                    last.then_inc(kv_done, 1)

                def transpose(n, i):
                    t = n % MT
                    pe.wait_ge(ks_ready, val(i, PERIOD, n + 1))
                    wait(pe, kt_ready, val(i, PERIOD, n))
                    flat = ks[:, n % 2, :, :, :].rearrange("p h s d -> p (h s d)")
                    for g in range(G0):
                        last = nc.tensor.transpose(ktp[:, g * P:g * P + MSZ[t]], flat[0:MSZ[t], g * P:(g + 1) * P],
                                                   k.ident16[0:MSZ[t], 0:MSZ[t]])
                    last.then_inc(kt_done, 1)

                def scores(n, r, i):
                    b, t = divmod(n, MT)
                    if r == 0:
                        pe.wait_ge(kt_ready, val(i, PERIOD, n + 1))
                        if t == 0:
                            pe.wait_ge(qbd_ready, val(i, 2, b + 1))
                    if t == 1 and r < 2 and (b > 0 or i is not None):
                        pe.wait_ge(o_read, val(i, 4, 2 * (b - 1) + r + 1))
                    wait(pe, exp_done, val(i, PERIOD * 4, 4 * n + r - 1))
                    for g in (2 * r, 2 * r + 1):
                        last = nc.tensor.matmul(k.psum[0:MSZ[t], SC + 2 * (r % 2) + g % 2, 0:4 * S],
                                                kt[:, n % 2, g, 0:MSZ[t]],
                                                qbd[:, b % 2, g, :, :].rearrange("p h n -> p (h n)"),
                                                start=True, stop=True)
                    last.then_inc(s_done, 1)

                def values(n, r, i):
                    b, t = divmod(n, MT)
                    if r == 0:
                        pe.wait_ge(v_ready, val(i, PERIOD, n + 1))
                        if t == 0:
                            wait(pe, ot_ready, val(i, 4, 2 * b))
                    pe.wait_ge(exp_done, val(i, PERIOD * 4, 4 * n + r + 1))
                    for g in (2 * r, 2 * r + 1):
                        for h in range(4):
                            last = nc.tensor.matmul(
                                k.psum[32 * h:32 * h + 32, PV + g // 4, (g % 4) * S:(g % 4 + 1) * S],
                                vs[0:MSZ[t], n % VS, 4 * g + h, :], pr[0:MSZ[t], n % 2, r, g % 2, h * S:(h + 1) * S],
                                start=(t == 0 and g % 4 == 0), stop=(t == MT - 1), skip_group_check=True)
                    if r == 3:
                        last.then_inc(pv_done, 1)

                def outputs(n, i):
                    b = n // MT
                    for r in range(2):
                        pe.wait_ge(ot_ready, val(i, 4, 2 * b + r + 1))
                        pe.wait_ge(exp_done, val(i, PERIOD * 4, 4 * (min(n + 1, NT - 1 if i is None else n + 1)) + 3 + r))
                        for g in range(4):
                            last = nc.tensor.transpose(k.psum[0:S, SC + 2 * r, g * P:(g + 1) * P],
                                                       ot[:, r, g * S:(g + 1) * S], k.ident[:])
                        last.then_inc(o_done, 1)

                def step(s, i):
                    if s - LO >= 0 and (s - LO) % MT == MT - 1:
                        outputs(s - LO, i)
                    for r in range(4):
                        if s >= LS and (i is not None or s - LS < NT):
                            scores(s - LS, r, i)
                        if r == 0 and (i is not None or s < NT):
                            project(s, i)
                        if r == 1 and s >= LT and (i is not None or s - LT < NT):
                            transpose(s - LT, i)
                        if s >= LV and (i is not None or s - LV < NT):
                            values(s - LV, r, i)

                pipeline(nc.tensor, NT, PERIOD, LO, step, peel=MT + LO + 1)

            @block.scalar
            def _(act):
                nc.scalar.preload_act_table_set(LN_EXP)
                act.wait_ge(vs_clear, 2)

                def keys_values(n, i):
                    t = n % MT
                    m = MSZ[t]
                    act.wait_ge(kv_done, val(i, PERIOD, n + 1))
                    kv = k.psum[0:m, KV, :].rearrange("p (h d two) -> p two h d", h=H0, two=2)
                    nc.scalar.activation(ksq[0:m, :].rearrange("p (h d) -> p h d", h=H0), kv[:, 0], ACT.Square).then_inc(sq_ready, 1)
                    wait(act, pv_done, val(i, PERIOD, n - VS + 1))
                    nc.scalar.activation(vs[0:m, n % VS, :, 0:HD0], kv[:, 1], ACT.Copy).then_inc(v_ready, 1)

                def norm(n, i):
                    m = MSZ[n % MT]
                    act.wait_ge(ssq_ready, val(i, PERIOD, n + 1))
                    nc.scalar.activation(lnk[0:m, :], ssq[0:m, :], ACT.Ln, scale=1.0 / HD0,
                                         bias=k.eps[0:m, 1:2]).then_inc(ln_ready, 1)
                    act.wait_ge(ln_ready, val(i, PERIOD, n + 1))
                    nc.scalar.activation(rk[0:m, :], lnk[0:m, :], ACT.Exp, scale=-0.5).then_inc(rk_ready, 1)

                def exps(n, r, i):
                    m = MSZ[n % MT]
                    if r == 0:
                        wait(act, pv_done, val(i, PERIOD, n - 1))
                    act.wait_ge(s_done, val(i, PERIOD * 4, 4 * n + r + 1))
                    bank = SC + 2 * (r % 2)
                    nc.scalar.activation(pr[0:m, n % 2, r, :, :], k.psum[0:m, bank:bank + 2, 0:4 * S],
                                         ACT.Exp).then_inc(exp_done, 1)

                def step(s, i):
                    live = s >= LS and (i is not None or s - LS < NT)
                    for r in range(4):
                        if live:
                            exps(s - LS, r, i)
                        if r == 0 and (i is not None or s < NT):
                            keys_values(s, i)
                        if r == 1 and (i is not None or s < NT):
                            norm(s, i)

                pipeline(nc.scalar, NT, PERIOD, LO, step, peel=MT + LO + 1)

            @block.vector
            def _(dve):
                nc.vector.memset(vs[:], 0.0).then_inc(vs_clear, 1)
                dve.wait_ge(vs_clear, 1)
                nc.vector.memset(vs[:, :, :, HD0:HD0 + 1], 1.0).then_inc(vs_clear, 1)

                def keys(n, i):
                    t = n % MT
                    m = MSZ[t]
                    dve.wait_ge(sq_ready, val(i, PERIOD, n + 1))
                    nc.vector.reduce_sum(ssq[0:m, :], ksq[0:m, :].rearrange("p (h d) -> p h d", d=HD0),
                                         AX.X).then_inc(ssq_ready, 1)

                def split(n, i):
                    m = MSZ[n % MT]
                    dve.wait_ge(rk_ready, val(i, PERIOD, n + 1))
                    keys = k.psum[0:m, KV, :].rearrange("p (h d two) -> p two h d", h=H0, two=2)[:, 0]
                    nc.vector.tensor_tensor(kn[0:m], keys, rk[0:m, :].unsqueeze(2).to_broadcast([m, H0, HD0]),
                                            ALU.mult).then_inc(kn_ready, 1)
                    dve.wait_ge(kn_ready, val(i, PERIOD, n + 1))
                    wait(dve, kt_done, val(i, PERIOD, n - 1))
                    for part in range(2):
                        last = nc.vector.tensor_copy(ks[0:m, n % 2, :, 2 * part, :], kn[0:m])
                    last.then_inc(kh_ready, 1)
                    dve.wait_ge(kh_ready, val(i, PERIOD, n + 1))
                    for part in range(2):
                        last = nc.vector.tensor_tensor(ks[0:m, n % 2, :, 2 * part + 1, :], kn[0:m],
                                                       ks[0:m, n % 2, :, 2 * part, :], ALU.subtract)
                    last.then_inc(ks_ready, 1)

                def keys_out(n, i):
                    m = MSZ[n % MT]
                    dve.wait_ge(kt_done, val(i, PERIOD, n + 1))
                    wait(dve, s_done, val(i, PERIOD * 4, 4 * (n - 1)))
                    nc.vector.tensor_copy(kt[:, n % 2, :, 0:m], ktp.rearrange("p (g m) -> p g m", g=G0)[:, :, 0:m]).then_inc(kt_ready, 1)

                def outputs_out(n, i):
                    b = n // MT
                    dve.wait_ge(pv_done, val(i, PERIOD, n + 1))
                    for r in range(2):
                        wait(dve, o_done, val(i, 4, 2 * b))
                        nc.vector.tensor_copy(ot[:, r, :], k.psum[:, PV + r, 0:4 * S]).then_inc(ot_ready, 1)

                def largest(n, i):
                    b, t = divmod(n, MT)
                    piece = t // 2 - 1
                    c, half = divmod(piece, 2)
                    to = k.ctx_max[:, b, piece:piece + 1] if i is None else \
                        k.ctx_max[:, bass.ds(i * 2 + b, 1), piece:piece + 1].rearrange("p a n -> p (a n)")
                    nc.vector.tensor_reduce(to, ctxT[:, b % 2, c, half * M // 2:(half + 1) * M // 2], AX.X, ALU.max,
                                            apply_absolute_value=True)

                def add(n, i):
                    b = n // MT
                    for r in range(2):
                        dve.wait_ge(o_done, val(i, 4, 2 * b + r + 1))
                        o = k.psum[0:S, SC + 2 * r, :].rearrange("p (h e) -> p h e", e=32)
                        nc.vector.reciprocal(rs[:, r, :], o[:, :, HD0]).then_inc(rs_ready, 1)
                        dve.wait_ge(rs_ready, val(i, 4, 2 * b + r + 1))
                        nc.vector.tensor_tensor(on[:, r, :, :], o[:, :, 0:HD0],
                                                rs[:, r, :].unsqueeze(2).to_broadcast([S, H0 // 2, HD0]),
                                                ALU.mult).then_inc(o_read, 1)
                        dve.wait_ge(o_read, val(i, 4, 2 * b + r + 1))
                        half = slice(r * D // 2, (r + 1) * D // 2)
                        xb = k.X[:, b, half] if i is None else k.X[:, bass.ds(i * 2 + b, 1), half].rearrange("p a d -> p (a d)")
                        nc.vector.tensor_tensor(xb, xb, on[:, r, :, :].rearrange("p h d -> p (h d)"), ALU.add).then_inc(x_ready, 1)

                def step(s, i):
                    if s - LO >= 0 and (s - LO) % MT == MT - 1:
                        add(s - LO, i)
                    if i is not None or s < NT:
                        keys(s, i)
                    if s >= LT and (i is not None or s - LT < NT):
                        keys_out(s - LT, i)
                    if i is not None or s < NT:
                        split(s, i)
                    if s >= LV and (s - LV) % MT == MT - 1:
                        outputs_out(s - LV, i)
                    if s % MT in range(2, 2 + 4 * DC, 2) and (i is not None or s < NT):
                        largest(s, i)

                pipeline(nc.vector, NT, PERIOD, LO, step, peel=MT + LO + 1)


def router(k, tag, Wr_dram, E, K, WE):
    nc = k.nc
    with ExitStack() as ctx:
        sb = lambda name, shape, dt=F32: ctx.enter_context(nc.sbuf_tensor(f"{tag}_{name}", shape, dt))
        sem = lambda name: k.sem(f"{tag}_{name}")
        Wr = sb("Wr", [P, DC, E])
        logit = sb("logit", [S, B, E])
        top = sb("top", [S, B, 8])
        left = sb("left", [S, B, E])
        arg = sb("arg", [S, B, 8], U32)
        argf = sb("argf", [S, B, 8])
        shift = sb("shift", [S, B, E])
        ex = sb("ex", [S, B, E])
        total = sb("total", [S, B])
        w_in, l_done, step, ex_ready = sem("w_in"), sem("l"), sem("step"), sem("ex")
        bank = 0
        wide = lambda ap: ap.to_broadcast([S, B, E])

        with nc.Block() as block:
            @block.sync
            def _(sp):
                sp.dma_start(Wr[:], Wr_dram.rearrange("(c p) n -> p c n", p=P)).then_inc(w_in, 16)
                sp.wait_ge(w_in, 16)

            @block.tensor
            def _(pe):
                pe.wait_ge(w_in, 16)
                for b in range(B):
                    for w in range(DC):
                        last = nc.tensor.matmul(k.psum[0:S, bank, b * E:(b + 1) * E], k.XT[:, w, b * S:(b + 1) * S],
                                                Wr[:, w, :], start=(w == 0), stop=(w == DC - 1))
                last.then_inc(l_done, 1)

            @block.scalar
            def _(act):
                act.wait_ge(step, 1 + 2 * B if K == 8 else 1 + B)
                act.wait_ge(ex_ready, 1)
                nc.scalar.activation(ex[:], shift[:], ACT.Exp).then_inc(ex_ready, 1)

            @block.vector
            def _(dve):
                count = [0]

                def link(ins):
                    count[0] += 1
                    ins.then_inc(step, 1)
                    dve.wait_ge(step, count[0])

                dve.wait_ge(l_done, 1)
                link(nc.vector.tensor_copy(logit[:], k.psum[0:S, bank, 0:B * E].rearrange("p (b e) -> p b e", b=B)))
                for b in range(B):
                    last = nc.vector.max(top[:, b, :], logit[:, b, :])
                    last.then_inc(step, 1)
                count[0] += B
                dve.wait_ge(step, count[0])
                for b in range(B):
                    if K == 8:
                        last = nc.vector.match_replace(out=left[:, b, :], in_to_replace=top[:, b, :],
                                                       in_values=logit[:, b, :], imm_value=-3.0e38)
                    else:
                        last = nc.vector.max_index(arg[:, b, :], top[:, b, :], logit[:, b, :])
                    last.then_inc(step, 1)
                count[0] += B
                dve.wait_ge(step, count[0])
                if K == 8:
                    link(nc.vector.tensor_tensor(left[:], left[:], logit[:], ALU.not_equal))
                else:
                    link(nc.vector.tensor_copy(argf[:], arg[:]))
                    for e in range(E):
                        last = nc.vector.memset(shift[:, :, e:e + 1], float(e))
                    link(last)
                    link(nc.vector.tensor_tensor(left[:], shift[:], wide(argf[:, :, 0:1]), ALU.is_equal))
                    link(nc.vector.tensor_tensor(ex[:], shift[:], wide(argf[:, :, 1:2]), ALU.is_equal))
                    link(nc.vector.tensor_tensor(left[:], left[:], ex[:], ALU.add))
                nc.vector.tensor_tensor(shift[:], logit[:], wide(top[:, :, 0:1]), ALU.subtract).then_inc(ex_ready, 1)
                dve.wait_ge(ex_ready, 2)
                link(nc.vector.tensor_tensor(ex[:], ex[:], left[:], ALU.mult))
                link(nc.vector.reduce_sum(total[:], ex[:], AX.X))
                link(nc.vector.reciprocal(total[:], total[:]))
                link(nc.vector.tensor_scalar(total[:], total[:], 0.5, None, ALU.mult))
                link(nc.vector.tensor_tensor(WE[:], ex[:], total[:].unsqueeze(2).to_broadcast([S, B, E]), ALU.mult))


def experts(k, tag, Wg_dram, Wu_dram, Wd_dram, E, F, WE, limit=None):
    nc = k.nc
    FP = min(F, P)
    NF = F // FP
    NQ = E * NCH
    EPI = 2
    PERQ = EPI * NCH
    with ExitStack() as ctx:
        sb = lambda name, shape, dt=F32: ctx.enter_context(nc.sbuf_tensor(f"{tag}_{name}", shape, dt))
        sem = lambda name: k.sem(f"{tag}_{name}")
        Wg = sb("Wg", [P, EPI, DC, F])
        Wu = sb("Wu", [P, EPI, DC, F])
        Wd = sb("Wd", [FP, EPI, NF, D])
        th = sb("th", [FP, 2, CT])
        a = sb("a", [FP, 2, CT])
        h = sb("h", [FP, 2, NF, CT])
        w_in = [sem("w_in0"), sem("w_in1")]
        gu_done, th_ready, a_ready, h_ready, d_done, x_ready = (sem(n) for n in ("gu", "th", "a", "h", "d", "x"))

        with nc.Block() as block:
            @block.sync
            def _(sp):
                def load(e, i):
                    wait(sp, d_done, val(i, 2 * PERQ, (e - 1) * 2 * NCH))
                    for W, src in ((Wg, Wg_dram), (Wu, Wu_dram), (Wd, Wd_dram)):
                        src = src[e] if i is None else src[bass.ds(i * EPI + e, 1)].rearrange("a k n -> (a k) n")
                        sp.dma_start(W[:, e % 2, :, :], src.rearrange("(c p) n -> p c n", p=W.shape[0])).then_inc(w_in[e % 2], 16)

                load(0, None)
                load(1, None)
                with nc.sync.Fori(0, E // 2 - 1) as i:
                    load(2, i)
                    load(3, i)

            @block.tensor
            def _(pe):
                def up(q, i):
                    e, c = divmod(q, NCH)
                    if c == 0:
                        pe.wait_ge(w_in[e % 2], val(i, 48, 48 * (e // 2 + 1)))
                    for f in range(NF):
                        u = q * NF + f
                        wait(pe, h_ready, val(i, PERQ * NF, u - 1))
                        for n, W in enumerate((Wg, Wu)):
                            for w in range(DC):
                                last = nc.tensor.matmul(k.psum[0:FP, 2 * (u % 2) + n, 0:CT],
                                                        W[:, e % 2, w, f * FP:(f + 1) * FP],
                                                        k.XT[:, w, c * CT:(c + 1) * CT],
                                                        start=(w == 0), stop=(w == DC - 1))
                        last.then_inc(gu_done, 1)

                def down(q, i):
                    e, c = divmod(q, NCH)
                    pe.wait_ge(h_ready, val(i, PERQ * NF, (q + 1) * NF))
                    for r in range(2):
                        wait(pe, x_ready, val(i, PERQ * 2, 2 * (q - 2) + r + 1))
                        for j in (2 * r, 2 * r + 1):
                            for f in range(NF):
                                last = nc.tensor.matmul(k.psum[0:S, 4 + 2 * (q % 2) + r, (j % 2) * D:(j % 2 + 1) * D],
                                                        h[:, q % 2, f, j * S:(j + 1) * S], Wd[:, e % 2, f, :],
                                                        start=(f == 0), stop=(f == NF - 1))
                        last.then_inc(d_done, 1)

                def step(s, i):
                    if i is not None or s < NQ:
                        up(s, i)
                    if s >= 1:
                        down(s - 1, i)

                pipeline(nc.tensor, NQ, PERQ, 1, step, peel=NCH + 1)

            @block.scalar
            def _(act):
                def step(s, i):
                    for f in range(NF):
                        u = s * NF + f
                        act.wait_ge(gu_done, val(i, PERQ * NF, u + 1))
                        nc.scalar.activation(th[:, u % 2, :], k.psum[0:FP, 2 * (u % 2), 0:CT], ACT.Tanh,
                                             scale=0.5).then_inc(th_ready, 1)

                pipeline(nc.scalar, NQ, PERQ, 0, step, peel=0)

            @block.vector
            def _(dve):
                def gate(q, i):
                    for f in range(NF):
                        u = q * NF + f
                        dve.wait_ge(th_ready, val(i, PERQ * NF, u + 1))
                        nc.vector.scalar_tensor_tensor(a[:, u % 2, :], th[:, u % 2, :], 1.0,
                                                       k.psum[0:FP, 2 * (u % 2), 0:CT], ALU.add, ALU.mult).then_inc(a_ready, 1)
                        dve.wait_ge(a_ready, val(i, PERQ * NF, u + 1))
                        wait(dve, d_done, val(i, PERQ * 2, 2 * (q - 1)))
                        up = k.psum[0:FP, 2 * (u % 2) + 1, 0:CT]
                        if limit is None:
                            last = nc.vector.tensor_tensor(h[:, q % 2, f, :], a[:, u % 2, :], up, ALU.mult)
                        else:
                            last = nc.vector.scalar_tensor_tensor(h[:, q % 2, f, :], a[:, u % 2, :], 2.0 * limit, up,
                                                                  ALU.min, ALU.mult)
                        last.then_inc(h_ready, 1)

                def add(q, i):
                    e, c = divmod(q, NCH)
                    for r in range(2):
                        dve.wait_ge(d_done, val(i, PERQ * 2, 2 * q + r + 1))
                        wait(dve, x_ready, val(i, PERQ * 2, 2 * (q - NCH) + r + 1))
                        for j in (2 * r, 2 * r + 1):
                            b = c * CH + j
                            we = WE[:, b, e:e + 1] if i is None else WE[:, b, bass.ds(i * EPI + e, 1)]
                            last = nc.vector.scalar_tensor_tensor(
                                k.X[:, b, :], k.psum[0:S, 4 + 2 * (q % 2) + r, (j % 2) * D:(j % 2 + 1) * D],
                                we, k.X[:, b, :], ALU.mult, ALU.add)
                        last.then_inc(x_ready, 1)

                def step(s, i):
                    if i is not None or s < NQ:
                        gate(s, i)
                    if s >= 1:
                        add(s - 1, i)

                pipeline(nc.vector, NQ, PERQ, 1, step, peel=NCH + 1)


def mixture(k, tag, Wr_dram, Wg_dram, Wu_dram, Wd_dram, E, K, F, limit=None):
    with k.nc.sbuf_tensor(f"{tag}_WE", [S, B, E], F32) as WE:
        layernorm_transposed(k, f"{tag}_ln")
        router(k, f"{tag}_r", Wr_dram, E, K, WE)
        experts(k, f"{tag}_e", Wg_dram, Wu_dram, Wd_dram, E, F, WE, limit)


def wide_projections(k, tag, WqT_dram, WkT_dram, WvT_dram, QT, KNT, VN):
    nc = k.nc
    with ExitStack() as ctx:
        sb = lambda name, shape, dt=F32: ctx.enter_context(nc.sbuf_tensor(f"{tag}_{name}", shape, dt))
        sem = lambda name: k.sem(f"{tag}_{name}")
        Wq, Wk, Wv = sb("Wq", [P, DC, D]), sb("Wk", [P, DC, D]), sb("Wv", [P, DC, D])
        w_in, done, read = sem("w_in"), sem("done"), sem("read")
        NQ = NCH * 2 * DC
        with nc.Block() as block:
            @block.sync
            def _(sp):
                for W, src in ((Wq, WqT_dram), (Wk, WkT_dram), (Wv, WvT_dram)):
                    sp.dma_start(W[:], src.rearrange("(c p) n -> p c n", p=P)).then_inc(w_in, 16)
                sp.wait_ge(w_in, 48)

            @block.tensor
            def _(pe):
                pe.wait_ge(w_in, 48)
                with nc.tensor.Fori(0, NCH) as c:
                    for n, (W, o) in enumerate(((Wq, 0), (Wq, 1), (Wk, 0), (Wk, 1))):
                        pe.wait_ge(read, c * 4 + n + 1)
                        for w in range(DC):
                            last = nc.tensor.matmul(k.psum[:, n, 0:CT], W[:, w, o * P:(o + 1) * P],
                                                    k.XT[:, w, bass.ds(c * CT, CT)], start=(w == 0), stop=(w == DC - 1))
                        last.then_inc(done, 1)
                for b in range(B):
                    pe.wait_ge(read, NQ + b + 1)
                    for w in range(DC):
                        last = nc.tensor.matmul(k.psum[0:S, 4 + b % 4, 0:D], k.XT[:, w, b * S:(b + 1) * S], Wv[:, w, :],
                                                start=(w == 0), stop=(w == DC - 1))
                    last.then_inc(done, 1)

            @block.scalar
            def _(act):
                act.sem_inc(read, 4)
                with nc.scalar.Fori(0, NCH) as c:
                    for n, (T, o) in enumerate(((QT, 0), (QT, 1), (KNT, 0), (KNT, 1))):
                        act.wait_ge(done, c * 4 + n + 1)
                        nc.scalar.activation(T[:, o, bass.ds(c * CT, CT)], k.psum[:, n, 0:CT], ACT.Copy).then_inc(read, 1)
                for b in range(B):
                    act.wait_ge(done, NQ + b + 1)
                    nc.scalar.activation(VN[:, b, :], k.psum[0:S, 4 + b % 4, 0:D], ACT.Copy).then_inc(read, 1)


def wide_attention(k, tag, ctxT_dram, ctx_dram, QT, mask_dram=None, new=None):
    nc = k.nc
    NEW = S if new else 0
    W = (M + NEW) // 4
    TILES = list(zip(MOFF, MSZ)) + ([(M, S)] if new else [])
    NT = len(TILES)
    TB = 5
    NB = -(-NT // TB)
    SC, TR, OUT = 0, 4, 7
    OT = 3 * S
    SCALE = D ** -0.5
    assert W * 4 == M + NEW and W <= BANK and (NT - 2 * TB) * S <= OT and OT + DC * S <= BANK
    with ExitStack() as ctx:
        sb = lambda name, shape, dt=F32: ctx.enter_context(nc.sbuf_tensor(f"{tag}_{name}", shape, dt))
        sem = lambda name: k.sem(f"{tag}_{name}")
        ctxT = sb("ctxT", [P, 2, DC, M])
        cx = sb("cx", [P, 2, MT, D])
        qb = sb("qb", [P, 2, DC, S])
        pr = sb("pr", [S, 2, M + NEW])
        pt = sb("pt", [P, NT, S])
        mx = sb("mx", [S, 2])
        nb = sb("nb", [S, 2])
        total = sb("total", [S, 2])
        rs = sb("rs", [S, 2])
        keys_in = [sem("keys_in0"), sem("keys_in1")]
        values_in = [sem("values_in0"), sem("values_in1")]
        qb_ready, s_done, mx_ready, nb_ready, p_ready, t_done, pt_ready = (sem(n) for n in ("qb", "s", "mx", "nb", "p", "t", "pt"))
        v_done, rs_ready, o_read = sem("v"), sem("rs"), sem("oread")
        if mask_dram is not None:
            keep = sb("keep", [S, B, M], U8)
            pen = sb("pen", [S, 2, M])
            sm = sb("sm", [S, M])
            valid = sb("valid", [S, 2])
            mask_in, pen_ready, sm_ready, valid_ready = sem("mask_in"), sem("pen"), sem("sm"), sem("valid")
        if new:
            KNT, VN, WoT_dram = new
            Wo = sb("Wo", [P, DC, D])
            on = sb("on", [S, 2, D])
            ont = sb("ont", [P, DC, S])
            w_in, on_ready, ot_done, ont_ready, y_done, y_read = (sem(n) for n in ("w_in", "on", "ot", "ont", "y", "yread"))

        def batch(T, i, b, rows=slice(None)):
            return T[rows, b] if i is None else T[rows, bass.ds(i * 2 + b, 1)].rearrange("p a n -> p (a n)")

        with nc.Block() as block:
            @block.sync
            def _(sp):
                if new:
                    sp.dma_start(Wo[:], WoT_dram.rearrange("(c p) n -> p c n", p=P)).then_inc(w_in, 16)
                if mask_dram is not None:
                    sp.dma_start(keep[:], mask_dram.unsqueeze(0).to_broadcast([S, B, M])).then_inc(mask_in, 16)

                def load(b, i):
                    one = lambda T: T[b] if i is None else T[bass.ds(i * 2 + b, 1)].rearrange("a r c -> (a r) c")
                    full = (MT - 2) * P
                    wait(sp, s_done, val(i, 2, b - 1))
                    sp.dma_start(ctxT[:, b % 2, :, :], one(ctxT_dram).rearrange("(c p) m -> p c m", p=P)).then_inc(keys_in[b % 2], 16)
                    wait(sp, v_done, val(i, 2, b - 1))
                    sp.dma_start(cx[:, b % 2, 0:MT - 2, :],
                                 one(ctx_dram)[0:full, :].rearrange("(t p) d -> p t d", p=P)).then_inc(values_in[b % 2], 16)
                    for t in (MT - 2, MT - 1):
                        sp.dma_start(cx[0:MSZ[t], b % 2, t, :],
                                     one(ctx_dram)[MOFF[t]:MOFF[t] + MSZ[t], :]).then_inc(values_in[b % 2], 16)

                load(0, None)
                load(1, None)
                with nc.sync.Fori(0, B // 2 - 1) as i:
                    load(2, i)
                    load(3, i)

            if mask_dram is not None:
                @block.gpsimd
                def _(pool):
                    pool.wait_ge(mask_in, 16)

                    for b in range(B):
                        wait(pool, sm_ready, b - 1)
                        nc.gpsimd.tensor_scalar(pen[:, b % 2, :], keep[:, b, :], 1.0, 1e30,
                                                ALU.subtract, ALU.mult).then_inc(pen_ready, 1)

            @block.tensor
            def _(pe):
                if new:
                    pe.wait_ge(w_in, 16)

                def scores(b, i):
                    pe.wait_ge(keys_in[b % 2], val(i, 16, 16 * (b // 2 + 1)))
                    pe.wait_ge(qb_ready, val(i, 2, b + 1))
                    wait(pe, sm_ready if mask_dram is not None else p_ready, val(i, 2, b))
                    for g in range(4):
                        old = min(W, M - g * W)
                        for w in range(DC):
                            last = nc.tensor.matmul(k.psum[0:S, SC + g, 0:old], qb[:, b % 2, w, :],
                                                    ctxT[:, b % 2, w, g * W:g * W + old], start=(w == 0), stop=(w == DC - 1))
                        if old < W:
                            for w in range(DC):
                                at = slice(b * S, (b + 1) * S) if i is None else bass.ds(i * (2 * S) + b * S, S)
                                last = nc.tensor.matmul(k.psum[0:S, SC + g, old:W], qb[:, b % 2, w, :], KNT[:, w, at],
                                                        start=(w == 0), stop=(w == DC - 1))
                    last.then_inc(s_done, 1)

                def transpose(b, i):
                    pe.wait_ge(p_ready, val(i, 2, b + 1))
                    for g in range(NB):
                        wait(pe, pt_ready, val(i, 2 * NB, NB * (b - 1) + g + 1))
                        if new and g == 2:
                            wait(pe, ont_ready, val(i, 2, b - 1))
                        for t in range(g * TB, min(NT, (g + 1) * TB)):
                            at, m = TILES[t]
                            last = nc.tensor.transpose(k.psum[0:m, TR + g, (t % TB) * S:(t % TB + 1) * S],
                                                       pr[:, b % 2, at:at + m], k.ident[0:S, 0:S])
                        last.then_inc(t_done, 1)

                def values(b, i):
                    pe.wait_ge(values_in[b % 2], val(i, 48, 48 * (b // 2 + 1)))
                    wait(pe, o_read, val(i, 2, b))
                    if new:
                        wait(pe, y_read, val(i, 2, b))
                    for t, (at, m) in enumerate(TILES):
                        if t % TB == 0:
                            pe.wait_ge(pt_ready, val(i, 2 * NB, NB * b + t // TB + 1))
                        rhs = cx[0:m, b % 2, t, :] if t < MT else batch(VN, i, b)
                        last = nc.tensor.matmul(k.psum[0:S, OUT, 0:D], pt[0:m, t, :], rhs, start=(t == 0), stop=(t == NT - 1))
                    last.then_inc(v_done, 1)

                def turn(b, i):
                    pe.wait_ge(on_ready, val(i, 2, b + 1))
                    wait(pe, ont_ready, val(i, 2, b))
                    for w in range(DC):
                        last = nc.tensor.transpose(k.psum[:, TR + 2, OT + w * S:OT + (w + 1) * S],
                                                   on[:, b % 2, w * P:(w + 1) * P], k.ident[0:S, 0:S])
                    last.then_inc(ot_done, 1)

                def project(b, i):
                    pe.wait_ge(ont_ready, val(i, 2, b + 1))
                    pe.wait_ge(o_read, val(i, 2, b + 1))
                    for w in range(DC):
                        last = nc.tensor.matmul(k.psum[0:S, OUT, 0:D], ont[:, w, :], Wo[:, w, :], start=(w == 0), stop=(w == DC - 1))
                    last.then_inc(y_done, 1)

                def step(s, i):
                    if s >= 1 and (i is not None or s - 1 < B):
                        transpose(s - 1, i)
                    if new and s >= 2:
                        turn(s - 2, i)
                    if i is not None or s < B:
                        scores(s, i)
                    if new and s >= 2:
                        project(s - 2, i)
                    if s >= 1 and (i is not None or s - 1 < B):
                        values(s - 1, i)

                pipeline(nc.tensor, B, 2, 2, step, peel=4)

            @block.scalar
            def _(act):
                def queries(b, i):
                    wait(act, s_done, val(i, 2, b - 1))
                    at = slice(b * S, (b + 1) * S) if i is None else bass.ds(i * (2 * S) + b * S, S)
                    nc.scalar.activation(qb[:, b % 2, :, :], QT[:, :, at], ACT.Copy).then_inc(qb_ready, 1)

                def exps(b, i):
                    act.wait_ge(nb_ready, val(i, 2, b + 1))
                    wait(act, t_done, val(i, 2 * NB, NB * (b - 1)))
                    wait(act, rs_ready, val(i, 2, b - 1))
                    src = sm[:].rearrange("p (g n) -> p g n", g=4) if mask_dram is not None else k.psum[0:S, SC:SC + 4, 0:W]
                    nc.scalar.activation(pr[:, b % 2, :].rearrange("p (g n) -> p g n", g=4), src, ACT.Exp,
                                         scale=SCALE, bias=nb[:, b % 2:b % 2 + 1],
                                         accum_out=total[:, b % 2:b % 2 + 1]).then_inc(p_ready, 1)

                def step(s, i):
                    if i is not None or s < B:
                        queries(s, i)
                    if s >= 1 and (i is not None or s - 1 < B):
                        exps(s - 1, i)

                pipeline(nc.scalar, B, 2, 2, step, peel=4)

            @block.vector
            def _(dve):
                def probabilities_out(b, i):
                    for g in range(NB):
                        dve.wait_ge(t_done, val(i, 2 * NB, NB * b + g + 1))
                        if g == 0:
                            wait(dve, v_done, val(i, 2, b))
                        if new and g == 2:
                            wait(dve, ot_done, val(i, 2, b))
                        for t0, n in equal_runs([m for _, m in TILES], g * TB, min(NT, (g + 1) * TB)):
                            m = TILES[t0][1]
                            src = k.psum[0:m, TR + g, (t0 % TB) * S:(t0 % TB + n) * S]
                            last = nc.vector.tensor_copy(pt[0:m, t0:t0 + n, :].rearrange("p t n -> p (t n)"), src)
                        last.then_inc(pt_ready, 1)

                def maximum(b, i):
                    dve.wait_ge(s_done, val(i, 2, b + 1))
                    m = mx[:, b % 2:b % 2 + 1]
                    wait(dve, p_ready, val(i, 2, b))
                    if mask_dram is not None:
                        dve.wait_ge(pen_ready, val(i, 2, b + 1))
                        nc.vector.tensor_tensor(sm[:].rearrange("p (g n) -> p g n", g=4), k.psum[0:S, SC:SC + 4, 0:W],
                                                pen[:, b % 2, :].rearrange("p (g n) -> p g n", g=4), ALU.add).then_inc(sm_ready, 1)
                        dve.wait_ge(sm_ready, val(i, 2, b + 1))
                        nc.vector.tensor_reduce(m, sm[:], AX.X, ALU.max).then_inc(mx_ready, 1)
                    else:
                        nc.vector.tensor_reduce(m, k.psum[0:S, SC:SC + 4, 0:W], AX.XY, ALU.max).then_inc(mx_ready, 1)
                    dve.wait_ge(mx_ready, val(i, 2, b + 1))
                    nc.vector.tensor_scalar(nb[:, b % 2:b % 2 + 1], m, -SCALE, None, ALU.mult).then_inc(nb_ready, 1)

                def outputs(b, i):
                    r = rs[:, b % 2:b % 2 + 1]
                    dve.wait_ge(p_ready, val(i, 2, b + 1))
                    if mask_dram is not None:
                        nc.vector.tensor_scalar(valid[:, b % 2:b % 2 + 1], mx[:, b % 2:b % 2 + 1], -1e29, None,
                                                ALU.is_gt).then_inc(valid_ready, 1)
                        nc.vector.reciprocal(total[:, b % 2:b % 2 + 1], total[:, b % 2:b % 2 + 1]).then_inc(valid_ready, 1)
                        dve.wait_ge(valid_ready, val(i, 4, 2 * b + 2))
                        nc.vector.tensor_tensor(r, total[:, b % 2:b % 2 + 1], valid[:, b % 2:b % 2 + 1], ALU.mult).then_inc(rs_ready, 1)
                    else:
                        nc.vector.reciprocal(r, total[:, b % 2:b % 2 + 1]).then_inc(rs_ready, 1)
                    dve.wait_ge(rs_ready, val(i, 2, b + 1))
                    dve.wait_ge(v_done, val(i, 2, b + 1))
                    if new:
                        wait(dve, ot_done, val(i, 2, b - 1))
                        nc.vector.tensor_scalar(on[:, b % 2, :], k.psum[0:S, OUT, 0:D], r, None, ALU.mult).then_inc(on_ready, 1)
                        dve.wait_ge(on_ready, val(i, 2, b + 1))
                        dve.sem_inc(o_read, 1)
                    else:
                        xb = batch(k.X, i, b)
                        nc.vector.scalar_tensor_tensor(xb, k.psum[0:S, OUT, 0:D], r, xb, ALU.mult, ALU.add).then_inc(o_read, 1)

                def turned_out(b, i):
                    dve.wait_ge(ot_done, val(i, 2, b + 1))
                    wait(dve, y_done, val(i, 2, b))
                    nc.vector.tensor_copy(ont[:].rearrange("p c n -> p (c n)"), k.psum[:, TR + 2, OT:OT + DC * S]).then_inc(ont_ready, 1)

                def add(b, i):
                    dve.wait_ge(y_done, val(i, 2, b + 1))
                    xb = batch(k.X, i, b)
                    nc.vector.tensor_tensor(xb, k.psum[0:S, OUT, 0:D], xb, ALU.add).then_inc(y_read, 1)

                def step(s, i):
                    if s >= 1 and (i is not None or s - 1 < B):
                        probabilities_out(s - 1, i)
                    if new and s >= 2:
                        turned_out(s - 2, i)
                    if i is not None or s < B:
                        maximum(s, i)
                    if new and s >= 2:
                        add(s - 2, i)
                    if s >= 1 and (i is not None or s - 1 < B):
                        outputs(s - 1, i)

                pipeline(nc.vector, B, 2, 2, step, peel=4)


H2, KV2, HD2 = 16, 4, 128
GRP = H2 // KV2
QI = H2 // KV2
ITEMS = QI + MT
PAIRS = H2 // 2
TAIL = 6


def grouped_attention(k, ctxT_dram, Wq_dram, Wk_dram, Wv_dram, Wo_dram, qw_dram, kw_dram):
    nc = k.nc
    LT = 2
    TB = 5
    NB = -(-MT // TB)
    NS = -(-M // BANK)
    SC, TR, OUT, Y = 0, 3, 6, 7
    KB, TA, VB = 0, 3, 6
    SCALE = HD2 ** -0.5
    KVW = KV2 * HD2
    IN_SLOT = {6: [0], 9: [1], 12: [2], 15: [3], 17: [4]}
    IN_STEP = {0: [5, 6], 1: [7, 8], 2: [9], 3: [10, 11]}
    SPLIT_STEPS = [5, 6, 7, 8]
    with ExitStack() as ctx:
        sb = lambda name, shape, dt=F32: ctx.enter_context(nc.sbuf_tensor(f"g2_{name}", shape, dt))
        sem = lambda name: k.sem(f"g2_{name}")
        Wq, Wo = sb("Wq", [P, DC, H2 * HD2]), sb("Wo", [P, H2, D])
        Wkv = sb("Wkv", [P, 2, 2, DC, KVW], F16)
        w2 = sb("w2", [P, 2])
        wrow = sb("wrow", [P, 2, HD2])
        w = sb("w", [P, 1])
        wmax = sb("wmax", [P, 1])
        pos, neg, inv = sb("pos", [P, 1]), sb("neg", [P, 1]), sb("inv", [P, 1])
        big = sb("big", [P, 4])
        row = sb("row", [1, 2])
        ones = sb("ones", [1, P])
        pow2 = sb("pow2", [P, 2])
        up, undo = sb("up", [P, 2]), sb("undo", [P, 1])
        ctxT = sb("ctxT", [P, DC, M])
        cs = sb("cs", [P, 2, DC, M], F16)
        xb = sb("xb", [P, DC, S])
        sq = sb("sq", [P, KVW])
        ssq = sb("ssq", [P, KV2])
        lnn = sb("lnn", [P, KV2])
        rn = sb("rn", [P, KV2])
        nn = sb("nn", [P, 2, KVW])
        KT = sb("KT", [P, 2, KV2, M], F16)
        QT = sb("QT", [P, 2, H2, S], F16)
        V = sb("V", [P, MT, KVW])
        pr = sb("pr", [S, 2, M])
        pt = sb("pt", [P, 2, MT, 2, S])
        ot = sb("ot", [P, 2, 2 * S])
        mx, top, nb, total, rs = sb("mx", [S, 2, NS]), sb("top", [S, 2]), sb("nb", [S, 2]), sb("total", [S, 2]), sb("rs", [S, 2])
        w_in, wo_in, wkv_in, w2_in, wk_step, ctx_in = sem("w_in"), sem("wo_in"), sem("wkv_in"), sem("w2_in"), sem("wk"), sem("ctx_in")
        big_step, big_pe, up_ready, wh_ready, wl_ready, ch_ready, cl_ready = (sem(n) for n in ("big", "bigpe", "up", "wh", "wl", "ch", "cl"))
        xb_ready, a_done, vp_done, v_ready, sq_ready, ssq_ready, ln_ready, rn_ready, nn_ready, ta_done, qhi_ready, khi_ready, ta_read = (
            sem(n) for n in ("xb", "a", "vp", "v", "sq", "ssq", "ln", "rn", "nn", "ta", "qhi", "khi", "tar"))
        s_done, mx_ready, top_ready, nb_ready, e_ready, rs_ready, p_ready, t_done, pt_ready, o_done, ot_ready, y_done, y_read = (
            sem(n) for n in ("s", "mx", "top", "nb", "e", "rs", "p", "t", "pt", "o", "ot", "y", "yr"))
        rows = [S] * QI + MSZ

        class At:

            def __init__(self, b, i):
                self.b, self.i = b, i
                self.first = i is None and b == 0

            def item(self, j):
                return val(self.i, 2 * ITEMS, self.b * ITEMS + j)

            def tile(self, t):
                return val(self.i, 2 * MT, self.b * MT + t)

            def unit(self, h, per=1, extra=0):
                return val(self.i, 2 * H2 * per, (self.b * H2 + h) * per + extra)

            def parts(self, n):
                return val(self.i, 2 * DC, self.b * DC + n)

            def pair(self, p):
                return val(self.i, 2 * PAIRS, self.b * PAIRS + p)

            def batch(self, n):
                return val(self.i, 2, self.b + n)

        def batches(eng, body, tail=None):
            body(0, None)
            body(1, None)
            with eng.Fori(0, B // 2 - 1) as i:
                body(2, i)
                body(3, i)
            for s in range(H2, H2 + TAIL) if tail else ():
                tail(s, At(B - 1, None))

        with nc.Block() as block:
            @block.sync
            def _(sp):
                sp.dma_start(wrow[:, 0, :], qw_dram.unsqueeze(0).to_broadcast([P, HD2])).then_inc(w2_in, 16)
                sp.dma_start(wrow[:, 1, :], kw_dram.unsqueeze(0).to_broadcast([P, HD2])).then_inc(w2_in, 16)
                sp.dma_start(w2[:, 0:1], qw_dram.unsqueeze(1)).then_inc(w2_in, 16)
                sp.dma_start(w2[:, 1:2], kw_dram.unsqueeze(1)).then_inc(w2_in, 16)
                sp.dma_start(V[:, 0:DC, :], Wk_dram.rearrange("(c p) n -> p c n", p=P)).then_inc(wkv_in, 16)
                sp.dma_start(V[:, DC:2 * DC, :], Wv_dram.rearrange("(c p) n -> p c n", p=P)).then_inc(wkv_in, 16)
                sp.dma_start(Wq[:], Wq_dram.rearrange("(c p) n -> p c n", p=P)).then_inc(w_in, 16)

                def load(b, i):
                    wait(sp, cl_ready, val(i, 2 * DC, b * DC))
                    src = ctxT_dram[b] if i is None else ctxT_dram[bass.ds(i * 2 + b, 1)].rearrange("a d m -> (a d) m")
                    sp.dma_start(ctxT[:], src.rearrange("(c p) m -> p c m", p=P)).then_inc(ctx_in, 16)

                load(0, None)
                sp.dma_start(Wo[:], Wo_dram.rearrange("(c p) n -> p c n", p=P)).then_inc(wo_in, 16)
                load(1, None)
                with nc.sync.Fori(0, B // 2 - 1) as i:
                    load(2, i)
                    load(3, i)

            @block.tensor
            def _(pe):
                pe.wait_ge(big_step, 1)
                for n in range(2):
                    last = nc.tensor.transpose(k.psum[0:1, n, 0:P], big[:, 3 * n:3 * n + 1], k.ident[:])
                last.then_inc(big_pe, 1)
                pe.wait_ge(big_step, 2)
                nc.tensor.matmul(k.psum[:, 2, 0:2], ones[:], row[:], start=True, stop=True).then_inc(big_pe, 1)
                pe.wait_ge(up_ready, 1)
                pe.wait_ge(w_in, 16)

                def products(out, m, t, kv):
                    for c in range(DC):
                        for j, (x, y) in enumerate(((0, 0), (0, 1), (1, 0))):
                            last = nc.tensor.matmul(out, cs[:, x, c, MOFF[t]:MOFF[t] + m], Wkv[:, kv, y, c, :],
                                                    start=(c == 0 and j == 0), stop=(c == DC - 1 and j == 2))
                    return last

                def project(j, at):
                    m, bank = rows[j], KB + j % 3
                    if j == 0:
                        pe.wait_ge(xb_ready, at.batch(1))
                        wait(pe, e_ready, at.unit(0))
                    if j < 3:
                        wait(pe, nn_ready, at.item(0))
                    else:
                        pe.wait_ge(nn_ready, at.item(j - 2))
                    if j == QI:
                        if at.first:
                            pe.wait_ge(wl_ready, 2)
                        pe.wait_ge(cl_ready, at.parts(DC))
                    if j < QI:
                        for c in range(DC):
                            last = nc.tensor.matmul(k.psum[0:m, bank, :], xb[:, c, :], Wq[:, c, j * KVW:(j + 1) * KVW],
                                                    start=(c == 0), stop=(c == DC - 1))
                    else:
                        last = products(k.psum[0:m, bank, :], m, j - QI, 0)
                    last.then_inc(a_done, 1)

                def project_values(t, at):
                    m = MSZ[t]
                    if t == 0:
                        wait(pe, ot_ready, at.pair(0))
                    elif t == 1:
                        wait(pe, y_read, at.batch(0))
                    else:
                        pe.wait_ge(v_ready, at.tile(t - 1))
                    products(k.psum[0:m, VB + t % 2, :], m, t, 1).then_inc(vp_done, 1)

                def turn(j, at):
                    m = rows[j]
                    pe.wait_ge(nn_ready, at.item(j + 1))
                    if j < 2:
                        wait(pe, pt_ready, at.unit(0, NB))
                        wait(pe, ta_read, at.item(0))
                    else:
                        pe.wait_ge(ta_read, at.item(j - 1))
                    for g in range(KV2):
                        last = nc.tensor.transpose(k.psum[:, TA + j % 2, g * m:(g + 1) * m],
                                                   nn[0:m, j % 2, g * HD2:(g + 1) * HD2], k.ident[0:m, 0:m])
                    last.then_inc(ta_done, 1)

                def scores(h, at):
                    if h == 0:
                        pe.wait_ge(ta_read, at.item(ITEMS))
                    wait(pe, e_ready, at.unit(h))
                    for g in range(NS):
                        n = min(BANK, M - g * BANK)
                        for j, (q, key) in enumerate(((0, 0), (0, 1), (1, 0))):
                            last = nc.tensor.matmul(k.psum[0:S, SC + g, 0:n], QT[:, q, h, :],
                                                    KT[:, key, h // GRP, g * BANK:g * BANK + n], start=(j == 0), stop=(j == 2))
                        last.then_inc(s_done, 1)

                def transpose(h, at):
                    pe.wait_ge(p_ready, at.unit(h + 1))
                    for g in range(NB):
                        wait(pe, pt_ready, at.unit(h - 1, NB, g + 1))
                        for t in range(g * TB, min(MT, (g + 1) * TB)):
                            last = nc.tensor.transpose(k.psum[0:MSZ[t], TR + g, (t % TB) * S:(t % TB + 1) * S],
                                                       pr[:, h % 2, MOFF[t]:MOFF[t] + MSZ[t]], k.ident[0:S, 0:S])
                        last.then_inc(t_done, 1)

                def values(p, half, at):
                    if half == 0:
                        wait(pe, ot_ready, at.pair(p))
                        if p == 0:
                            pe.wait_ge(v_ready, at.tile(MT))
                        pe.wait_ge(pt_ready, at.unit(2 * p + 2, NB))
                    for t in range(half * MT // 2, (half + 1) * MT // 2):
                        g = 2 * p // GRP
                        last = nc.tensor.matmul(k.psum[:, OUT, 0:2 * S], V[0:MSZ[t], t, g * HD2:(g + 1) * HD2],
                                                pt[0:MSZ[t], p % 2, t, :, :].rearrange("p h n -> p (h n)"),
                                                start=(t == 0), stop=(t == MT - 1))
                    if half == 1:
                        last.then_inc(o_done, 1)

                def output(p, at):
                    if at.first and p == 0:
                        pe.wait_ge(wo_in, 16)
                    pe.wait_ge(ot_ready, at.pair(p + 1))
                    for h in (2 * p, 2 * p + 1):
                        last = nc.tensor.matmul(k.psum[0:S, Y, 0:D], ot[:, p % 2, (h % 2) * S:(h % 2 + 1) * S], Wo[:, h, :],
                                                start=(h == 0), stop=(h == H2 - 1), skip_group_check=True)
                    last.then_inc(y_done, 1)

                def head_step(s, at):
                    if s < H2:
                        scores(s, at)
                    if 2 <= s < H2 + 2:
                        transpose(s - 2, at)
                    for t in IN_STEP.get(s, []):
                        project_values(t, at)
                    if s >= 6 and s % 2 == 0 and s < H2 + 4:
                        output((s - 6) // 2, at)
                    if 4 <= s < H2 + 4:
                        values((s - 4) // 2, s % 2, at)
                    if s == H2 + 5:
                        output(PAIRS - 1, at)

                def body(b, i):
                    at = At(b, i)
                    for j in range(ITEMS + LT):
                        if j < TAIL and not at.first:
                            head_step(H2 + j, At(b - 1, i))
                        if j < ITEMS:
                            project(j, at)
                        for t in IN_SLOT.get(j, []):
                            project_values(t, at)
                        if j >= LT:
                            turn(j - LT, at)
                    for s in range(H2):
                        head_step(s, at)

                batches(nc.tensor, body, head_step)

            @block.scalar
            def _(act):
                nc.scalar.preload_act_table_set(LN_EXP)
                act.wait_ge(up_ready, 1)
                for n in range(2):
                    nc.scalar.activation(Wkv[:, n, 0, :, :], V[:, n * DC:(n + 1) * DC, :], ACT.Copy, scale=up[:, 1:2]).then_inc(wh_ready, 1)
                act.wait_ge(wl_ready, 2)
                act.wait_ge(wk_step, 6)

                def split(n, at):
                    c = n // 2
                    if n == 0:
                        act.wait_ge(ctx_in, val(at.i, 32, 16 * (at.b + 1)))
                        wait(act, vp_done, at.tile(0))
                    if n % 2 == 0:
                        nc.scalar.activation(cs[:, 0, c, :], ctxT[:, c, :], ACT.Copy, scale=up[:, 0:1])
                    else:
                        nc.scalar.activation(ctxT[:, c, :], ctxT[:, c, :], ACT.Copy, scale=up[:, 0:1]).then_inc(ch_ready, 1)

                def square(j, at):
                    m, bank = rows[j], KB + j % 3
                    act.wait_ge(a_done, at.item(j + 1))
                    nc.scalar.activation(sq[0:m, :], k.psum[0:m, bank, :], ACT.Square,
                                         scale=1.0 if j < QI else undo[0:m, 0:1]).then_inc(sq_ready, 1)

                def values_out(t, at):
                    m = MSZ[t]
                    act.wait_ge(vp_done, at.tile(t + 1))
                    nc.scalar.activation(V[0:m, t, :], k.psum[0:m, VB + t % 2, :], ACT.Copy, scale=undo[0:m, 0:1]).then_inc(v_ready, 1)

                def norm(j, at):
                    m = rows[j]
                    act.wait_ge(ssq_ready, at.item(j + 1))
                    nc.scalar.activation(lnn[0:m, :], ssq[0:m, :], ACT.Ln, scale=1.0 / HD2,
                                         bias=k.eps[0:m, 1:2]).then_inc(ln_ready, 1)
                    act.wait_ge(ln_ready, at.item(j + 1))
                    nc.scalar.activation(rn[0:m, :], lnn[0:m, :], ACT.Exp, scale=-0.5).then_inc(rn_ready, 1)

                def keys_hi(t, at):
                    m, j = MSZ[t], QI + t
                    act.wait_ge(ta_done, at.item(j + 1))
                    src = k.psum[:, TA + j % 2, 0:KV2 * m].rearrange("p (g m) -> p g m", g=KV2)
                    nc.scalar.activation(KT[:, 0, :, MOFF[t]:MOFF[t] + m], src, ACT.Copy).then_inc(khi_ready, 1)

                def exps(h, at):
                    act.wait_ge(nb_ready, at.unit(h + 1))
                    wait(act, t_done, at.unit(h - 1, NB))
                    nc.scalar.activation(pr[:, h % 2, :], k.psum[0:S, SC:SC + 3, :].rearrange("p g n -> p (g n)")[:, 0:M],
                                         ACT.Exp, scale=pos[0:S, 0:1], bias=nb[:, h % 2:h % 2 + 1],
                                         accum_out=total[:, h % 2:h % 2 + 1]).then_inc(e_ready, 1)

                def outputs_out(p, at):
                    act.wait_ge(o_done, at.pair(p + 1))
                    wait(act, y_done, at.pair(p - 1))
                    nc.scalar.activation(ot[:, p % 2, :], k.psum[:, OUT, 0:2 * S], ACT.Copy).then_inc(ot_ready, 1)

                def head_step(s, at):
                    if s >= 6 and s % 2 == 0 and s < H2 + 4:
                        outputs_out((s - 6) // 2, at)
                    if s < H2:
                        exps(s, at)
                        for t in IN_STEP.get(s, []):
                            values_out(t, at)
                    if s == H2 + 4:
                        outputs_out(PAIRS - 1, at)

                def body(b, i, last=False):
                    at = At(b, i)
                    wait(act, a_done, at.item(0))
                    tokens = slice(b * S, (b + 1) * S) if i is None else bass.ds(i * (2 * S) + b * S, S)
                    nc.scalar.activation(xb[:], k.XT[:, :, tokens], ACT.Copy).then_inc(xb_ready, 1)
                    for j in range(ITEMS + LT):
                        if j < TAIL and not at.first:
                            head_step(H2 + j, At(b - 1, i))
                        if j < ITEMS:
                            square(j, at)
                        if j >= LT + QI:
                            keys_hi(j - LT - QI, at)
                        if j < ITEMS:
                            norm(j, at)
                        for t in IN_SLOT.get(j, []):
                            values_out(t, at)
                    for s in range(H2):
                        head_step(s, at)
                        if not last and s in SPLIT_STEPS:
                            split(SPLIT_STEPS.index(s), At(b + 1, i))

                for n in range(2 * DC):
                    split(n, At(0, None))
                body(0, None)
                body(1, None)
                with nc.scalar.Fori(0, B // 2 - 2) as i:
                    body(2, i)
                    body(3, i)
                body(B - 2, None)
                body(B - 1, None, last=True)
                for s in range(H2, H2 + TAIL):
                    head_step(s, At(B - 1, None))

            @block.gpsimd
            def _(pool):
                def body(b, i):
                    at = At(b, i)
                    for c in range(DC):
                        pool.wait_ge(ch_ready, at.parts(c + 1))
                        nc.gpsimd.tensor_tensor(cs[:, 1, c, :], ctxT[:, c, :], cs[:, 0, c, :], ALU.subtract).then_inc(cl_ready, 1)

                batches(nc.gpsimd, body)

            @block.vector
            def _(dve):
                nc.vector.memset(ones[:], 1.0)
                dve.wait_ge(wkv_in, 32)
                nc.vector.tensor_reduce(big[:, 0:1], k.ctx_max[:], AX.XY, ALU.max)
                nc.vector.tensor_reduce(big[:, 3:4], V[:, 0:2 * DC, :], AX.XY, ALU.max, apply_absolute_value=True).then_inc(big_step, 1)
                dve.wait_ge(big_pe, 1)
                nc.vector.tensor_reduce(row[:], k.psum[0:1, 0:2, 0:P], AX.X, ALU.max).then_inc(big_step, 1)
                dve.wait_ge(big_pe, 2)
                nc.vector.tensor_scalar(pow2[:], k.psum[:, 2, 0:2], 1e-30, None, ALU.max).then_inc(big_step, 1)
                dve.wait_ge(big_step, 3)
                nc.vector.tensor_scalar(pow2[:].bitcast(U32), pow2[:].bitcast(U32), 0x7F800000, None, ALU.bitwise_and).then_inc(big_step, 1)
                dve.wait_ge(big_step, 4)
                nc.vector.reciprocal(up[:], pow2[:]).then_inc(big_step, 1)
                nc.vector.scalar_tensor_tensor(undo[:], pow2[:, 0:1], 2.0 ** -24, pow2[:, 1:2], ALU.mult, ALU.mult)
                dve.wait_ge(big_step, 5)
                nc.vector.tensor_scalar(up[:], up[:], 2.0 ** 12, None, ALU.mult).then_inc(up_ready, 1)
                dve.wait_ge(up_ready, 1)
                for n in range(2):
                    dve.wait_ge(wh_ready, n + 1)
                    nc.vector.scalar_tensor_tensor(Wkv[:, n, 1, :, :], V[:, n * DC:(n + 1) * DC, :], up[:, 1:2],
                                                   Wkv[:, n, 0, :, :], ALU.mult, ALU.subtract).then_inc(wl_ready, 1)

                dve.wait_ge(w2_in, 64)
                nc.vector.tensor_tensor(w[:], w2[:, 0:1], w2[:, 1:2], ALU.mult)
                nc.vector.tensor_tensor(wrow[:, 0, :], wrow[:, 0, :], wrow[:, 1, :], ALU.mult).then_inc(wk_step, 1)
                dve.wait_ge(wk_step, 1)
                nc.vector.tensor_reduce(wmax[:], wrow[:, 0, :], AX.X, ALU.max, apply_absolute_value=True).then_inc(wk_step, 1)
                dve.wait_ge(wk_step, 2)
                nc.vector.tensor_scalar(wmax[:], wmax[:], 1e-30, None, ALU.max).then_inc(wk_step, 1)
                dve.wait_ge(wk_step, 3)
                nc.vector.reciprocal(inv[:], wmax[:])
                nc.vector.tensor_scalar(pos[:], wmax[:], SCALE, None, ALU.mult)
                nc.vector.tensor_scalar(neg[:], wmax[:], -SCALE, None, ALU.mult).then_inc(wk_step, 2)
                dve.wait_ge(wk_step, 5)
                nc.vector.tensor_tensor(w[:], w[:], inv[:], ALU.mult).then_inc(wk_step, 1)
                dve.wait_ge(wk_step, 6)

                dve.wait_ge(up_ready, 1)

                def squares(j, at):
                    m = rows[j]
                    dve.wait_ge(sq_ready, at.item(j + 1))
                    nc.vector.reduce_sum(ssq[0:m, :], sq[0:m, :].rearrange("p (g d) -> p g d", g=KV2), AX.X).then_inc(ssq_ready, 1)

                def normalise(j, at):
                    m, bank = rows[j], KB + j % 3
                    dve.wait_ge(rn_ready, at.item(j + 1))
                    wait(dve, ta_done, at.item(j - 1))
                    dst = nn[0:m, j % 2, :].rearrange("p (g d) -> p g d", g=KV2)
                    src = k.psum[0:m, bank, :].rearrange("p (g d) -> p g d", g=KV2)
                    factor = rn[0:m, :].unsqueeze(2).to_broadcast([m, KV2, HD2])
                    if j < QI:
                        last = nc.vector.tensor_tensor(dst, src, factor, ALU.mult)
                    else:
                        last = nc.vector.scalar_tensor_tensor(dst, src, undo[0:m, 0:1], factor, ALU.mult, ALU.mult)
                    last.then_inc(nn_ready, 1)

                def turned_out(j, at):
                    m = rows[j]
                    dve.wait_ge(ta_done, at.item(j + 1))
                    src = k.psum[:, TA + j % 2, 0:KV2 * m].rearrange("p (g m) -> p g m", g=KV2)
                    if j < QI:
                        hi, lo = (QT[:, n, j * GRP:(j + 1) * GRP, :] for n in range(2))
                        nc.vector.tensor_scalar(hi, src, w[:, 0:1], None, ALU.mult).then_inc(qhi_ready, 1)
                        dve.wait_ge(qhi_ready, val(at.i, 2 * QI, at.b * QI + j + 1))
                        last = nc.vector.scalar_tensor_tensor(lo, src, w[:, 0:1], hi, ALU.mult, ALU.subtract)
                    else:
                        t = j - QI
                        hi, lo = (KT[:, n, :, MOFF[t]:MOFF[t] + m] for n in range(2))
                        dve.wait_ge(khi_ready, at.tile(t + 1))
                        last = nc.vector.tensor_tensor(lo, src, hi, ALU.subtract)
                    last.then_inc(ta_read, 1)

                def maximum(h, at):
                    for g in range(NS):
                        dve.wait_ge(s_done, at.unit(h, NS, g + 1))
                        nc.vector.tensor_reduce(mx[:, h % 2, g:g + 1], k.psum[0:S, SC + g, 0:min(BANK, M - g * BANK)],
                                                AX.X, ALU.max).then_inc(mx_ready, 1)
                    dve.wait_ge(mx_ready, at.unit(h + 1, NS))
                    nc.vector.tensor_reduce(top[:, h % 2:h % 2 + 1], mx[:, h % 2, :], AX.X, ALU.max).then_inc(top_ready, 1)
                    dve.wait_ge(top_ready, at.unit(h + 1))
                    nc.vector.tensor_scalar(nb[:, h % 2:h % 2 + 1], top[:, h % 2:h % 2 + 1], neg[0:S, 0:1], None,
                                            ALU.mult).then_inc(nb_ready, 1)

                def divide(h, at):
                    dve.wait_ge(e_ready, at.unit(h + 1))
                    nc.vector.reciprocal(rs[:, h % 2:h % 2 + 1], total[:, h % 2:h % 2 + 1]).then_inc(rs_ready, 1)
                    dve.wait_ge(rs_ready, at.unit(h + 1))
                    nc.vector.tensor_scalar(pr[:, h % 2, :], pr[:, h % 2, :], rs[:, h % 2:h % 2 + 1], None,
                                            ALU.mult).then_inc(p_ready, 1)

                def probabilities_out(h, at):
                    p = h // 2
                    for g in range(NB):
                        dve.wait_ge(t_done, at.unit(h, NB, g + 1))
                        if g == 0 and h % 2 == 0:
                            wait(dve, o_done, at.pair(p - 1))
                        for t0, n in equal_runs(MSZ, g * TB, min(MT, (g + 1) * TB)):
                            m = MSZ[t0]
                            src = k.psum[0:m, TR + g, (t0 % TB) * S:(t0 % TB + n) * S].rearrange("p (t n) -> p t n", t=n)
                            last = nc.vector.tensor_copy(pt[0:m, p % 2, t0:t0 + n, h % 2, :], src)
                        last.then_inc(pt_ready, 1)

                def add(at):
                    dve.wait_ge(y_done, at.pair(PAIRS))
                    xr = k.X[:, at.b, :] if at.i is None else k.X[:, bass.ds(at.i * 2 + at.b, 1), :].rearrange("p a d -> p (a d)")
                    nc.vector.tensor_tensor(xr, k.psum[0:S, Y, 0:D], xr, ALU.add).then_inc(y_read, 1)

                def head_step(s, at):
                    if s < H2:
                        maximum(s, at)
                    if 1 <= s < H2 + 1:
                        divide(s - 1, at)
                    if 2 <= s < H2 + 2:
                        probabilities_out(s - 2, at)
                    if s == H2 + 5:
                        add(at)

                def body(b, i):
                    at = At(b, i)
                    for j in range(ITEMS + LT):
                        if j < TAIL and not at.first:
                            head_step(H2 + j, At(b - 1, i))
                        if j < ITEMS:
                            squares(j, at)
                        if j >= LT:
                            turned_out(j - LT, at)
                        if j < ITEMS:
                            normalise(j, at)
                    for s in range(H2):
                        head_step(s, at)

                batches(nc.vector, body, head_step)


QMAX = 127.0
ROUND = 1.5 * 2.0 ** 23


def quantise(nc, link, T, amax, scale, inv):
    p, g, n = T.shape
    wide = lambda ap: ap.unsqueeze(2).to_broadcast([p, g, n])
    link(nc.vector.tensor_reduce(amax, T, AX.X, ALU.max, apply_absolute_value=True))
    link(nc.vector.tensor_scalar(scale, amax, 0.0, None, ALU.is_equal))
    link(nc.vector.scalar_tensor_tensor(scale, amax, 1.0 / QMAX, scale, ALU.mult, ALU.add))
    link(nc.vector.reciprocal(inv, scale))
    link(nc.vector.tensor_tensor(T, T, wide(inv), ALU.mult))
    link(nc.vector.tensor_scalar(T, T, ROUND, ROUND, ALU.add, ALU.subtract))
    link(nc.vector.tensor_scalar(T, T, QMAX, -QMAX, ALU.min, ALU.max))
    link(nc.vector.tensor_tensor(T, T, wide(scale), ALU.mult))


def quantised_layer(k, KT_dram, bias_dram):
    nc = k.nc
    with ExitStack() as ctx:
        sb = lambda name, shape, dt=F32: ctx.enter_context(nc.sbuf_tensor(f"q3_{name}", shape, dt))
        sem = lambda name: k.sem(f"q3_{name}")
        KTq = sb("KTq", [P, DC, D])
        Kq = sb("Kq", [P, DC, D])
        bq = sb("bq", [S, 1, D])
        T = sb("T", [S, B, D])
        stats, mv, lnv, rstd = sb("stats", [S, B, 6]), sb("mv", [S, B, 2]), sb("lnv", [S, B]), sb("rstd", [S, B])
        amax, scale, inv = sb("amax", [P, B]), sb("scale", [P, B]), sb("inv", [P, B])
        w_in, step, mv_ready, ln_ready, rstd_ready = sem("w_in"), sem("step"), sem("mv"), sem("ln"), sem("rstd")
        kq_ready, kt_done, kq_read, t_ready, xt_done, xt_read, y_done = (
            sem(n) for n in ("kq", "ktd", "kqr", "t", "xtd", "xtr", "y"))
        with nc.Block() as block:
            @block.sync
            def _(sp):
                sp.dma_start(KTq[:], KT_dram.rearrange("(c p) n -> p c n", p=P)).then_inc(w_in, 16)
                sp.dma_start(bq[:], bias_dram.unsqueeze(0).unsqueeze(0).to_broadcast([S, 1, D])).then_inc(w_in, 16)
                sp.wait_ge(w_in, 32)

            @block.scalar
            def _(act):
                nc.scalar.preload_act_table_set(LN_EXP)
                act.wait_ge(mv_ready, B)
                nc.scalar.activation(lnv[:], mv[:, :, 1], ACT.Ln, bias=k.eps[0:S, 0:1]).then_inc(ln_ready, 1)
                act.wait_ge(ln_ready, 1)
                nc.scalar.activation(rstd[:], lnv[:], ACT.Exp, scale=-0.5).then_inc(rstd_ready, 1)
                act.wait_ge(kt_done, 1)
                nc.scalar.activation(Kq[:], k.psum[:, 0:DC, 0:D], ACT.Copy).then_inc(kq_read, 1)
                for c in range(NCH):
                    act.wait_ge(xt_done, c + 1)
                    nc.scalar.activation(k.XT[:, :, c * CT:(c + 1) * CT], k.psum[:, 2 + 2 * (c % 2):4 + 2 * (c % 2), 0:CT],
                                         ACT.Copy).then_inc(xt_read, 1)

            @block.tensor
            def _(pe):
                pe.wait_ge(kq_ready, 1)
                for o in range(DC):
                    for w in range(DC):
                        last = nc.tensor.transpose(k.psum[:, w, o * P:(o + 1) * P], KTq[:, o, w * P:(w + 1) * P], k.ident[:])
                last.then_inc(kt_done, 1)
                pe.wait_ge(t_ready, 1)
                for c in range(NCH):
                    wait(pe, xt_read, c - 1)
                    for j in range(CH):
                        for w in range(DC):
                            last = nc.tensor.transpose(k.psum[:, 2 + 2 * (c % 2) + w, j * S:(j + 1) * S],
                                                       T[:, c * CH + j, w * P:(w + 1) * P], k.ident[0:S, 0:S])
                    last.then_inc(xt_done, 1)
                pe.wait_ge(kq_read, 1)
                pe.wait_ge(xt_read, NCH)
                for b in range(B):
                    for w in range(DC):
                        last = nc.tensor.matmul(k.psum[0:S, b // 2, (b % 2) * D:(b % 2 + 1) * D],
                                                k.XT[:, w, b * S:(b + 1) * S], Kq[:, w, :], start=(w == 0), stop=(w == DC - 1))
                last.then_inc(y_done, 1)

            @block.vector
            def _(dve):
                count = [0]

                def link(ins):
                    count[0] += 1
                    ins.then_inc(step, 1)
                    dve.wait_ge(step, count[0])

                for b in range(B):
                    last = nc.vector.bn_stats(stats[:, b, :], k.X[:, b, :])
                    last.then_inc(step, 1)
                count[0] += B
                dve.wait_ge(step, count[0])
                for b in range(B):
                    nc.vector.bn_aggr(mv[:, b, :], stats[:, b, :]).then_inc(mv_ready, 1)
                dve.wait_ge(w_in, 32)
                quantise(nc, link, KTq[:], amax[:, 0:DC], scale[:, 0:DC], inv[:, 0:DC])
                dve.sem_inc(kq_ready, 1)
                quantise(nc, link, bq[:], amax[0:S, 0:1], scale[0:S, 0:1], inv[0:S, 0:1])
                dve.wait_ge(rstd_ready, 1)
                for b in range(B):
                    last = nc.vector.tensor_scalar(T[:, b, :], k.X[:, b, :], mv[:, b, 0:1], rstd[:, b:b + 1],
                                                   ALU.subtract, ALU.mult)
                    last.then_inc(step, 1)
                count[0] += B
                dve.wait_ge(step, count[0])
                quantise(nc, link, T[:], amax[0:S, :], scale[0:S, :], inv[0:S, :])
                dve.sem_inc(t_ready, 1)
                dve.wait_ge(y_done, 1)
                y = k.psum[0:S, :, 0:2 * D].rearrange("p g (two d) -> p (g two) d", two=2)[:, 0:B, :]
                link(nc.vector.tensor_tensor(T[:], y, bq[:].to_broadcast([S, B, D]), ALU.add))
                link(nc.vector.tensor_scalar(T[:], T[:], 0.0, None, ALU.max))
                quantise(nc, link, T[:], amax[0:S, :], scale[0:S, :], inv[0:S, :])
                link(nc.vector.tensor_tensor(k.X[:], k.X[:], T[:], ALU.add))


def program(nc, x, ctx, ctxT, mask, L0_WqT, L0_WkvT, L0_Wr, L0_Wg, L0_Wu, L0_Wd, L1_Wr, L1_Wg, L1_Wu, L1_Wd,
            L2_Wq, L2_Wk, L2_Wv, L2_Wo, L2_qw, L2_kw, L2_WrT, L2_w1, L2_v1, L2_w2,
            L3_WqT, L3_WkT, L3_WvT, L3_WoT, L3_kernelT, L3_bias, out):
    with ExitStack() as stack:
        k = Kernel(nc, stack)
        setup(k, x)
        layernorm_transposed(k, "ln0")
        with nc.sbuf_tensor("QT0", [P, B, G0, S], F16) as QT:
            heads32_queries(k, L0_WqT, QT)
            heads32_attention(k, ctxT, L0_WkvT, QT)
        mixture(k, "m0", L0_Wr, L0_Wg, L0_Wu, L0_Wd, 8, 2, 256, limit=7.0)
        layernorm_transposed(k, "ln1")
        wide_attention(k, "w1", ctxT, ctx, k.XT, mask_dram=mask.bitcast(U8))
        mixture(k, "m1", L1_Wr, L1_Wg, L1_Wu, L1_Wd, 8, 2, 256)
        k.recycle_semaphores()
        layernorm_transposed(k, "ln2")
        grouped_attention(k, ctxT, L2_Wq, L2_Wk, L2_Wv, L2_Wo, L2_qw, L2_kw)
        mixture(k, "m2", L2_WrT, L2_w1, L2_v1, L2_w2, 32, 8, 96)
        layernorm_transposed(k, "ln3")
        with (nc.sbuf_tensor("QT3", [P, DC, B * S], F32) as QT, nc.sbuf_tensor("KNT3", [P, DC, B * S], F32) as KNT,
              nc.sbuf_tensor("VN3", [S, B, D], F32) as VN):
            wide_projections(k, "p3", L3_WqT, L3_WkT, L3_WvT, QT, KNT, VN)
            wide_attention(k, "w3", ctxT, ctx, QT, new=(KNT, VN, L3_WoT))
        quantised_layer(k, L3_kernelT, L3_bias)
        store(k, out)


def kernel(x, ctx_2048, mask_BxS2_bk0, mask_BxSx4224_bf0, L0_xattn_Wq, L0_xattn_Wk, L0_xattn_Wv, L0_ffn_Wr, L0_ffn_Wg,
           L0_ffn_Wu, L0_ffn_Wd, L1_ffn_Wr, L1_ffn_Wg, L1_ffn_Wu, L1_ffn_Wd, L2_xattn_Wq, L2_xattn_Wk, L2_xattn_Wv,
           L2_xattn_Wo, L2_xattn_q_norm_w, L2_xattn_k_norm_w, L2_ffn_wg, L2_ffn_w1, L2_ffn_v1, L2_ffn_w2,
           L3_xattn_wq, L3_xattn_wk, L3_xattn_wv, L3_xattn_wo, L3_ffn_kernel, L3_ffn_bias):
    import numpy as np
    import concourse.bacc as bacc
    from concourse.bass_utils import run_bass_kernel_spmd

    a = {n: np.asarray(v) for n, v in locals().items() if n not in ("np", "bacc", "run_bass_kernel_spmd")}
    ins = dict(
        x=a["x"], ctx=a["ctx_2048"], ctxT=a["ctx_2048"].transpose(0, 2, 1), mask=a["mask_BxS2_bk0"].view(np.int32),
        L0_WqT=a["L0_xattn_Wq"].T, L0_WkvT=np.concatenate([a["L0_xattn_Wk"], a["L0_xattn_Wv"]]).T,
        L0_Wr=a["L0_ffn_Wr"], L0_Wg=a["L0_ffn_Wg"], L0_Wu=a["L0_ffn_Wu"], L0_Wd=a["L0_ffn_Wd"],
        L1_Wr=a["L1_ffn_Wr"], L1_Wg=a["L1_ffn_Wg"], L1_Wu=a["L1_ffn_Wu"], L1_Wd=a["L1_ffn_Wd"],
        L2_Wq=a["L2_xattn_Wq"], L2_Wk=a["L2_xattn_Wk"], L2_Wv=a["L2_xattn_Wv"], L2_Wo=a["L2_xattn_Wo"],
        L2_qw=a["L2_xattn_q_norm_w"], L2_kw=a["L2_xattn_k_norm_w"], L2_WrT=a["L2_ffn_wg"].T,
        L2_w1=a["L2_ffn_w1"], L2_v1=a["L2_ffn_v1"], L2_w2=a["L2_ffn_w2"],
        L3_WqT=a["L3_xattn_wq"].T, L3_WkT=a["L3_xattn_wk"].T, L3_WvT=a["L3_xattn_wv"].T, L3_WoT=a["L3_xattn_wo"].T,
        L3_kernelT=a["L3_ffn_kernel"].T, L3_bias=a["L3_ffn_bias"],
    )
    ins = {n: np.ascontiguousarray(v) for n, v in ins.items()}
    nc = bacc.Bacc("TRN2", target_bir_lowering=False, num_devices=1)
    aps = {n: nc.dram_tensor(f"in_{n}", v.shape, mybir.dt.from_np(v.dtype), kind="ExternalInput").ap() for n, v in ins.items()}
    out = nc.dram_tensor("out", (B, S, D), F32, kind="ExternalOutput").ap()
    program(nc, out=out, **aps)
    got = run_bass_kernel_spmd(nc, [{f"in_{n}": v for n, v in ins.items()}], core_ids=[0])
    return got.results[0]["out"]
```
